# Optimizing a Trainium2 kernel written in Bass

```python
import numpy as np
import jax
import jax.numpy as jnp

def _softmax(x, axis=-1):
    return jax.nn.softmax(x, axis=axis)

def _gelu(x):
    return jax.nn.gelu(x, approximate=True)

def _silu(x):
    return jax.nn.silu(x)

def _sigmoid(x):
    return jax.nn.sigmoid(x)

def _layernorm(x, axis=-1, eps=1e-05):
    m = jnp.mean(x, axis=axis, keepdims=True)
    v = jnp.var(x, axis=axis, keepdims=True)
    return (x - m) / jnp.sqrt(v + eps)

def _scatter_add(tgt, idx, src, axis=0):
    return tgt.at[idx].add(src)

def _segment_sum(src, seg, n):
    return jax.ops.segment_sum(src, seg, n)
kernel_name = 'mk_early_fusion_d2_tok_img768_r4_2f24eb'

def setup_inputs(seed: int=0):
    np.random.seed(seed)
    _w = jnp.asarray

    def _rec_inputs():
        import jax
        import jax.numpy as jnp
        _rk = jax.random.key(seed)
        x = -0.000222058 + 0.999998 * jax.random.normal(jax.random.fold_in(_rk, 1), (32, 64, 64, 3), jnp.float32)
        txt = -0.00015822 + 0.554492 * jax.random.normal(jax.random.fold_in(_rk, 2), (32, 128, 192), jnp.float32)
        return (x, txt)
    x, txt = _rec_inputs()

    def _L0_tok_setup():
        import jax, jax.numpy as jnp
        import numpy as np
        PATCH = 16

        def _extract_patches(x, p):
            B, H, W, C = x.shape
            x = x.reshape(B, H // p, p, W // p, p, C)
            x = x.transpose(0, 1, 3, 2, 4, 5)
            return x.reshape(B, H // p * (W // p), p * p * C)
        key = jax.random.key(seed)
        k1, k2, k3 = jax.random.split(key, 3)
        B, H, W, C = (128, 64, 64, 3)
        patch_dim = PATCH * PATCH * C
        hidden = 192
        n_patches = H // PATCH * (W // PATCH)
        x = jax.random.normal(k1, (B, H, W, C), dtype=jnp.float32)
        Wp = jax.random.normal(k2, (patch_dim, hidden), dtype=jnp.float32) * 0.02
        b = jnp.zeros((hidden,), dtype=jnp.float32)
        pos_emb = jax.random.normal(k3, (n_patches, hidden), dtype=jnp.float32) * 0.02
        return {'x': x, 'W': Wp, 'b': b, 'pos_emb': pos_emb}
    _L0_tok_all = _L0_tok_setup()
    _L0_tok_in = {k: v for k, v in _L0_tok_all.items() if k in ('W', 'b', 'pos_emb')}
    del _L0_tok_all

    def _L0_attn_setup():
        import jax, jax.numpy as jnp
        import numpy as np
        import math
        B, N, DIM = (8, 1024, 192)
        H, D = (12, 64)
        STAGES = 3
        LN_EPS = 1e-05

        def _ln(x, g, b):
            mu = jnp.mean(x, axis=-1, keepdims=True)
            var = jnp.mean(jnp.square(x - mu), axis=-1, keepdims=True)
            return (x - mu) * jax.lax.rsqrt(var + LN_EPS) * g + b

        def _mlp(x, W, b, g, be):
            return jax.nn.gelu(_ln(x @ W + b, g, be), approximate=False)
        key = jax.random.key(seed)
        ks = jax.random.split(key, 16)
        s = lambda i, shape, sc: jax.random.normal(ks[i], shape, jnp.float32) * sc
        return {'x': s(0, (B, N, DIM), 1.0), 'Wq': s(1, (DIM, H * D), DIM ** (-0.5)), 'Wk': s(2, (DIM, H * D), DIM ** (-0.5)), 'Wv': s(3, (DIM, H * D), DIM ** (-0.5)), 'pool_W': s(4, (STAGES, D, D), D ** (-0.5)), 'pool_b': jnp.zeros((STAGES, D), jnp.float32), 'pool_g': jnp.ones((STAGES, D), jnp.float32), 'pool_be': jnp.zeros((STAGES, D), jnp.float32), 'exp_W': s(5, (STAGES, D, D), D ** (-0.5)), 'exp_b': jnp.zeros((STAGES, D), jnp.float32), 'exp_g': jnp.ones((STAGES, D), jnp.float32), 'exp_be': jnp.zeros((STAGES, D), jnp.float32), 'Wo': s(6, (H * D, DIM), (H * D) ** (-0.5)), 'bo': jnp.zeros((DIM,), jnp.float32)}
    _L0_attn_all = _L0_attn_setup()
    _L0_attn_in = {k: v for k, v in _L0_attn_all.items() if k in ('Wq', 'Wk', 'Wv', 'pool_W', 'pool_b', 'pool_g', 'pool_be', 'exp_W', 'exp_b', 'exp_g', 'exp_be', 'Wo', 'bo')}
    del _L0_attn_all

    def _L0_ffn_setup():
        import jax, jax.numpy as jnp
        import numpy as np
        E = 16
        K = 4
        H = 192
        I = 384
        LIMIT = 7.0
        ALPHA = 1.702
        EPS = 1e-05

        def rmsnorm(x, scale):
            xf = x.astype(jnp.float32)
            inv = jax.lax.rsqrt(jnp.mean(xf * xf, axis=-1, keepdims=True) + EPS)
            return (xf * inv).astype(x.dtype) * scale

        def swiglu(x, limit=LIMIT, alpha=ALPHA):
            x_glu = x[..., ::2]
            x_lin = x[..., 1::2]
            x_glu = jnp.minimum(x_glu, limit)
            x_lin = jnp.clip(x_lin, -limit, limit)
            return x_glu * jax.nn.sigmoid(alpha * x_glu) * (x_lin + 1.0)
        key = jax.random.key(seed)
        ks = jax.random.split(key, 7)
        s = 0.02
        return {'x': jax.random.normal(ks[0], (2, 256, H), dtype=jnp.float32), 'norm_scale': jnp.ones((H,), dtype=jnp.float32), 'gate_w': jax.random.normal(ks[1], (E, H), dtype=jnp.float32) * s, 'gate_b': jnp.zeros((E,), dtype=jnp.float32), 'mlp1_w': jax.random.normal(ks[2], (E, 2 * I, H), dtype=jnp.float32) * s, 'mlp1_b': jax.random.normal(ks[3], (E, 2 * I), dtype=jnp.float32) * s, 'mlp2_w': jax.random.normal(ks[4], (E, H, I), dtype=jnp.float32) * s, 'mlp2_b': jax.random.normal(ks[5], (E, H), dtype=jnp.float32) * s}
    _L0_ffn_all = _L0_ffn_setup()
    _L0_ffn_in = {k: v for k, v in _L0_ffn_all.items() if k in ('norm_scale', 'gate_w', 'gate_b', 'mlp1_w', 'mlp1_b', 'mlp2_w', 'mlp2_b')}
    del _L0_ffn_all

    def _L1_attn_setup():
        import jax, jax.numpy as jnp
        import numpy as np
        LEVEL = 8
        NUM_HEADS = 12
        QN_SYM = float(-(LEVEL // 2))
        QP_SYM = float(LEVEL // 2 - 1)
        QN_ASYM = 0.0
        QP_ASYM = float(LEVEL - 1)

        def fake_quant(x, s, qn, qp):
            xc = jnp.clip(x / s, qn, qp)
            xr = xc + jax.lax.stop_gradient(jnp.round(xc) - xc)
            return s * xr
        key = jax.random.key(seed)
        k0, k1, k2 = jax.random.split(key, 3)
        B, N, C = (4, 512, 192)
        x = jax.random.normal(k0, (B, N, C), dtype=jnp.float32)
        Wqkv = jax.random.normal(k1, (3 * C, C), dtype=jnp.float32) * C ** (-0.5)
        Wproj = jax.random.normal(k2, (C, C), dtype=jnp.float32) * C ** (-0.5)
        bproj = jnp.zeros((C,), dtype=jnp.float32)
        s_q = jnp.asarray(1.0, dtype=jnp.float32)
        s_k = jnp.asarray(1.0, dtype=jnp.float32)
        s_v = jnp.asarray(1.0, dtype=jnp.float32)
        s_attn = jnp.asarray(1.0 / QP_ASYM, dtype=jnp.float32)
        s_after = jnp.asarray(1.0, dtype=jnp.float32)
        return {'x': x, 'Wqkv': Wqkv, 'Wproj': Wproj, 'bproj': bproj, 's_q': s_q, 's_k': s_k, 's_v': s_v, 's_attn': s_attn, 's_after': s_after}
    _L1_attn_all = _L1_attn_setup()
    _L1_attn_in = {k: v for k, v in _L1_attn_all.items() if k in ('Wqkv', 'Wproj', 'bproj', 's_q', 's_k', 's_v', 's_attn', 's_after')}
    del _L1_attn_all

    def _L1_ffn_setup():
        import jax, jax.numpy as jnp
        import numpy as np
        B, N, D, E, F, K = (2, 512, 192, 8, 768, 2)
        V_MAX = 3.0
        FEAT_CLAMP = 10.0

        def bk_green_diag(a):
            aT = jnp.swapaxes(a, 0, 1)

            def step(c, ai):
                d = ai - 1.0 / c
                return (d, d)
            d0 = aT[0]
            _, d_rest = jax.lax.scan(step, d0, aT[1:])
            d = jnp.concatenate([d0[None], d_rest], axis=0)
            eN = aT[-1]
            _, e_rest = jax.lax.scan(step, eN, aT[:-1], reverse=True)
            e = jnp.concatenate([e_rest, eN[None]], axis=0)
            G = 1.0 / (d + e - aT)
            return jnp.swapaxes(G, 0, 1)
        key = jax.random.key(seed)
        ks = jax.random.split(key, 8)
        s = lambda k, shape, sc: jax.random.normal(k, shape, jnp.float32) * sc
        return {'x': s(ks[0], (B, N, D), 1.0), 'v_w': s(ks[1], (D,), 0.02), 'v_b': jnp.zeros((), jnp.float32), 'gate_w': s(ks[2], (D, E), 0.02), 'gate_b': jnp.zeros((E,), jnp.float32), 'w1': s(ks[3], (E, D, F), 0.02), 'b1': jnp.zeros((E, F), jnp.float32), 'w2': s(ks[4], (E, F, D), 0.02), 'b2': jnp.zeros((E, D), jnp.float32), 'out_w': s(ks[5], (2, D), 0.02), 'out_b': jnp.zeros((D,), jnp.float32), 'bk_scale': jnp.ones((D,), jnp.float32)}
    _L1_ffn_all = _L1_ffn_setup()
    _L1_ffn_in = {k: v for k, v in _L1_ffn_all.items() if k in ('v_w', 'v_b', 'gate_w', 'gate_b', 'w1', 'b1', 'w2', 'b2', 'out_w', 'out_b', 'bk_scale')}
    del _L1_ffn_all
    return {'x': x, 'txt': txt, 'L0_tok_W': _L0_tok_in['W'], 'L0_tok_b': _L0_tok_in['b'], 'L0_tok_pos_emb': _L0_tok_in['pos_emb'], 'L0_attn_Wq': _L0_attn_in['Wq'], 'L0_attn_Wk': _L0_attn_in['Wk'], 'L0_attn_Wv': _L0_attn_in['Wv'], 'L0_attn_pool_W': _L0_attn_in['pool_W'], 'L0_attn_pool_b': _L0_attn_in['pool_b'], 'L0_attn_pool_g': _L0_attn_in['pool_g'], 'L0_attn_pool_be': _L0_attn_in['pool_be'], 'L0_attn_exp_W': _L0_attn_in['exp_W'], 'L0_attn_exp_b': _L0_attn_in['exp_b'], 'L0_attn_exp_g': _L0_attn_in['exp_g'], 'L0_attn_exp_be': _L0_attn_in['exp_be'], 'L0_attn_Wo': _L0_attn_in['Wo'], 'L0_attn_bo': _L0_attn_in['bo'], 'L0_ffn_norm_scale': _L0_ffn_in['norm_scale'], 'L0_ffn_gate_w': _L0_ffn_in['gate_w'], 'L0_ffn_gate_b': _L0_ffn_in['gate_b'], 'L0_ffn_mlp1_w': _L0_ffn_in['mlp1_w'], 'L0_ffn_mlp1_b': _L0_ffn_in['mlp1_b'], 'L0_ffn_mlp2_w': _L0_ffn_in['mlp2_w'], 'L0_ffn_mlp2_b': _L0_ffn_in['mlp2_b'], 'L1_attn_Wqkv': _L1_attn_in['Wqkv'], 'L1_attn_Wproj': _L1_attn_in['Wproj'], 'L1_attn_bproj': _L1_attn_in['bproj'], 'L1_attn_s_q': _L1_attn_in['s_q'], 'L1_attn_s_k': _L1_attn_in['s_k'], 'L1_attn_s_v': _L1_attn_in['s_v'], 'L1_attn_s_attn': _L1_attn_in['s_attn'], 'L1_attn_s_after': _L1_attn_in['s_after'], 'L1_ffn_v_w': _L1_ffn_in['v_w'], 'L1_ffn_v_b': _L1_ffn_in['v_b'], 'L1_ffn_gate_w': _L1_ffn_in['gate_w'], 'L1_ffn_gate_b': _L1_ffn_in['gate_b'], 'L1_ffn_w1': _L1_ffn_in['w1'], 'L1_ffn_b1': _L1_ffn_in['b1'], 'L1_ffn_w2': _L1_ffn_in['w2'], 'L1_ffn_b2': _L1_ffn_in['b2'], 'L1_ffn_out_w': _L1_ffn_in['out_w'], 'L1_ffn_out_b': _L1_ffn_in['out_b'], 'L1_ffn_bk_scale': _L1_ffn_in['bk_scale']}

def reference(x, txt, L0_tok_W, L0_tok_b, L0_tok_pos_emb, L0_attn_Wq, L0_attn_Wk, L0_attn_Wv, L0_attn_pool_W, L0_attn_pool_b, L0_attn_pool_g, L0_attn_pool_be, L0_attn_exp_W, L0_attn_exp_b, L0_attn_exp_g, L0_attn_exp_be, L0_attn_Wo, L0_attn_bo, L0_ffn_norm_scale, L0_ffn_gate_w, L0_ffn_gate_b, L0_ffn_mlp1_w, L0_ffn_mlp1_b, L0_ffn_mlp2_w, L0_ffn_mlp2_b, L1_attn_Wqkv, L1_attn_Wproj, L1_attn_bproj, L1_attn_s_q, L1_attn_s_k, L1_attn_s_v, L1_attn_s_attn, L1_attn_s_after, L1_ffn_v_w, L1_ffn_v_b, L1_ffn_gate_w, L1_ffn_gate_b, L1_ffn_w1, L1_ffn_b1, L1_ffn_w2, L1_ffn_b2, L1_ffn_out_w, L1_ffn_out_b, L1_ffn_bk_scale):
    import jax
    import jax.numpy as jnp

    def _L0_tok_ref(x, W, b, pos_emb):
        import jax, jax.numpy as jnp
        import numpy as np
        PATCH = 16

        def _extract_patches(x, p):
            B, H, W, C = x.shape
            x = x.reshape(B, H // p, p, W // p, p, C)
            x = x.transpose(0, 1, 3, 2, 4, 5)
            return x.reshape(B, H // p * (W // p), p * p * C)
        patches = _extract_patches(x, PATCH)
        proj = jnp.einsum('bnd,dh->bnh', patches, W) + b
        return proj + pos_emb[None, :, :]

    def _L0_attn_ref(x, Wq, Wk, Wv, pool_W, pool_b, pool_g, pool_be, exp_W, exp_b, exp_g, exp_be, Wo, bo):
        import jax, jax.numpy as jnp
        import numpy as np
        import math
        B, N, DIM = (8, 1024, 192)
        H, D = (12, 64)
        STAGES = 3
        LN_EPS = 1e-05

        def _ln(x, g, b):
            mu = jnp.mean(x, axis=-1, keepdims=True)
            var = jnp.mean(jnp.square(x - mu), axis=-1, keepdims=True)
            return (x - mu) * jax.lax.rsqrt(var + LN_EPS) * g + b

        def _mlp(x, W, b, g, be):
            return jax.nn.gelu(_ln(x @ W + b, g, be), approximate=False)
        b, n, _ = x.shape

        def heads(y):
            return y.reshape(b, n, H, D).transpose(0, 2, 1, 3)
        q = heads(x @ Wq)
        k = heads(x @ Wk)
        v = heads(x @ Wv)
        fmap = lambda t: jax.nn.elu(t) + 1.0
        q = fmap(q)
        k = fmap(k)
        kc, vc = (k, v)
        for i in range(STAGES):
            s = kc.shape[2]
            if s > 1:
                pad = -s % 2
                if pad:
                    kc = jnp.pad(kc, ((0, 0), (0, 0), (0, pad), (0, 0)))
                    vc = jnp.pad(vc, ((0, 0), (0, 0), (0, pad), (0, 0)))
                kc = kc.reshape(b, H, -1, 2, D).mean(axis=3)
                kc = _mlp(kc, pool_W[i], pool_b[i], pool_g[i], pool_be[i])
                vc = vc.reshape(b, H, -1, 2, D).mean(axis=3)
        kc = kc / math.sqrt(kc.shape[2])
        kv = jnp.einsum('bhnd,bhne->bhde', kc, vc)
        out = jnp.einsum('bhnd,bhde->bhne', q, kv)
        k_sum = kc.sum(axis=2, keepdims=True)
        q_k_sum = jnp.sum(q * k_sum, axis=-1, keepdims=True)
        out = out / (q_k_sum + 1e-06)
        for i in reversed(range(STAGES)):
            out = _mlp(out, exp_W[i], exp_b[i], exp_g[i], exp_be[i])
        out = out.transpose(0, 2, 1, 3).reshape(b, n, H * D)
        return out @ Wo + bo

    def _L0_ffn_ref(x, norm_scale, gate_w, gate_b, mlp1_w, mlp1_b, mlp2_w, mlp2_b):
        import jax, jax.numpy as jnp
        import numpy as np
        E = 16
        K = 4
        H = 192
        I = 384
        LIMIT = 7.0
        ALPHA = 1.702
        EPS = 1e-05

        def rmsnorm(x, scale):
            xf = x.astype(jnp.float32)
            inv = jax.lax.rsqrt(jnp.mean(xf * xf, axis=-1, keepdims=True) + EPS)
            return (xf * inv).astype(x.dtype) * scale

        def swiglu(x, limit=LIMIT, alpha=ALPHA):
            x_glu = x[..., ::2]
            x_lin = x[..., 1::2]
            x_glu = jnp.minimum(x_glu, limit)
            x_lin = jnp.clip(x_lin, -limit, limit)
            return x_glu * jax.nn.sigmoid(alpha * x_glu) * (x_lin + 1.0)
        B, T, _ = x.shape
        t = rmsnorm(x, norm_scale)
        g = jnp.einsum('bth,eh->bte', t, gate_w) + gate_b
        top_vals, top_idx = jax.lax.top_k(g, K)
        route_w = jax.nn.softmax(top_vals, axis=-1)
        t_flat = t.reshape(B * T, H)
        idx_flat = top_idx.reshape(B * T, K)
        w_flat = route_w.reshape(B * T, K)
        onehot = jax.nn.one_hot(idx_flat, E, dtype=t_flat.dtype)
        comb = jnp.einsum('nke,nk->ne', onehot, w_flat)
        h = jnp.einsum('nh,ech->nec', t_flat, mlp1_w) + mlp1_b
        a = swiglu(h)
        y = jnp.einsum('nec,ehc->neh', a, mlp2_w) + mlp2_b
        out_flat = jnp.einsum('neh,ne->nh', y, comb)
        return x + out_flat.reshape(B, T, H)

    def _L1_attn_ref(x, Wqkv, Wproj, bproj, s_q, s_k, s_v, s_attn, s_after):
        import jax, jax.numpy as jnp
        import numpy as np
        LEVEL = 8
        NUM_HEADS = 12
        QN_SYM = float(-(LEVEL // 2))
        QP_SYM = float(LEVEL // 2 - 1)
        QN_ASYM = 0.0
        QP_ASYM = float(LEVEL - 1)

        def fake_quant(x, s, qn, qp):
            xc = jnp.clip(x / s, qn, qp)
            xr = xc + jax.lax.stop_gradient(jnp.round(xc) - xc)
            return s * xr
        B, N, C = x.shape
        H = NUM_HEADS
        D = C // H
        scale = D ** (-0.5)
        qkv = jnp.einsum('bnc,dc->bnd', x, Wqkv).reshape(B, N, 3, H, D).transpose(2, 0, 3, 1, 4)
        q, k, v = (qkv[0], qkv[1], qkv[2])
        q = fake_quant(q, s_q, QN_SYM, QP_SYM) * scale
        k = fake_quant(k, s_k, QN_SYM, QP_SYM)
        v = fake_quant(v, s_v, QN_SYM, QP_SYM)
        attn = jnp.einsum('bhnd,bhmd->bhnm', q, k)
        attn = fake_quant(attn / N, s_attn, QN_ASYM, QP_ASYM)
        out = jnp.einsum('bhnm,bhmd->bhnd', attn, v)
        out = fake_quant(out, s_after, QN_SYM, QP_SYM)
        out = out.transpose(0, 2, 1, 3).reshape(B, N, C)
        return out @ Wproj.T + bproj

    def _L1_ffn_ref(x, v_w, v_b, gate_w, gate_b, w1, b1, w2, b2, out_w, out_b, bk_scale):
        import jax, jax.numpy as jnp
        import numpy as np
        B, N, D, E, F, K = (2, 512, 192, 8, 768, 2)
        V_MAX = 3.0
        FEAT_CLAMP = 10.0

        def bk_green_diag(a):
            aT = jnp.swapaxes(a, 0, 1)

            def step(c, ai):
                d = ai - 1.0 / c
                return (d, d)
            d0 = aT[0]
            _, d_rest = jax.lax.scan(step, d0, aT[1:])
            d = jnp.concatenate([d0[None], d_rest], axis=0)
            eN = aT[-1]
            _, e_rest = jax.lax.scan(step, eN, aT[:-1], reverse=True)
            e = jnp.concatenate([e_rest, eN[None]], axis=0)
            G = 1.0 / (d + e - aT)
            return jnp.swapaxes(G, 0, 1)
        v = jnp.clip(x @ v_w + v_b, -V_MAX, V_MAX)
        a = (-2.0 + v).astype(jnp.complex64) - 1j
        G = bk_green_diag(a)
        feats = jnp.stack([G.real, G.imag], axis=-1)
        logits = x @ gate_w + gate_b
        probs = jax.nn.softmax(logits, axis=-1)
        topv, topi = jax.lax.top_k(probs, K)
        topv = topv / jnp.sum(topv, axis=-1, keepdims=True)
        comb = jnp.sum(topv[..., None] * jax.nn.one_hot(topi, E, dtype=x.dtype), axis=2)
        h = jax.nn.gelu(jnp.einsum('bnd,edf->bnef', x, w1) + b1)
        y = jnp.einsum('bnef,efd->bned', h, w2) + b2
        ffn_out = jnp.einsum('bne,bned->bnd', comb, y)
        feats_c = jnp.clip(feats, -FEAT_CLAMP, FEAT_CLAMP)
        spec_out = feats_c @ out_w + out_b
        return ffn_out + bk_scale * spec_out
    h = _L0_tok_ref(x, L0_tok_W, L0_tok_b, L0_tok_pos_emb)
    h = jnp.concatenate([h, txt], axis=1)
    h = h + _L0_attn_ref(_layernorm(h, axis=-1), L0_attn_Wq, L0_attn_Wk, L0_attn_Wv, L0_attn_pool_W, L0_attn_pool_b, L0_attn_pool_g, L0_attn_pool_be, L0_attn_exp_W, L0_attn_exp_b, L0_attn_exp_g, L0_attn_exp_be, L0_attn_Wo, L0_attn_bo)
    h = h + _L0_ffn_ref(_layernorm(h, axis=-1), L0_ffn_norm_scale, L0_ffn_gate_w, L0_ffn_gate_b, L0_ffn_mlp1_w, L0_ffn_mlp1_b, L0_ffn_mlp2_w, L0_ffn_mlp2_b)
    h = h + _L1_attn_ref(_layernorm(h, axis=-1), L1_attn_Wqkv, L1_attn_Wproj, L1_attn_bproj, L1_attn_s_q, L1_attn_s_k, L1_attn_s_v, L1_attn_s_attn, L1_attn_s_after)
    h = h + _L1_ffn_ref(_layernorm(h, axis=-1), L1_ffn_v_w, L1_ffn_v_b, L1_ffn_gate_w, L1_ffn_gate_b, L1_ffn_w1, L1_ffn_b1, L1_ffn_w2, L1_ffn_b2, L1_ffn_out_w, L1_ffn_out_b, L1_ffn_bk_scale)
    return h

_drawn_inputs = setup_inputs


def setup_inputs(seed=0):
    import zlib

    import numpy as np

    out = dict(_drawn_inputs(seed))
    spreads = {'L0_tok_b': (0.0, 0.1),
     'L0_attn_pool_b': (0.0, 0.8),
     'L0_attn_pool_g': (1.0, 0.6),
     'L0_attn_pool_be': (0.0, 0.8),
     'L0_attn_exp_b': (0.0, 0.1),
     'L0_attn_exp_g': (1.0, 0.2),
     'L0_attn_exp_be': (0.0, 0.1),
     'L0_attn_bo': (0.0, 0.1),
     'L0_ffn_norm_scale': (1.0, 0.6),
     'L0_ffn_gate_b': (0.0, 0.751),
     'L1_attn_bproj': (0.0, 0.1),
     'L1_ffn_gate_b': (0.0, 0.286),
     'L1_ffn_b1': (0.0, 0.683),
     'L1_ffn_b2': (0.0, 0.1),
     'L1_ffn_out_b': (0.0, 0.1),
     'L1_ffn_bk_scale': (1.0, 0.6)}
    factors = {'L0_tok_pos_emb': 5.259,
     'L0_attn_Wq': 2.875,
     'L0_ffn_gate_w': 3.684,
     'L0_ffn_mlp1_w': 3.27,
     'L0_ffn_mlp1_b': 8.0,
     'L0_ffn_mlp2_w': 3.107,
     'L0_ffn_mlp2_b': 8.0,
     'L1_ffn_v_w': 8.0,
     'L1_ffn_out_w': 8.0}
    for name, (base, spread) in spreads.items():
        noise = np.random.default_rng([zlib.crc32(name.encode()), seed]).standard_normal(out[name].shape)
        drawn = base * np.exp(spread * noise) if base else spread * noise
        out[name] = jnp.asarray(drawn.astype(out[name].dtype))
    for name, factor in factors.items():
        out[name] = (out[name] * factor).astype(out[name].dtype)
    return out
```

```python
from contextlib import ExitStack

import numpy as np
import concourse.bass as bass
from concourse import mybir
from concourse.alu_op_type import AluOpType as ALU

F32 = mybir.dt.float32
BF16 = mybir.dt.bfloat16
I32 = mybir.dt.int32
U32 = mybir.dt.uint32
ACT = mybir.ActivationFunctionType
AX = mybir.AxisListType.X

P = 128
B, N, NIMG = 32, 144, 16
D = 192
DC = D // 2
TOK = B * N
NT = TOK // P
LN_EPS = 1e-5
NH, HD = 12, 64
HP = NH // 2
A0 = NH * HD
POOL = 8
NPOOL = N // POOL
TPOOL = B * NPOOL
NPT = -(-TPOOL // P)
E0, K0, I0 = 16, 4, 384
E1, K1, I1 = 8, 2, 768
SLOT0 = (TOK * K0 + E0 * (P - 1)) // P
SLOT1 = (TOK * K1 + E1 * (P - 1)) // P
SLOT0 += SLOT0 % 2
SLOT1 += SLOT1 % 2
QH, QD = 12, 16
QC = QH // 4
CSLOT = 32


def later(i, ring):
    return not isinstance(i, int) or i >= ring


def pipelined(eng, count, unroll, *stages):
    lag = max(s[0] for s in stages)
    first = unroll * (-(-(lag + 2 * unroll) // unroll))
    if count <= first or (count - first) < 2 * unroll:
        first = count
    last = first + (count - first) // unroll * unroll

    def step(i, slot):
        for behind, f in stages:
            if not isinstance(i, int) or 0 <= i - behind < count:
                f(i - behind, (slot - behind) % unroll)

    for i in range(first):
        step(i, i % unroll)
    if last > first:
        with eng.Fori(first // unroll, last // unroll) as j:
            for u in range(unroll):
                step(j * unroll + u, u)
    for i in range(last, count + lag):
        step(i, i % unroll)


class Model:

    def __init__(self, nc, ins, out, ctx):
        self.nc, self.ins, self.out, self.ctx = nc, ins, out, ctx
        self.finished = []
        self.var_raw, self.var_raws = ctx.enter_context(nc.semaphore('var_raw')), 0
        self.passed = ctx.enter_context(nc.semaphore('passed'))

    def sb(self, ctx, name, shape, dt=F32):
        return ctx.enter_context(self.nc.sbuf_tensor(name, shape, dt))

    def psum(self, ctx, name, shape, dt=F32):
        return ctx.enter_context(self.nc.psum_tensor(name, shape, dt))

    def sem(self, ctx, name):
        handle = self.nc.alloc_semaphore(name=name)
        ctx.callback(self.finished.append, handle)
        return handle

    def recycle(self):
        self.nc.clear_and_free_semaphores(self.finished)
        self.finished = []
        self.nc.all_engine_barrier()

    def sems(self, ctx, prefix, names):
        return [self.sem(ctx, f"{prefix}_{n}") for n in names.split()]


def embed(m, ctx, h, posb):
    nc, ins = m.nc, m.ins
    with ExitStack() as c:
        patches = m.sb(c, "patches", [P, 6, 512])
        tok_w = m.sb(c, "tok_w", [P, 6, D])
        tok_b = m.sb(c, "tok_b", [P, D])
        zero = m.sb(c, "zero", [P, 1536])
        emb = m.sb(c, "emb", [P, 4, D])
        ps = m.psum(c, "emb_ps", [P, 4, 512])
        loaded, posb_ready, emb_mm, emb_done, h0_text, h0_img, h_in, zeroed, xs_zero = m.sems(
            c, "em", "loaded posb_ready emb_mm emb_done h0_text h0_img h_in zeroed xs_zero")
        xs_all = m.xs.rearrange("(c p n) d -> c p (n d)", p=P, n=8)
        with nc.Block() as block:
            @block.sync
            def _(sp):
                sp.dma_start(tok_w[:], ins["tok_w"]).then_inc(loaded, 16)
                sp.dma_start(patches[:], ins["patchesT"]).then_inc(loaded, 16)
                sp.dma_start(posb[:], ins["pos"]).then_inc(loaded, 16)
                sp.dma_start(tok_b[:], ins["tok_b"]).then_inc(loaded, 16)
                for g in range(4):
                    sp.wait_ge(emb_done, g + 1)
                    for b in range(8):
                        sp.dma_start(m.h0[(8 * g + b) * N:(8 * g + b) * N + NIMG, :],
                                     emb[b * NIMG:(b + 1) * NIMG, g, :]).then_inc(h0_img, 16)
                sp.wait_ge(h0_img, 32 * 16)
                sp.wait_ge(h0_text, 16)
                sp.dma_start(h[:], m.h0.rearrange("(t p) d -> p t d", p=P)).then_inc(h_in, 16)
                sp.wait_ge(h_in, 16)

            @block.scalar
            def _(act):
                act.dma_start(m.h0.rearrange("(b n) d -> b n d", n=N)[:, NIMG:, :], ins["txt"]).then_inc(h0_text, 16)
                act.wait_ge(zeroed, 1)
                for k in range(SLOT0 // 8):
                    act.dma_start(xs_all[k], zero[:]).then_inc(xs_zero, 16)
                act.wait_ge(xs_zero, SLOT0 // 8 * 16)

            @block.gpsimd
            def _(pool):
                pool.memset(zero[:], 0.0).then_inc(zeroed, 1)

            @block.tensor
            def _(pe):
                pe.wait_ge(loaded, 64)
                for g in range(4):
                    for k in range(6):
                        mm = pe.matmul(ps[:, g, 0:D], patches[:, k, g * P:(g + 1) * P], tok_w[:, k, :],
                                       start=(k == 0), stop=(k == 5))
                    mm.then_inc(emb_mm, 1)

            @block.vector
            def _(dve):
                dve.wait_ge(loaded, 64)
                dve.tensor_tensor(posb[:], posb[:], tok_b[:], ALU.add).then_inc(posb_ready, 1)
                dve.wait_ge(posb_ready, 1)
                for g in range(4):
                    dve.wait_ge(emb_mm, g + 1)
                    dve.tensor_tensor(emb[:, g, :], ps[:, g, 0:D], posb[:], ALU.add).then_inc(emb_done, 1)


def constants(m, ctx):
    nc, ins = m.nc, m.ins
    m.ident = m.sb(ctx, "ident", [P, P])
    m.mlp_w = m.sb(ctx, "mlp_w", [P, 6, P])
    m.mlp_g = m.sb(ctx, "mlp_g", [P, 6])
    m.mlp_be = m.sb(ctx, "mlp_be", [P, 6])
    m.mlp_b3 = m.sb(ctx, "mlp_b3", [3, 6, 384], BF16)
    m.ones3 = m.sb(ctx, "ones3", [3, P], BF16)
    m.half = m.sb(ctx, "half", [P, NH])
    m.eps = m.sb(ctx, "eps", [P, 1])
    with ExitStack() as c:
        mean = m.sb(c, "w_mean", [P, 12])
        braw = m.sb(c, "b_raw", [3, 6, HD])
        bmean = m.sb(c, "b_mean", [3, 6])
        rest = m.sb(c, "b_rest", [3, 6, HD])
        part = m.sb(c, "b_part", [3, 3, 6, HD], BF16)
        psel = m.sb(c, "b_sel", [3, 6, HD], BF16)
        loaded, done, step = m.sems(c, "ct", "loaded done step")
        with nc.Block() as block:
            @block.sync
            def _(sp):
                for t, name in ((m.ident, "ident"), (m.mlp_w, "mlp_w"), (m.mlp_g, "mlp_g"),
                                (m.mlp_be, "mlp_be"), (braw, "mlp_b")):
                    sp.dma_start(t[:], ins[name]).then_inc(loaded, 16)

            @block.gpsimd
            def _(pool):
                pool.memset(m.half[:], -0.5).then_inc(done, 1)
                pool.memset(m.ones3[:], 1.0).then_inc(done, 1)
                pool.memset(m.eps[:], LN_EPS).then_inc(done, 1)

            @block.vector
            def _(dve):
                count = [0]

                def link(ins_):
                    count[0] += 1
                    ins_.then_inc(step, 1)
                    dve.wait_ge(step, count[0])

                dve.wait_ge(loaded, 80)
                w = m.mlp_w[:].rearrange("p s (h d) -> p (s h) d", h=2)
                link(dve.tensor_reduce(mean[:], w, AX, ALU.add))
                link(dve.tensor_scalar(mean[:], mean[:], 1.0 / HD, None, ALU.mult))
                link(dve.tensor_tensor(w, w, mean[:].unsqueeze(2).to_broadcast([P, 12, HD]), ALU.subtract))
                link(dve.tensor_scalar(m.mlp_w[:, 0:3, :], m.mlp_w[:, 0:3, :], 0.5, None, ALU.mult))
                link(dve.tensor_reduce(bmean[:], braw[:], AX, ALU.add))
                link(dve.tensor_scalar(bmean[:], bmean[:], 1.0 / HD, None, ALU.mult))
                link(dve.tensor_tensor(rest[:], braw[:], bmean[:].unsqueeze(2).to_broadcast([3, 6, HD]), ALU.subtract))
                for k in range(3):
                    link(dve.tensor_copy(part[:, k], rest[:]))
                    link(dve.tensor_tensor(rest[:], rest[:], part[:, k], ALU.subtract))
                link(dve.tensor_scalar(psel[:], part[:, 0], m.ident[0:3, 0:1], None, ALU.mult))
                for k in (1, 2):
                    link(dve.scalar_tensor_tensor(out=psel[:], in0=part[:, k], scalar=m.ident[0:3, k:k + 1],
                                                  in1=psel[:], op0=ALU.mult, op1=ALU.add))
                for h in range(6):
                    dve.tensor_copy(m.mlp_b3[:, :, h * HD:(h + 1) * HD], psel[:]).then_inc(done, 1)


def layernorm_T(m, h, xT, tag, xpT=None):
    nc = m.nc
    with ExitStack() as c:
        stats = m.sb(c, tag + "stats", [P, NT, 6])
        mean = m.sb(c, tag + "mean", [P, NT])
        var = m.sb(c, tag + "var", [P, NT])
        tmp = m.sb(c, tag + "tmp", [P, NT])
        rstd = m.sb(c, tag + "rstd", [P, NT])
        xn = m.sb(c, tag + "xn", [P, 2, D])
        tp = m.psum(c, tag + "tp", [P, 2, 512])
        stat, step, var_ok, std_ok, xn_ok, tp_ok, xT_ok, xp_ok = m.sems(
            c, tag, "stat step var_ok std_ok xn_ok tp_ok xT_ok xp_ok")
        with nc.Block() as block:
            @block.vector
            def _(dve):
                pipelined(dve, NT, 2, (0, lambda i, s: dve.bn_stats(stats[:, i, :], h[:, i, :]).then_inc(stat, 1)))
                dve.wait_ge(stat, NT)
                moments(m, dve, stats, mean, var, tmp, step)
                dve.wait_ge(std_ok, 1)
                dve.reciprocal(rstd[:], tmp[:]).then_inc(step, 1)
                dve.wait_ge(step, MOMENTS + 1)

                def norm(i, s):
                    if later(i, 2):
                        dve.wait_ge(tp_ok, i - 1)
                    dve.tensor_scalar(xn[:, s, :], h[:, i, :], mean[:, bass.ds(i, 1)], rstd[:, bass.ds(i, 1)],
                                      ALU.subtract, ALU.mult).then_inc(xn_ok, 1)

                def pool(i, s):
                    dve.wait_ge(xT_ok, i + 1)
                    dve.sem_inc(m.passed, 1)
                    dve.tensor_reduce(xpT[:, :, bass.ds(i * (P // POOL), P // POOL)],
                                      xT[:, :, bass.ds(i * P, P)].rearrange("p c (n k) -> p c n k", k=POOL),
                                      AX, ALU.add).then_inc(xp_ok, 1)
                pipelined(dve, NT, 2, (0, norm), *([(1, pool)] if xpT is not None else []))

            @block.tensor
            def _(pe):
                def turn(i, s):
                    pe.wait_ge(xn_ok, i + 1)
                    if later(i, 2):
                        pe.wait_ge(xT_ok, i - 1)
                    for k in range(2):
                        mm = pe.transpose(tp[0:DC, s, k * P:(k + 1) * P], xn[:, s, k * DC:(k + 1) * DC], m.ident[:])
                    mm.then_inc(tp_ok, 1)
                pipelined(pe, NT, 2, (0, turn))

            @block.scalar
            def _(act):
                act.wait_ge(step, MOMENTS)
                act.activation(tmp[:], var[:], ACT.Sqrt, bias=m.eps[:, 0:1]).then_inc(std_ok, 1)

                def copy(i, s):
                    act.wait_ge(tp_ok, i + 1)
                    act.sem_inc(m.passed, 1)
                    act.activation(xT[:, :, bass.ds(i * P, P)],
                                   tp[0:DC, s, 0:2 * P].rearrange("p (c n) -> p c n", c=2), ACT.Copy).then_inc(xT_ok, 1)
                pipelined(act, NT, 2, (0, copy))


MOMENTS = 6


def moments(m, dve, stats, mean, var, tmp, step):
    even, odd, sq_e, sq_o = (stats[:, :, k] for k in (1, 4, 2, 5))
    n = [0]

    def link(i):
        n[0] += 1
        i.then_inc(step, 1)
        dve.wait_ge(step, n[0])
    link(dve.tensor_tensor(mean[:], even, odd, ALU.add))
    link(dve.tensor_tensor(tmp[:], even, odd, ALU.subtract))
    link(dve.tensor_scalar(mean[:], mean[:], 0.5, None, ALU.mult))
    link(dve.scalar_tensor_tensor(out=tmp[:], in0=tmp[:], scalar=D / 4.0, in1=tmp[:], op0=ALU.mult, op1=ALU.mult))
    link(dve.tensor_tensor(var[:], sq_e, sq_o, ALU.add))
    dve.tensor_tensor(var[:], var[:], tmp[:], ALU.add).then_inc(m.var_raw, 1)
    m.var_raws += 1
    dve.wait_ge(m.var_raw, m.var_raws)
    link(dve.tensor_scalar(var[:], var[:], 1.0 / D, None, ALU.mult))


def keys(m, xT, wk, kpT):
    with ExitStack() as c:
        ex = m.sb(c, "k_exp", [P, 2, HP, N])
        kf = m.sb(c, "k_feat", [P, 2, HP, N])
        ps = m.psum(c, "k_ps", [P, 2, 2, 512])
        loaded, mm_ok, exp_ok, min_ok, k_ok, kp_ok = m.sems(c, "ky", "loaded mm_ok exp_ok min_ok k_ok kp_ok")
        proj = lambda s: ps[:, s, :, 0:3 * N]
        with m.nc.Block() as block:
            @block.sync
            def _(sp):
                sp.dma_start(wk[:], m.ins["attn_wk"]).then_inc(loaded, 16)

            @block.tensor
            def _(pe):
                pe.wait_ge(loaded, 16)

                def project(b, s):
                    if later(b, 2):
                        pe.wait_ge(k_ok, b - 1)
                    pe_project(pe, ps, s, wk, xT, b).then_inc(mm_ok, 1)
                pipelined(pe, B, 2, (0, project))

            @block.scalar
            def _(act):
                def exp(b, s):
                    act.wait_ge(mm_ok, b + 1)
                    if later(b, 2):
                        act.wait_ge(k_ok, b - 1)
                    act.activation(ex[:, s].rearrange("p (g h) n -> p g (h n)", g=2), proj(s), ACT.Exp).then_inc(exp_ok, 1)
                pipelined(act, B, 2, (0, exp))

            @block.vector
            def _(dve):
                def elu(b, s):
                    dve.wait_ge(exp_ok, b + 1)
                    dve.tensor_scalar(ex[:, s], ex[:, s], 1.0, None, ALU.min).then_inc(min_ok, 1)
                    dve.wait_ge(min_ok, b + 1)
                    dve.scalar_tensor_tensor(out=kf[:, s].rearrange("p (g h) n -> p g (h n)", g=2), in0=proj(s), scalar=0.0,
                                             in1=ex[:, s].rearrange("p (g h) n -> p g (h n)", g=2),
                                             op0=ALU.max, op1=ALU.add).then_inc(k_ok, 1)
                    dve.wait_ge(k_ok, b + 1)
                    two = kf[:, s].rearrange("p h (n k) -> p h n k", k=2)
                    dve.tensor_tensor(kpT[:, :, bass.ds(b * (N // 2), N // 2)], two[:, :, :, 0], two[:, :, :, 1],
                                      ALU.add).then_inc(kp_ok, 1)
                pipelined(dve, B, 2, (0, elu))
                dve.wait_ge(kp_ok, B)


def pe_project(pe, ps, s, w, xT, b):
    for h in range(HP):
        for k in range(2):
            mm = pe.matmul(ps[:, s, h // 3, (h % 3) * N:(h % 3 + 1) * N], w[:, k, h * P:(h + 1) * P],
                           xT[:, k, bass.ds(b * N, N)], start=(k == 0), stop=(k == 1))
    return mm


def mlp(m, tag, stage, src, dst, tiles, pairs):
    with ExitStack() as c:
        x = m.sb(c, tag + "x", [P, 3, HP, P])
        sq = m.sb(c, tag + "sq", [P, 3, NH, HD])
        ss = m.sb(c, tag + "ss", [P, 3, NH])
        rstd = m.sb(c, tag + "rstd", [P, 3, NH])
        z = m.sb(c, tag + "z", [P, 3, HP, P])
        g = m.sb(c, tag + "g", [P, 3, HP, P]) if pairs else None
        y = m.psum(c, tag + "y", [P, 3, 2, 512])
        tp = m.psum(c, tag + "tp", [P, 2, 512])
        x_ok, mm_ok, sq_ok, ss_ok, var_ok, rstd_ok, z_ok, tp0_ok, tp1_ok, g0_ok, g1_ok, pair_ok = m.sems(
            c, tag, "x_ok mm_ok sq_ok ss_ok var_ok rstd_ok z_ok tp0_ok tp1_ok g0_ok g1_ok pair_ok")
        tp_ok, g_ok = (tp0_ok, tp1_ok), (g0_ok, g1_ok)
        with m.nc.Block() as block:
            @block.vector
            def _(dve):
                def stage_in(i, s):
                    if later(i, 3):
                        dve.wait_ge(mm_ok, i - 2)
                        dve.sem_inc(m.passed, 1)
                    dve.tensor_copy(x[:, s], src[:, :, bass.ds(i * P, P)]).then_inc(x_ok, 1)

                def squares(i, s):
                    dve.wait_ge(sq_ok, i + 1)
                    dve.tensor_reduce(ss[:, s], sq[:, s], AX, ALU.add).then_inc(ss_ok, 1)
                    dve.wait_ge(ss_ok, i + 1)
                    dve.tensor_scalar(ss[:, s], ss[:, s], 1.0 / HD, LN_EPS, ALU.mult, ALU.add).then_inc(var_ok, 1)

                def scale(i, s):
                    dve.wait_ge(rstd_ok, i + 1)
                    if later(i, 3):
                        dve.wait_ge(tp_ok[1], i - 2)
                    dve.tensor_tensor(z[:, s].rearrange("p (a b) (e d) -> p a (b e) d", a=2, d=HD),
                                      y[:, s, :, 0:384].rearrange("p a (h d) -> p a h d", d=HD),
                                      rstd[:, s].rearrange("p (a h) -> p a h", a=2).unsqueeze(3).to_broadcast([P, 2, 6, HD]),
                                      ALU.mult).then_inc(z_ok, 1)

                def add_pairs(i, s):
                    dve.wait_ge(g_ok[1], i + 1)
                    two = g[:, s].rearrange("p h (n k) -> p h n k", k=2)
                    dve.tensor_tensor(dst[:, :, bass.ds(i * (P // 2), P // 2)], two[:, :, :, 0], two[:, :, :, 1],
                                      ALU.add).then_inc(pair_ok, 1)
                pipelined(dve, tiles, 3, (0, stage_in), (1, squares), (2, scale), *([(3, add_pairs)] if pairs else []))
                if pairs:
                    dve.wait_ge(pair_ok, tiles)

            @block.tensor
            def _(pe):
                def dense(i, s):
                    pe.wait_ge(x_ok, i + 1)
                    if later(i, 3):
                        pe.wait_ge(z_ok, i - 2)
                    for a in range(2):
                        pe.matmul(y[:, s, a, 0:384], m.ones3[:], m.mlp_b3[:, stage, :], start=True, stop=False)
                        for h in range(3):
                            mm = pe.matmul(y[:, s, a, h * P:(h + 1) * P], x[:, s, 3 * a + h, :], m.mlp_w[:, stage, :],
                                           start=False, stop=(h == 2))
                    mm.then_inc(mm_ok, 1)

                def turn(i, s):
                    pe.wait_ge(z_ok, i + 1)
                    for a in range(2):
                        if later(i, 1):
                            pe.wait_ge(g_ok[a], i)
                        for h in range(3):
                            mm = pe.transpose(tp[:, a, h * P:(h + 1) * P], z[:, s, 3 * a + h, :], m.ident[:])
                        mm.then_inc(tp_ok[a], 1)
                pipelined(pe, tiles, 3, (0, dense), (2, turn))

            @block.scalar
            def _(act):
                def square(i, s):
                    act.wait_ge(mm_ok, i + 1)
                    if later(i, 3):
                        act.wait_ge(ss_ok, i - 2)
                    act.activation(sq[:, s].rearrange("p (a h) d -> p a (h d)", a=2), y[:, s, :, 0:384],
                                   ACT.Square).then_inc(sq_ok, 1)

                def gelu(i, s):
                    for a in range(2):
                        act.wait_ge(tp_ok[a], i + 1)
                        if pairs and later(i, 3):
                            act.wait_ge(pair_ok, i - 2)
                        act.sem_inc(m.passed, 1)
                        to = g[:, s, 3 * a:3 * a + 3, :] if pairs else dst[:, 3 * a:3 * a + 3, bass.ds(i * P, P)]
                        act.activation(to, tp[:, a, 0:384].rearrange("p (h n) -> p h n", n=P), ACT.Gelu,
                                       bias=m.mlp_be[:, stage:stage + 1],
                                       scale=m.mlp_g[:, stage:stage + 1]).then_inc(g_ok[a], 1)
                pipelined(act, tiles, 3, (0, square), (2, gelu))
                act.wait_ge(g_ok[1], tiles)

            @block.gpsimd
            def _(pool):
                def rsqrt(i, s):
                    pool.wait_ge(var_ok, i + 1)
                    if later(i, 3):
                        pool.wait_ge(z_ok, i - 2)
                    pool.tensor_tensor(rstd[:, s], ss[:, s], m.half[:], ALU.pow).then_inc(rstd_ok, 1)
                pipelined(pool, tiles, 3, (0, rsqrt))


def pooled_state(m, kcT, xpT, wv, ksum):
    with ExitStack() as c:
        kt = m.sb(c, "kt", [P, NPT, HP, P])
        vt = m.sb(c, "vt", [P, NPT, A0])
        kps = m.psum(c, "kps", [P, 2, 2, 512])
        vps = m.psum(c, "vps", [P, 2, 2, 512])
        loaded, scaled, sums, k_mm, v_mm, k_ok, v_ok, stored = m.sems(
            c, "pl", "loaded scaled sums k_mm v_mm k_ok v_ok stored")
        rows = [min(P, TPOOL - P * i) for i in range(NPT)]
        with m.nc.Block() as block:
            @block.vector
            def _(dve):
                dve.tensor_scalar(kcT[:, :, 0:TPOOL], kcT[:, :, 0:TPOOL], float(NPOOL) ** -0.5, None,
                                  ALU.mult).then_inc(scaled, 1)
                dve.tensor_scalar(xpT[:], xpT[:], 1.0 / POOL, None, ALU.mult).then_inc(scaled, 1)
                dve.wait_ge(scaled, 2)
                for h in range(HP):
                    dve.tensor_reduce(ksum[:, :, h], kcT[:, h, 0:TPOOL].rearrange("p (b n) -> p b n", n=NPOOL),
                                      AX, ALU.add).then_inc(sums, 1)
                for i in range(NPT):
                    dve.wait_ge(v_mm, i + 1)
                    dve.tensor_copy(vt[0:rows[i], i, :].rearrange("p (a n) -> p a n", a=2),
                                    vps[0:rows[i], i % 2, :, 0:384]).then_inc(v_ok, 1)
                dve.wait_ge(sums, HP)

            @block.tensor
            def _(pe):
                pe.wait_ge(loaded, 16)
                pe.wait_ge(scaled, 2)
                for i, r in enumerate(rows):
                    if i >= 2:
                        pe.wait_ge(k_ok, i - 1)
                        pe.wait_ge(v_ok, i - 1)
                    for h in range(HP):
                        mm = pe.transpose(kps[0:r, i % 2, h // 3, (h % 3) * P:(h % 3 + 1) * P],
                                          kcT[:, h, i * P:i * P + r], m.ident[:])
                    mm.then_inc(k_mm, 1)
                    for a in range(2):
                        for k in range(2):
                            mm = pe.matmul(vps[0:r, i % 2, a, 0:384], xpT[:, k, i * P:i * P + r],
                                           wv[:, k, a * 384:(a + 1) * 384], start=(k == 0), stop=(k == 1))
                    mm.then_inc(v_mm, 1)

            @block.scalar
            def _(act):
                for i, r in enumerate(rows):
                    act.wait_ge(k_mm, i + 1)
                    act.activation(kt[0:r, i].rearrange("p (a h) n -> p a (h n)", a=2), kps[0:r, i % 2, :, 0:384],
                                   ACT.Copy).then_inc(k_ok, 1)

            @block.sync
            def _(sp):
                sp.dma_start(wv[:], m.ins["attn_wv"]).then_inc(loaded, 16)
                for i, r in enumerate(rows):
                    sp.wait_ge(k_ok, i + 1)
                    sp.dma_start(m.kv_rows[i * P:i * P + r, 0:A0], kt[0:r, i].rearrange("p h n -> p (h n)")).then_inc(stored, 16)
                    sp.wait_ge(v_ok, i + 1)
                    sp.dma_start(m.kv_rows[i * P:i * P + r, A0:], vt[0:r, i, :]).then_inc(stored, 16)
                sp.wait_ge(stored, 32 * NPT)


def linear_attention(m, xT, wq, ksum, aT):
    with ExitStack() as c:
        ex = m.sb(c, "q_exp", [P, 2, HP, N])
        q = m.sb(c, "q", [P, 2, HP, N])
        kv_in = m.sb(c, "kv_in", [NPOOL, 2, 2 * A0])
        kv = m.sb(c, "kv", [P, 2, HP, P])
        hsel = m.sb(c, "hsel", [P, HP, NH])
        hexp = m.sb(c, "hexp", [NH, HP, P])
        ksel = m.sb(c, "ksel", [P, 2, HP, NH])
        rden = m.sb(c, "rden", [NH, 2, N])
        rb = m.sb(c, "rb", [P, 2, HP, N])
        qps = m.psum(c, "q_ps", [P, 1, 2, 512])
        kvps = m.psum(c, "kv_ps", [P, 2, 512])
        nps = m.psum(c, "num_ps", [P, 2, 512])
        rps = m.psum(c, "rb_ps", [P, 2, 512])
        (loaded, kv_zero, q_mm, exp_ok, min_ok, q_ok, kv_mm, kv_top, kv_low, ksel_ok, den_mm, den_ok, rden_ok,
         num_mm, rb_mm, rb_ok, out_ok) = m.sems(
            c, "la", "loaded kv_zero q_mm exp_ok min_ok q_ok kv_mm kv_top kv_low ksel_ok den_mm den_ok rden_ok "
            "num_mm rb_mm rb_ok out_ok")
        arrived = m.sems(c, "la_kv", "in0 in1")
        split = lambda t: t.rearrange("p (g h) n -> p g (h n)", g=2)
        with m.nc.Block() as block:
            @block.sync
            def _(sp):
                sp.dma_start(wq[:], m.ins["attn_wq"]).then_inc(loaded, 16)
                sp.dma_start(hsel[:], m.ins["hsel"]).then_inc(loaded, 16)
                sp.dma_start(hexp[:], m.ins["hexp"]).then_inc(loaded, 16)

                def load(b, s):
                    if later(b, 2):
                        sp.wait_ge(kv_mm, b - 1)
                    sp.dma_start(kv_in[:, s, :], m.kv_rows[bass.ds(b * NPOOL, NPOOL), :]).then_inc(arrived[s], 16)
                pipelined(sp, B, 2, (0, load))

            @block.gpsimd
            def _(pool):
                pool.memset(kv[:], 0.0).then_inc(kv_zero, 1)

            @block.tensor
            def _(pe):
                pe.wait_ge(loaded, 48)

                def first(b, s):
                    if later(b, 1):
                        pe.wait_ge(q_ok, b)
                    pe_project(pe, qps, 0, wq, xT, b).then_inc(q_mm, 1)

                def state(b, s):
                    pe.wait_ge(arrived[s], landed(b, s))
                    if later(b, 1):
                        pe.wait_ge(kv_top, b)
                        pe.wait_ge(kv_low, b)
                    for h in range(HP):
                        mm = pe.matmul(kvps[:, h // 3, (h % 3) * P:(h % 3 + 1) * P], kv_in[:, s, h * P:(h + 1) * P],
                                       kv_in[:, s, A0 + h * P:A0 + (h + 1) * P], start=True, stop=True)
                    mm.then_inc(kv_mm, 1)

                def apply(b, s):
                    pe.wait_ge(q_ok, b + 1)
                    pe.wait_ge(ksel_ok, b + 1)
                    if later(b, 1):
                        pe.wait_ge(rb_ok, b)
                    for h in range(HP):
                        mm = pe.matmul(rps[0:NH, 0, 0:N], ksel[:, s, h, :], q[:, s, h, :], start=(h == 0), stop=(h == HP - 1))
                    mm.then_inc(den_mm, 1)
                    pe.wait_ge(kv_top, b + 1)
                    pe.wait_ge(kv_low, b + 1)
                    if later(b, 1):
                        pe.wait_ge(out_ok, b)
                    for h in range(HP):
                        mm = pe.matmul(nps[:, h // 3, (h % 3) * N:(h % 3 + 1) * N], kv[:, s, h, :], q[:, s, h, :],
                                       start=True, stop=True)
                    mm.then_inc(num_mm, 1)

                def spread(b, s):
                    pe.wait_ge(rden_ok, b + 1)
                    for h in range(HP):
                        mm = pe.matmul(rps[:, h // 3, (h % 3) * N:(h % 3 + 1) * N], hexp[:, h, :], rden[:, s, :],
                                       start=True, stop=True)
                    mm.then_inc(rb_mm, 1)
                pipelined(pe, B, 2, (0, first), (1, apply), (0, state), (1, spread))

            @block.scalar
            def _(act):
                act.wait_ge(kv_zero, 1)

                def exp(b, s):
                    act.wait_ge(q_mm, b + 1)
                    if later(b, 2):
                        act.wait_ge(q_ok, b - 1)
                    act.activation(split(ex[:, s]), qps[:, 0, :, 0:3 * N], ACT.Exp).then_inc(exp_ok, 1)

                def diagonal(b, s):
                    act.wait_ge(kv_mm, b + 1)
                    if later(b, 2):
                        act.wait_ge(num_mm, b - 1)
                    for half, done in ((0, kv_top), (HD, kv_low)):
                        act.activation(kv[half:half + HD, s, :, half:half + HD].rearrange("p (a b) e -> p a b e", a=2),
                                       kvps[half:half + HD, :, 0:384].rearrange("p a (b n) -> p a b n", n=P)[:, :, :, half:half + HD],
                                       ACT.Copy).then_inc(done, 1)

                def widen(b, s):
                    act.wait_ge(rb_mm, b + 1)
                    if later(b, 2):
                        act.wait_ge(out_ok, b - 1)
                    act.activation(split(rb[:, s]), rps[:, :, 0:3 * N], ACT.Copy).then_inc(rb_ok, 1)
                pipelined(act, B, 2, (0, exp), (0, diagonal), (1, widen))

            @block.vector
            def _(dve):
                dve.wait_ge(loaded, 48)

                def elu(b, s):
                    dve.wait_ge(exp_ok, b + 1)
                    dve.tensor_scalar(ex[:, s], ex[:, s], 1.0, None, ALU.min).then_inc(min_ok, 1)
                    dve.wait_ge(min_ok, b + 1)
                    if later(b, 2):
                        dve.wait_ge(num_mm, b - 1)
                    dve.scalar_tensor_tensor(out=split(q[:, s]), in0=qps[:, 0, :, 0:3 * N], scalar=0.0,
                                             in1=split(ex[:, s]), op0=ALU.max, op1=ALU.add).then_inc(q_ok, 1)
                    dve.tensor_tensor(ksel[:, s], hsel[:], ksum[:, b, :].unsqueeze(2).to_broadcast([P, HP, NH]),
                                      ALU.mult).then_inc(ksel_ok, 1)

                def divide(b, s):
                    dve.wait_ge(den_mm, b + 1)
                    if later(b, 2):
                        dve.wait_ge(rb_mm, b - 1)
                    dve.tensor_scalar(rden[:, s, :], rps[0:NH, 0, 0:N], 1e-6, None, ALU.add).then_inc(den_ok, 1)
                    dve.wait_ge(den_ok, b + 1)
                    dve.reciprocal(rden[:, s, :], rden[:, s, :]).then_inc(rden_ok, 1)

                def result(b, s):
                    dve.wait_ge(rb_ok, b + 1)
                    dve.wait_ge(num_mm, b + 1)
                    dve.tensor_tensor(aT[:, :, bass.ds(b * N, N)].rearrange("p (g h) n -> p g h n", g=2),
                                      nps[:, :, 0:3 * N].rearrange("p g (h n) -> p g h n", n=N),
                                      rb[:, s].rearrange("p (g h) n -> p g h n", g=2), ALU.mult).then_inc(out_ok, 1)
                pipelined(dve, B, 2, (1, divide), (0, elu), (1, result))
                dve.wait_ge(out_ok, B)


def landed(i, s, ring=2):
    return (i - s) * (16 // ring) + 16



def project(m, tag, srcT, chunks, w_name, b_name, h, stats, from_h0):
    with ExitStack() as c:
        x = m.sb(c, tag + "x", [P, 2, chunks, P])
        w = m.sb(c, tag + "w", [P, chunks, D])
        bias = m.sb(c, tag + "b", [P, D])
        ps = m.psum(c, tag + "ps", [P, 2, 512])
        loaded, h_in, x_ok, hb_ok, mm_ok, h_ok, stat = m.sems(c, tag, "loaded h_in x_ok hb_ok mm_ok h_ok stat")
        with m.nc.Block() as block:
            @block.sync
            def _(sp):
                sp.dma_start(w[:], m.ins[w_name]).then_inc(loaded, 16)
                sp.dma_start(bias[:], m.ins[b_name]).then_inc(loaded, 16)
                if from_h0:
                    sp.dma_start(h[:], m.h0.rearrange("(t p) d -> p t d", p=P)).then_inc(h_in, 16)

            @block.gpsimd
            def _(pool):
                pool.wait_ge(loaded, 32)
                if from_h0:
                    pool.wait_ge(h_in, 16)
                pipelined(pool, NT, 2, (0, lambda i, s: pool.tensor_tensor(
                    h[:, i, :], h[:, i, :], bias[:], ALU.add).then_inc(hb_ok, 1)))

            @block.scalar
            def _(act):
                def stage_in(i, s):
                    if later(i, 2):
                        act.wait_ge(mm_ok, i - 1)
                        act.sem_inc(m.passed, 1)
                    act.activation(x[:, s], srcT[:, :, bass.ds(i * P, P)], ACT.Copy).then_inc(x_ok, 1)
                pipelined(act, NT, 2, (0, stage_in))

            @block.tensor
            def _(pe):
                pe.wait_ge(loaded, 32)

                def dense(i, s):
                    pe.wait_ge(x_ok, i + 1)
                    if later(i, 2):
                        pe.wait_ge(h_ok, i - 1)
                    for k in range(chunks):
                        mm = pe.matmul(ps[:, s, 0:D], x[:, s, k, :], w[:, k, :], start=(k == 0), stop=(k == chunks - 1))
                    mm.then_inc(mm_ok, 1)
                pipelined(pe, NT, 2, (0, dense))

            @block.vector
            def _(dve):
                def add(i, s):
                    dve.wait_ge(mm_ok, i + 1)
                    dve.wait_ge(hb_ok, i + 1)
                    dve.tensor_tensor(h[:, i, :], ps[:, s, 0:D], h[:, i, :], ALU.add).then_inc(h_ok, 1)

                def stat_of(i, s):
                    dve.wait_ge(h_ok, i + 1)
                    dve.bn_stats(stats[:, i, :], h[:, i, :]).then_inc(stat, 1)
                pipelined(dve, NT, 2, (0, add), (1, stat_of))
                dve.wait_ge(stat, NT)


def normalised(m, tag, stats, mean, rstd, inv=None):
    with ExitStack() as c:
        var = m.sb(c, tag + "var", [P, NT])
        tmp = m.sb(c, tag + "tmp", [P, NT])
        step, std_ok = m.sems(c, tag, "step std_ok")
        with m.nc.Block() as block:
            @block.vector
            def _(dve):
                moments(m, dve, stats, mean, var, tmp, step)
                dve.wait_ge(std_ok, 1)
                dve.reciprocal(rstd[:], tmp[:]).then_inc(step, 1)
                dve.wait_ge(step, MOMENTS + 1)
                if inv is not None:
                    dve.tensor_tensor(var[:], var[:], rstd[:], ALU.mult).then_inc(step, 1)
                    dve.wait_ge(step, MOMENTS + 2)
                    dve.tensor_tensor(var[:], var[:], rstd[:], ALU.mult).then_inc(step, 1)
                    dve.wait_ge(std_ok, 2)
                    dve.reciprocal(inv[:], tmp[:]).then_inc(step, 1)
                    dve.wait_ge(step, MOMENTS + 4)

            @block.scalar
            def _(act):
                act.wait_ge(step, MOMENTS)
                act.activation(tmp[:], var[:], ACT.Sqrt, bias=m.eps[:, 0:1]).then_inc(std_ok, 1)
                if inv is not None:
                    act.wait_ge(step, MOMENTS + 3)
                    act.activation(tmp[:], var[:], ACT.Sqrt, bias=m.eps[:, 0:1]).then_inc(std_ok, 1)


def gates(m, tag, h, mean, rstd, inv, G, cols, w_name, b_name):
    with ExitStack() as c:
        x = m.sb(c, tag + "x", [P, 4, D])
        tr = m.sb(c, tag + "tr", [P, 4, D])
        tT = m.sb(c, tag + "tT", [DC, 4, 2, P])
        scale = m.sb(c, tag + "scale", [P, D])
        w = m.sb(c, tag + "w", [DC, 2, cols])
        bias = m.sb(c, tag + "b", [P, cols])
        tp = m.psum(c, tag + "tp", [P, 4, 512])
        gp = m.psum(c, tag + "gp", [P, 4, 512])
        loaded, x_ok, t_ok, tp_ok, tT_ok, mm_ok, g_ok = m.sems(c, tag, "loaded x_ok t_ok tp_ok tT_ok mm_ok g_ok")
        with m.nc.Block() as block:
            @block.sync
            def _(sp):
                sp.dma_start(w[:], m.ins[w_name]).then_inc(loaded, 16)
                sp.dma_start(bias[:], m.ins[b_name]).then_inc(loaded, 16)
                sp.dma_start(scale[:], m.ins["norm_scale"]).then_inc(loaded, 16)

            @block.vector
            def _(dve):
                dve.wait_ge(loaded, 48)

                def norm(i, s):
                    if later(i, 4):
                        dve.wait_ge(tp_ok, i - 3)
                    to, done = (tr, t_ok) if inv is None else (x, x_ok)
                    dve.tensor_scalar(to[:, s, :], h[:, i, :], mean[:, bass.ds(i, 1)], rstd[:, bass.ds(i, 1)],
                                      ALU.subtract, ALU.mult).then_inc(done, 1)

                def rms(i, s):
                    dve.wait_ge(x_ok, i + 1)
                    dve.scalar_tensor_tensor(out=tr[:, s, :], in0=x[:, s, :], scalar=inv[:, bass.ds(i, 1)],
                                             in1=scale[:], op0=ALU.mult, op1=ALU.mult).then_inc(t_ok, 1)

                def logits(i, s):
                    dve.wait_ge(mm_ok, i + 1)
                    dve.tensor_tensor(G[:, :, i], gp[:, s, 0:cols], bias[:], ALU.add).then_inc(g_ok, 1)
                pipelined(dve, NT, 4, (0, norm), *([(1, rms)] if inv is not None else []), (3, logits))
                dve.wait_ge(g_ok, NT)

            @block.tensor
            def _(pe):
                pe.wait_ge(loaded, 48)

                def turn(i, s):
                    pe.wait_ge(t_ok, i + 1)
                    if later(i, 4):
                        pe.wait_ge(tT_ok, i - 3)
                    for k in range(2):
                        mm = pe.transpose(tp[0:DC, s, k * P:(k + 1) * P], tr[:, s, k * DC:(k + 1) * DC], m.ident[:])
                    mm.then_inc(tp_ok, 1)

                def dense(i, s):
                    pe.wait_ge(tT_ok, i + 1)
                    if later(i, 4):
                        pe.wait_ge(g_ok, i - 3)
                    for k in range(2):
                        mm = pe.matmul(gp[:, s, 0:cols], tT[:, s, k, :], w[:, k, :], start=(k == 0), stop=(k == 1))
                    mm.then_inc(mm_ok, 1)
                pipelined(pe, NT, 4, (0, turn), (1, dense))

            @block.scalar
            def _(act):
                def copy(i, s):
                    act.wait_ge(tp_ok, i + 1)
                    if later(i, 4):
                        act.wait_ge(mm_ok, i - 3)
                    act.activation(tT[:, s], tp[0:DC, s, 0:2 * P].rearrange("p (c n) -> p c n", c=2), ACT.Copy).then_inc(tT_ok, 1)
                pipelined(act, NT, 4, (0, copy))


def route(m, tag, G, E, K, tiles, slots, weight, comb, expert):
    with ExitStack() as c:
        sb = lambda name, shape, dt=F32: m.sb(c, tag + name, shape, dt)
        rank, cmp_, sel, tot, run, pos, gk = (sb(n, [P, E, NT]) for n in ("rank", "cmp", "sel", "tot", "run", "pos", "gk"))
        top = sb("top", [P, K, NT])
        den = sb("den", [P, NT])
        slot_f = sb("slot_f", [P, K, NT])
        first_mask = sb("mask", [P, E, NT])
        tri = sb("tri", [P, P])
        ones = sb("ones", [P, P])
        steps_of = sb("steps", [P, NT])
        full = sb("full", [P, E, NT])
        ntile, end, base = (sb(n, [P, E]) for n in ("ntile", "end", "base"))
        jrow = sb("jrow", [1, tiles])
        past = sb("past", [1, tiles, E])
        ex_f = sb("ex_f", [1, tiles])
        ps = m.psum(c, tag + "ps", [P, 4, 512])
        loaded, step, sel_ok, mm_ok, e_ok = m.sems(c, tag, "loaded step sel_ok mm_ok e_ok")
        half = E // 2
        with m.nc.Block() as block:
            @block.sync
            def _(sp):
                sp.dma_start(first_mask[:], m.ins["mask%d" % E]).then_inc(loaded, 16)
                sp.dma_start(tri[:], m.ins["tri"]).then_inc(loaded, 16)
                sp.dma_start(ones[:], m.ins["ones"]).then_inc(loaded, 16)
                sp.dma_start(steps_of[:], m.ins["steps"]).then_inc(loaded, 16)
                sp.dma_start(jrow[:], m.ins["jrow"][:, 0:tiles]).then_inc(loaded, 16)

            @block.tensor
            def _(pe):
                pe.wait_ge(loaded, 80)
                pe.wait_ge(sel_ok, 1)
                for a, w in enumerate((tri, ones)):
                    for q in range(2):
                        mm = pe.matmul(ps[:, 2 * a + q, 0:half * NT], w[:],
                                       sel[:, q * half:(q + 1) * half, :].rearrange("p e t -> p (e t)"), start=True, stop=True)
                mm.then_inc(mm_ok, 1)

            @block.scalar
            def _(act):
                act.wait_ge(sel_ok, 2)
                act.activation(gk[:], gk[:], ACT.Exp).then_inc(e_ok, 1)
                act.activation(top[:], top[:], ACT.Exp).then_inc(e_ok, 1)

            @block.vector
            def _(dve):
                n = [0]

                def link(i):
                    n[0] += 1
                    i.then_inc(step, 1)
                    dve.wait_ge(step, n[0])
                dve.wait_ge(loaded, 80)
                link(dve.memset(rank[:], 0.0))
                for e in range(E):
                    it = lambda k: G[:, e:e + 1, :].to_broadcast([P, k, NT])
                    link(dve.memset(cmp_[:, e, :], 0.0))
                    if e:
                        link(dve.tensor_tensor(cmp_[:, 0:e, :], it(e), G[:, 0:e, :], ALU.is_gt))
                    if e < E - 1:
                        link(dve.tensor_tensor(cmp_[:, e + 1:, :], it(E - 1 - e), G[:, e + 1:E, :], ALU.is_ge))
                    link(dve.tensor_tensor(rank[:], rank[:], cmp_[:], ALU.add))
                dve.tensor_scalar(sel[:], rank[:], float(K), None, ALU.is_lt).then_inc(sel_ok, 1)
                for k in range(K):
                    link(dve.scalar_tensor_tensor(out=cmp_[:], in0=rank[:], scalar=float(k), in1=G[:, 0:E, :],
                                                  op0=ALU.is_equal, op1=ALU.mult))
                    link(dve.tensor_reduce(top[:, k, :], cmp_[:].rearrange("p e t -> p t e"), AX, ALU.add))
                link(dve.tensor_tensor(gk[:], G[:, 0:E, :], top[:, 0:1, :].to_broadcast([P, E, NT]), ALU.subtract))
                link(dve.tensor_copy(den[:], top[:, 0, :]))
                link(dve.tensor_tensor(top[:], top[:], den[:].unsqueeze(1).to_broadcast([P, K, NT]), ALU.subtract))
                dve.sem_inc(sel_ok, 1)
                dve.wait_ge(e_ok, 2)
                link(dve.tensor_reduce(den[:], top[:].rearrange("p k t -> p t k"), AX, ALU.add))
                link(dve.reciprocal(den[:], den[:]))
                link(dve.tensor_tensor(weight[:], top[:], den[:].unsqueeze(1).to_broadcast([P, K, NT]), ALU.mult))
                link(dve.tensor_tensor(gk[:], gk[:], sel[:], ALU.mult))
                link(dve.tensor_tensor(comb[:, :, 0:E].rearrange("p t e -> p e t"), gk[:],
                                       den[:].unsqueeze(1).to_broadcast([P, E, NT]), ALU.mult))
                dve.wait_ge(mm_ok, 1)
                for q in range(2):
                    link(dve.tensor_copy(tot[:, q * half:(q + 1) * half, :],
                                         ps[:, 2 + q, 0:half * NT].rearrange("p (e t) -> p e t", t=NT)))
                flat = lambda t: t[:].rearrange("p e t -> p (e t)")
                link(dve.tensor_tensor_scan(flat(run), flat(first_mask), flat(tot), 0.0, ALU.mult, ALU.add))
                link(dve.tensor_tensor(full[:], run[:, :, NT - 1:NT].to_broadcast([P, E, NT]),
                                       steps_of[:].unsqueeze(1).to_broadcast([P, E, NT]), ALU.is_gt))
                link(dve.tensor_reduce(ntile[:], full[:], AX, ALU.add))
                link(dve.tensor_tensor_scan(end[:], ones[:, 0:E], ntile[:], 0.0, ALU.mult, ALU.add))
                link(dve.tensor_tensor(base[:], end[:], ntile[:], ALU.subtract))
                link(dve.tensor_scalar(base[:], base[:], float(P), None, ALU.mult))
                link(dve.tensor_tensor(pos[:], run[:], tot[:], ALU.subtract))
                link(dve.tensor_tensor(pos[:], pos[:], base[:].unsqueeze(2).to_broadcast([P, E, NT]), ALU.add))
                for q in range(2):
                    link(dve.tensor_tensor(pos[:, q * half:(q + 1) * half, :],
                                           ps[:, q, 0:half * NT].rearrange("p (e t) -> p e t", t=NT),
                                           pos[:, q * half:(q + 1) * half, :], ALU.add))
                for k in range(K):
                    link(dve.scalar_tensor_tensor(out=cmp_[:], in0=rank[:], scalar=float(k), in1=pos[:],
                                                  op0=ALU.is_equal, op1=ALU.mult))
                    link(dve.tensor_reduce(slot_f[:, k, :], cmp_[:].rearrange("p e t -> p t e"), AX, ALU.add))
                    link(dve.tensor_copy(slots[:, :, k], slot_f[:, k, :]))
                link(dve.tensor_tensor(past[:], jrow[:].unsqueeze(2).to_broadcast([1, tiles, E]),
                                       end[0:1, :].unsqueeze(1).to_broadcast([1, tiles, E]), ALU.is_ge))
                link(dve.tensor_reduce(ex_f[:], past[:], AX, ALU.add))
                link(dve.tensor_scalar(ex_f[:], ex_f[:], float(E - 1), None, ALU.min))
                link(dve.tensor_copy(expert[:], ex_f[:]))


def scatter(m, tag, h, mean, rstd, inv, slots, K, loads):
    with ExitStack() as c:
        x = m.sb(c, tag + "x", [P, 3, D])
        row = m.sb(c, tag + "row", [P, 3, D])
        scale = m.sb(c, tag + "scale", [P, D])
        at = m.sb(c, tag + "at", [P, 3, K], U32)
        x_ok, h_ok, row_ok, at_ok, loaded, scale_in = m.sems(c, tag, "x_ok h_ok row_ok at_ok loaded scale_in")
        sent = m.sems(c, tag, "sent0 sent1 sent2")
        with m.nc.Block() as block:
            @block.sync
            def _(sp):
                sp.dma_start(scale[:], m.ins["norm_scale"]).then_inc(scale_in, 16)
                for to, name in loads:
                    sp.dma_start(to, m.ins[name]).then_inc(loaded, 16)
                sp.wait_ge(loaded, 16 * len(loads))

            @block.vector
            def _(dve):
                dve.wait_ge(scale_in, 16)

                def prepare(i, s):
                    if later(i, 3):
                        dve.wait_ge(sent[s], (i - s) * 16 * K // 3)
                    dve.sem_inc(m.passed, 1)
                    dve.tensor_copy(at[:, s, :], slots[:, i, :]).then_inc(at_ok, 1)
                    to, done = (row, row_ok) if inv is None else (x, x_ok)
                    dve.tensor_scalar(to[:, s, :], h[:, i, :], mean[:, bass.ds(i, 1)], rstd[:, bass.ds(i, 1)],
                                      ALU.subtract, ALU.mult).then_inc(done, 1)
                    if inv is not None:
                        dve.wait_ge(x_ok, i + 1)
                        dve.scalar_tensor_tensor(out=row[:, s, :], in0=x[:, s, :], scalar=inv[:, bass.ds(i, 1)],
                                                 in1=scale[:], op0=ALU.mult, op1=ALU.mult).then_inc(row_ok, 1)
                        dve.tensor_tensor(h[:, i, :], h[:, i, :], x[:, s, :], ALU.add).then_inc(h_ok, 1)
                pipelined(dve, NT, 3, (0, prepare))
                if inv is not None:
                    dve.wait_ge(h_ok, NT)

            @block.gpsimd
            def _(pool):
                def send(i, s):
                    pool.wait_ge(row_ok, i + 1)
                    pool.sem_inc(m.passed, 1)
                    pool.wait_ge(at_ok, i + 1)
                    pool.sem_inc(m.passed, 1)
                    for k in range(K):
                        pool.indirect_dma_start(out=m.xs, out_offset=bass.IndirectOffsetOnAxis(ap=at[:, s, k:k + 1], axis=0),
                                                in_=row[:, s, :], in_offset=None).then_inc(sent[s], 16)
                pipelined(pool, NT, 3, (0, send))
                for s in range(3):
                    pool.wait_ge(sent[s], 16 * K * (NT // 3))


def experts(m, tag, E, C, gated, tiles, w1, w2, expert, beside=None):
    I = C * P
    HW = 384
    AB = -(-C // 3)
    XB = 2 if AB == 1 else 1
    with ExitStack() as c:
        xin = m.sb(c, tag + "xin", [P, 4, D])
        xT = m.sb(c, tag + "xT", [P, 2, 2, P])
        a = m.sb(c, tag + "a", [P, 2, I])
        glu, lin, sig = ((m.sb(c, tag + n, [P, 2, HW]) for n in ("glu", "lin", "sig")) if gated else (None,) * 3)
        aT = m.sb(c, tag + "aT", [P, 2, C, P])
        y = m.sb(c, tag + "y", [P, 2, D])
        xps = m.psum(c, tag + "xps", [P, XB, 512])
        hps = m.psum(c, tag + "hps", [P, 2, 2, 512])
        aps = m.psum(c, tag + "aps", [P, AB, 512])
        yps = m.psum(c, tag + "yps", [P, 512])
        ones_ok, xp_ok, xT_ok, h0_ok, h1_ok, glu_ok, sig_ok, lin_ok, prod_ok, a_ok, ap_ok, aT_ok, y_mm, y_ok = m.sems(
            c, tag, "ones_ok xp_ok xT_ok h0_ok h1_ok glu_ok sig_ok lin_ok prod_ok a_ok ap_ok aT_ok y_mm y_ok")
        arrived = m.sems(c, tag, "in0 in1 in2 in3")
        stored = m.sems(c, tag, "out0 out1")
        with m.nc.Block() as block:
            @block.sync
            def _(sp):
                def load(i, s):
                    if later(i, 4):
                        sp.wait_ge(xp_ok, i - 3)
                    sp.dma_start(xin[:, s, :], m.xs[bass.ds(i * P, P), :]).then_inc(arrived[s], 16)

                def store(i, s):
                    sp.wait_ge(y_ok, i + 1)
                    sp.dma_start(m.ys[bass.ds(i * P, P), :], y[:, s % 2, :]).then_inc(stored[s % 2], 16)
                pipelined(sp, tiles, 4, (0, load), (6, store))
                for s in range(2):
                    sp.wait_ge(stored[s], 16 * (tiles // 2))

            @block.gpsimd
            def _(pool):
                pool.memset(xT[DC:DC + 1, :, 1, :], 1.0).then_inc(ones_ok, 1)

            @block.tensor
            def _(pe):
                pe.wait_ge(ones_ok, 1)

                def turn_x(i, s):
                    pe.wait_ge(arrived[s], landed(i, s, 4))
                    if later(i, XB):
                        pe.wait_ge(xT_ok, i - XB + 1)
                    for k in range(2):
                        mm = pe.transpose(xps[0:DC, s % XB, k * P:(k + 1) * P], xin[:, s, k * DC:(k + 1) * DC], m.ident[:])
                    mm.then_inc(xp_ok, 1)

                def up(i, s, half):
                    s %= 2
                    if half == 0:
                        pe.wait_ge(xT_ok, i + 1)
                        if later(i, 2):
                            pe.wait_ge(lin_ok if gated else a_ok, i - 1)
                    e = expert_of["up"]
                    for k in range(2):
                        r = DC + k
                        mm = pe.matmul(hps[:, s, half, 0:HW], xT[0:r, s, k, :],
                                       w1[0:r, e, k, half * HW:(half + 1) * HW], start=(k == 0), stop=(k == 1))
                    mm.then_inc((h0_ok, h1_ok)[half], 1)

                def turn_a(i, s):
                    s %= 2
                    pe.wait_ge(a_ok, i + 1)
                    if later(i, 1):
                        pe.wait_ge(aT_ok, i * AB)
                    for k in range(C):
                        mm = pe.transpose(aps[:, k // 3, (k % 3) * P:(k % 3 + 1) * P], a[:, s, k * P:(k + 1) * P], m.ident[:])
                    mm.then_inc(ap_ok, 1)

                def down(i, s):
                    s %= 2
                    pe.wait_ge(aT_ok, (i + 1) * AB)
                    if later(i, 1):
                        pe.wait_ge(y_ok, i)
                    e = expert_of["down"]
                    for k in range(C):
                        mm = pe.matmul(yps[:, 0:D], aT[:, s, k, :], w2[:, e, k, :], start=(k == 0), stop=(k == C - 1))
                    mm.then_inc(y_mm, 1)

                expert_of = {}

                def look_up(use):
                    def fetch(i, s):
                        at = expert[0:1, i:i + 1] if isinstance(i, int) else expert[0:1, bass.ds(i, 1)]
                        expert_of[use] = pe.value_load(at, min_val=0, max_val=E - 1)
                    return fetch
                pipelined(pe, tiles, 4, (1, look_up("up")), (0, turn_x), (1, lambda i, s: up(i, s, 0)), (3, turn_a),
                          (1, lambda i, s: up(i, s, 1)), (3, look_up("down")), (3, down))

            @block.scalar
            def _(act):
                def copy_x(i, s):
                    act.wait_ge(xp_ok, i + 1)
                    if later(i, 2):
                        act.wait_ge(h1_ok, i - 1)
                    act.activation(xT[0:DC, s], xps[0:DC, s % XB, 0:2 * P].rearrange("p (c n) -> p c n", c=2),
                                   ACT.Copy).then_inc(xT_ok, 1)

                def copy_a(i, s):
                    act.wait_ge(ap_ok, i + 1)
                    if later(i, 2):
                        act.wait_ge(y_mm, i - 1)
                    act.activation(aT[:, s, 0:3, :], aps[:, 0, 0:HW].rearrange("p (c n) -> p c n", n=P),
                                   ACT.Copy).then_inc(aT_ok, 1)

                def squash(i, s):
                    act.wait_ge(glu_ok, i + 1)
                    if later(i, 2):
                        act.wait_ge(prod_ok, i - 1)
                    act.activation(sig[:, s, :], glu[:, s, :], ACT.Sigmoid, scale=1.702).then_inc(sig_ok, 1)

                def gelu(i, s):
                    act.wait_ge(h1_ok, i + 1)
                    if later(i, 2):
                        act.wait_ge(ap_ok, i - 1)
                    act.activation(a[:, s, :].rearrange("p (g n) -> p g n", g=2), hps[:, s, :, 0:HW],
                                   ACT.Gelu_apprx_tanh).then_inc(a_ok, 1)

                def copy_y(i, s):
                    act.wait_ge(y_mm, i + 1)
                    if later(i, 2):
                        act.wait_ge(stored[s], landed(i, s) - 16)
                    act.activation(y[:, s, :], yps[:, 0:D], ACT.Copy).then_inc(y_ok, 1)
                pipelined(act, tiles, 2, (0, copy_x), *([(3, copy_a), (1, squash)] if gated else [(1, gelu), (3, copy_a)]), (3, copy_y))

            @block.vector
            def _(dve):
                def gate(i, s):
                    dve.wait_ge(h0_ok, i + 1)
                    dve.tensor_scalar(glu[:, s, :], hps[:, s, 0, 0:HW], 7.0, None, ALU.min).then_inc(glu_ok, 1)
                    dve.wait_ge(sig_ok, i + 1)
                    dve.tensor_tensor(sig[:, s, :], glu[:, s, :], sig[:, s, :], ALU.mult).then_inc(prod_ok, 1)
                    dve.wait_ge(h1_ok, i + 1)
                    dve.tensor_scalar(lin[:, s, :], hps[:, s, 1, 0:HW], 7.0, -7.0, ALU.min, ALU.max).then_inc(lin_ok, 1)
                    dve.wait_ge(lin_ok, i + 1)
                    dve.wait_ge(prod_ok, i + 1)
                    if later(i, 2):
                        dve.wait_ge(ap_ok, i - 1)
                    dve.scalar_tensor_tensor(out=a[:, s, :], in0=lin[:, s, :], scalar=1.0, in1=sig[:, s, :],
                                             op0=ALU.add, op1=ALU.mult).then_inc(a_ok, 1)

                def copy_a(i, s):
                    dve.wait_ge(ap_ok, i + 1)
                    if later(i, 2):
                        dve.wait_ge(y_mm, i - 1)
                    dve.tensor_copy(aT[:, s, 3:6, :], aps[:, 1, 0:HW].rearrange("p (c n) -> p c n", n=P)).then_inc(aT_ok, 1)
                pipelined(dve, tiles, 2, *([(1, gate)] if gated else [
                    (0, lambda i, s: beside(dve, i, 0)), (3, copy_a), (0, lambda i, s: beside(dve, i, 1))]))


def gather(m, tag, h, slots, weight, comb, E, K, extra, stats=None):
    R = E + extra
    with ExitStack() as c:
        g = m.sb(c, tag + "g", [P, 3, K, D])
        at = m.sb(c, tag + "at", [P, 3, K], U32)
        cb = m.sb(c, tag + "cb", [P, 3, R])
        cT = m.sb(c, tag + "cT", [R, 3, P])
        rows = m.sb(c, tag + "rows", [R, D])
        times = m.sb(c, tag + "times", [R, D])
        tp = m.psum(c, tag + "tp", [P, 3, 512])
        ps = m.psum(c, tag + "ps", [P, 3, 512])
        at_ok, cb_ok, tp_ok, cT_ok, mm_ok, chain, bias_ok, used, stat, loaded, rows_ok, stored = m.sems(
            c, tag, "at_ok cb_ok tp_ok cT_ok mm_ok chain bias_ok used stat loaded rows_ok stored")
        here = m.sems(c, tag, "g0 g1 g2")
        with m.nc.Block() as block:
            @block.sync
            def _(sp):
                sp.dma_start(rows[:], m.ins[tag + "_rows"]).then_inc(loaded, 16)
                sp.dma_start(times[:], m.ins[tag + "_times"]).then_inc(loaded, 16)
                if stats is None:
                    def store(i, s):
                        sp.wait_ge(used, i + 1)
                        sp.dma_start(m.out[bass.ds(i * P, P), :], h[:, i, :]).then_inc(stored, 16)
                    pipelined(sp, NT, 3, (0, store))
                    sp.wait_ge(stored, 16 * NT)

            @block.scalar
            def _(act):
                def copy(i, s):
                    if later(i, 3):
                        act.wait_ge(tp_ok, i - 2)
                    act.sem_inc(m.passed, 1)
                    act.activation(cb[:, s, :], comb[:, i, 0:R], ACT.Copy).then_inc(cb_ok, 1)

                def rows_of(i, s):
                    act.wait_ge(tp_ok, i + 1)
                    if later(i, 3):
                        act.wait_ge(mm_ok, i - 2)
                    act.activation(cT[:, s, :], tp[0:R, s, 0:P], ACT.Copy).then_inc(cT_ok, 1)
                pipelined(act, NT, 3, (0, copy), (1, rows_of))

            @block.tensor
            def _(pe):
                pe.wait_ge(rows_ok, 1)

                def turn(i, s):
                    pe.wait_ge(cb_ok, i + 1)
                    if later(i, 3):
                        pe.wait_ge(cT_ok, i - 2)
                    pe.transpose(tp[0:R, s, 0:P], cb[:, s, :], m.ident[:]).then_inc(tp_ok, 1)

                def dense(i, s):
                    pe.wait_ge(cT_ok, i + 1)
                    if later(i, 3):
                        pe.wait_ge(bias_ok, i - 2)
                    pe.matmul(ps[:, s, 0:D], cT[:, s, :], rows[:], start=True, stop=True).then_inc(mm_ok, 1)
                pipelined(pe, NT, 3, (0, turn), (1, dense))

            @block.gpsimd
            def _(pool):
                def fetch(i, s):
                    pool.wait_ge(at_ok, i + 1)
                    pool.sem_inc(m.passed, 1)
                    if later(i, 3):
                        pool.wait_ge(used, i - 2)
                        pool.sem_inc(m.passed, 1)
                    for k in range(K):
                        pool.indirect_dma_start(out=g[:, s, k, :], out_offset=None, in_=m.ys,
                                                in_offset=bass.IndirectOffsetOnAxis(ap=at[:, s, k:k + 1], axis=0)
                                                ).then_inc(here[s], 16)
                pipelined(pool, NT, 3, (0, fetch))

            @block.vector
            def _(dve):
                dve.wait_ge(loaded, 32)
                dve.tensor_tensor(rows[:], rows[:], times[:], ALU.mult).then_inc(rows_ok, 1)

                def index(i, s):
                    if later(i, 3):
                        dve.wait_ge(here[s], K * (landed(i, s, 3) - 16) if isinstance(i, int) else (i - s) * 16 * K // 3)
                    dve.sem_inc(m.passed, 1)
                    dve.tensor_copy(at[:, s, :], slots[:, i, :]).then_inc(at_ok, 1)

                def add(i, s):
                    dve.wait_ge(mm_ok, i + 1)
                    dve.tensor_tensor(h[:, i, :], ps[:, s, 0:D], h[:, i, :], ALU.add).then_inc(bias_ok, 1)
                    dve.wait_ge(here[s], (i - s) * 16 * K // 3 + 16 * K)
                    dve.wait_ge(bias_ok, i + 1)
                    for k in range(K):
                        if k:
                            dve.wait_ge(chain, i * (K - 1) + k)
                        dve.scalar_tensor_tensor(out=h[:, i, :], in0=g[:, s, k, :], scalar=weight[:, k, bass.ds(i, 1)],
                                                 in1=h[:, i, :], op0=ALU.mult, op1=ALU.add
                                                 ).then_inc(chain if k < K - 1 else used, 1)
                    if stats is not None:
                        dve.wait_ge(used, i + 1)
                        dve.bn_stats(stats[:, i, :], h[:, i, :]).then_inc(stat, 1)
                pipelined(dve, NT, 3, (0, index), (2, add))
                if stats is not None:
                    dve.wait_ge(stat, NT)


MAGIC = 12582912.0


def quantised_attention(m, xT, oT):
    LAST = slice(N - 32, N)
    VC = QH * 32
    with ExitStack() as c:
        sb = lambda name, shape, dt=F32: m.sb(c, "qa_" + name, shape, dt)
        wqk = sb("wqk", [DC, 2, 2, QC * P])
        wv = sb("wv", [DC, 2, QH * 32])
        sc = sb("sc", [P, 6])
        inv = sb("inv", [P, 6])
        mul = sb("mul", [P, 4])
        magic = sb("magic", [P, 1])
        xs = sb("xs", [DC, 2, 2, N])
        r = sb("r", [P, 2, 2, QC * N])
        rv = sb("rv", [P, 2, VC + QC * 32])
        qk = sb("qk", [P, 2, 2, QC * N], BF16)
        v = sb("v", [P, 2, VC + QC * 32], BF16)
        rs = sb("rs", [P, 5, 3 * N])
        s = sb("s", [P, 2, 5, 3 * N], BF16)
        ro = sb("ro", [P, 2, QC * N])
        qps = m.psum(c, "qa_qps", [P, 2, 512])
        sps = m.psum(c, "qa_sps", [P, 5, 512])
        ops_ = m.psum(c, "qa_ops", [P, 512])
        (loaded, const, xs_ok, q_mm, r_ok, rc_ok, qk_ok, v_mm, rv_ok, rvc_ok, v_ok, s_mm, rs_ok, rsc_ok, s_ok, o_mm, ro_ok,
         roc_ok, o_ok, magic_ok) = m.sems(
            c, "qa", "loaded const xs_ok q_mm r_ok rc_ok qk_ok v_mm rv_ok rvc_ok v_ok s_mm rs_ok rsc_ok s_ok o_mm ro_ok "
            "roc_ok o_ok magic_ok")
        with m.nc.Block() as block:
            @block.sync
            def _(sp):
                sp.dma_start(wqk[:], m.ins["q_wqk"]).then_inc(loaded, 16)
                sp.dma_start(wv[:], m.ins["q_wv"]).then_inc(loaded, 16)
                sp.dma_start(sc[:], m.ins["q_scales"]).then_inc(loaded, 16)

            @block.gpsimd
            def _(pool):
                pool.memset(magic[:], MAGIC).then_inc(magic_ok, 1)

                def widen(b, p):
                    pool.wait_ge(rc_ok, b + 1)
                    if later(b, 2):
                        pool.wait_ge(s_mm, b - 1)
                    pool.sem_inc(m.passed, 1)
                    pool.tensor_scalar(qk[:, p], r[:, p], -MAGIC, 1.0, ALU.add, ALU.mult).then_inc(qk_ok, 1)

                def widen_v(b, p):
                    pool.wait_ge(rvc_ok, b + 1)
                    if later(b, 2):
                        pool.wait_ge(o_mm, b - 1)
                    pool.sem_inc(m.passed, 1)
                    pool.tensor_scalar(v[:, p], rv[:, p], -MAGIC, 1.0, ALU.add, ALU.mult).then_inc(v_ok, 1)
                pipelined(pool, B, 2, (0, widen), (0, widen_v))

            @block.tensor
            def _(pe):
                pe.wait_ge(loaded, 48)

                def project_(b, p):
                    pe.wait_ge(xs_ok, b + 1)
                    if later(b, 1):
                        pe.wait_ge(rv_ok, b)
                    for w in range(2):
                        for ch in range(QC):
                            for k in range(2):
                                mm = pe.matmul(qps[:, w, ch * N:(ch + 1) * N], wqk[:, k, w, ch * P:(ch + 1) * P],
                                               xs[:, p, k, :], start=(k == 0), stop=(k == 1))
                    mm.then_inc(q_mm, 1)

                def values(b, p):
                    pe.wait_ge(r_ok, b + 1)
                    for k in range(2):
                        pe.matmul(qps[:, 0, 0:QH * 32], xs[:, p, k, 0:P], wv[:, k, :], start=(k == 0), stop=(k == 1))
                    for j in range(4):
                        for k in range(2):
                            mm = pe.matmul(qps[32 * j:32 * j + 32, 1, 0:QC * 32], xs[:, p, k, LAST],
                                           wv[:, k, :].rearrange("p (c j d) -> p j c d", j=4, d=32)[:, j],
                                           start=(k == 0), stop=(k == 1), tile_position=(0, 32 * j))
                    mm.then_inc(v_mm, 1)

                def scores(b, p):
                    pe.wait_ge(qk_ok, b + 1)
                    if later(b, 1):
                        pe.wait_ge(rs_ok, b)
                    for h in range(QH):
                        ch, j = h // 4, h % 4
                        at = slice(32 * j, 32 * j + QD)
                        q_, k_ = (qk[at, p, w, ch * N:(ch + 1) * N] for w in (0, 1))
                        pe.matmul(sps[:, j, ch * N:(ch + 1) * N], k_[:, 0:P], q_, start=True, stop=True,
                                  tile_position=(32 * j, 0))
                        mm = pe.matmul(sps[32 * j:32 * j + 32, 4, ch * N:(ch + 1) * N], k_[:, LAST], q_, start=True, stop=True,
                                       tile_position=(32 * j, 32 * j))
                    mm.then_inc(s_mm, 1)

                def outputs(b, p):
                    pe.wait_ge(s_ok, b + 1)
                    pe.wait_ge(v_ok, b + 1)
                    if later(b, 1):
                        pe.wait_ge(ro_ok, b)
                    for h in range(QH):
                        ch, j = h // 4, h % 4
                        to = ops_[32 * j:32 * j + 32, ch * N:(ch + 1) * N]
                        pe.matmul(to, v[:, p, h * 32:(h + 1) * 32], s[:, p, j, ch * N:(ch + 1) * N],
                                  start=True, stop=False, tile_position=(0, 32 * j))
                        at = slice(32 * j, 32 * j + 32)
                        mm = pe.matmul(to, v[at, p, VC + ch * 32:VC + (ch + 1) * 32], s[at, p, 4, ch * N:(ch + 1) * N],
                                       start=False, stop=True, tile_position=(32 * j, 32 * j))
                    mm.then_inc(o_mm, 1)
                pipelined(pe, B, 2, (0, project_), (1, scores), (0, values), (2, outputs))

            @block.scalar
            def _(act):
                act.wait_ge(const, 2)
                act.wait_ge(magic_ok, 1)
                bias = magic[:, 0:1]

                def round_qk(b, p):
                    act.wait_ge(q_mm, b + 1)
                    if later(b, 2):
                        act.wait_ge(qk_ok, b - 1)
                    for w in range(2):
                        i = act.activation(r[:, p, w, :], qps[:, w, 0:QC * N], ACT.Identity, bias=bias, scale=inv[:, w:w + 1])
                    i.then_inc(r_ok, 1)

                def round_v(b, p):
                    act.wait_ge(v_mm, b + 1)
                    if later(b, 2):
                        act.wait_ge(v_ok, b - 1)
                    act.activation(rv[:, p, 0:VC], qps[:, 0, 0:VC], ACT.Identity, bias=bias, scale=inv[:, 2:3])
                    act.activation(rv[:, p, VC:], qps[:, 1, 0:QC * 32], ACT.Identity, bias=bias,
                                   scale=inv[:, 5:6]).then_inc(rv_ok, 1)

                def round_s(b, p):
                    act.wait_ge(s_mm, b + 1)
                    if later(b, 1):
                        act.wait_ge(s_ok, b)
                    act.activation(rs[:], sps[:, :, 0:3 * N], ACT.Identity, bias=bias, scale=mul[:, 0:1]).then_inc(rs_ok, 1)

                def round_o(b, p):
                    act.wait_ge(o_mm, b + 1)
                    if later(b, 2):
                        act.wait_ge(o_ok, b - 1)
                    act.activation(ro[:, p, :], ops_[:, 0:QC * N], ACT.Identity, bias=bias, scale=mul[:, 1:2]).then_inc(ro_ok, 1)
                pipelined(act, B, 2, (0, round_qk), (1, round_s), (0, round_v), (2, round_o))

            @block.vector
            def _(dve):
                dve.wait_ge(loaded, 48)
                dve.reciprocal(inv[:, 0:5], sc[:, 0:5]).then_inc(const, 1)
                n = [0]

                def link(i):
                    n[0] += 1
                    i.then_inc(m.var_raw, 1)
                    m.var_raws += 1
                    dve.wait_ge(m.var_raw, m.var_raws)
                dve.wait_ge(const, 1)
                link(dve.tensor_tensor(mul[:, 0:1], sc[:, 0:1], sc[:, 1:2], ALU.mult))
                link(dve.tensor_tensor(mul[:, 0:1], mul[:, 0:1], inv[:, 3:4], ALU.mult))
                link(dve.tensor_scalar(mul[:, 0:1], mul[:, 0:1], float(QD) ** -0.5 / N, None, ALU.mult))
                link(dve.tensor_tensor(mul[:, 1:2], sc[:, 3:4], sc[:, 2:3], ALU.mult))
                link(dve.tensor_tensor(inv[:, 5:6], inv[:, 2:3], sc[:, 5:6], ALU.mult))
                dve.tensor_tensor(mul[:, 1:2], mul[:, 1:2], inv[:, 4:5], ALU.mult).then_inc(const, 1)

                def stage_in(b, p):
                    if later(b, 2):
                        dve.wait_ge(v_mm, b - 1)
                    dve.sem_inc(m.passed, 1)
                    dve.tensor_copy(xs[:, p], xT[:, :, bass.ds(b * N, N)]).then_inc(xs_ok, 1)

                def clip(t, low, high, done):
                    dve.tensor_scalar(t, t, MAGIC + low, MAGIC + high, ALU.max, ALU.min).then_inc(done, 1)

                def inputs(b, p):
                    dve.wait_ge(r_ok, b + 1)
                    clip(r[:, p], -4.0, 3.0, rc_ok)

                def input_v(b, p):
                    dve.wait_ge(rv_ok, b + 1)
                    clip(rv[:, p], -4.0, 3.0, rvc_ok)

                def scores(b, p):
                    dve.wait_ge(rs_ok, b + 1)
                    clip(rs[:], 0.0, 7.0, rsc_ok)
                    dve.wait_ge(rsc_ok, b + 1)
                    if later(b, 2):
                        dve.wait_ge(o_mm, b - 1)
                    dve.tensor_scalar(s[:, p], rs[:], MAGIC, None, ALU.subtract).then_inc(s_ok, 1)

                def outputs(b, p):
                    dve.wait_ge(ro_ok, b + 1)
                    clip(ro[:, p, :], -4.0, 3.0, roc_ok)
                    dve.wait_ge(roc_ok, b + 1)
                    dve.tensor_scalar(oT[:, :, bass.ds(b * N, N)], ro[:, p, :].rearrange("p (c n) -> p c n", c=QC),
                                      MAGIC, sc[:, 4:5], ALU.subtract, ALU.mult).then_inc(o_ok, 1)
                pipelined(dve, B, 2, (0, stage_in), (1, inputs), (2, scores), (1, input_v), (3, outputs))
                dve.wait_ge(o_ok, B)


class Spectral:

    def __init__(self, m, ctx, steps):
        assert steps >= N - 1
        sb = lambda name, shape: m.sb(ctx, "sp_" + name, shape)
        self.m, self.steps = m, steps
        self.raw = sb("raw", [2 * B, N])
        self.sign = sb("sign", [2 * B, N])
        self.a2 = sb("a2", [2 * B, steps + 1, 2])
        self.d = sb("d", [2 * B, steps + 1, 2])
        self.cur = sb("cur", [2 * B, 2, 2])
        self.sq = sb("sq", [2 * B, 2, 2])
        self.mag = sb("mag", [2 * B, 2])
        self.rec = sb("rec", [2 * B, 2])
        self.sq_ok, self.rec_ok, self.cur_ok, self.d_ok = m.sems(ctx, "sp", "sq_ok rec_ok cur_ok d_ok")

    def start(self, G, col):
        m, raw, sign, a2 = self.m, self.raw, self.sign, self.a2
        with ExitStack() as c:
            v = m.sb(c, "sp_v", [P, NT])
            vT = m.sb(c, "sp_vT", [NT, P])
            ps = m.psum(c, "sp_ps", [P, 512])
            step, vp_ok, vT_ok, there, raw_ok, sign_ok = m.sems(c, "ss", "step vp_ok vT_ok there raw_ok sign_ok")
            with m.nc.Block() as block:
                @block.sync
                def _(sp):
                    sp.dma_start(sign[:], m.ins["sign"]).then_inc(sign_ok, 16)
                    sp.wait_ge(vT_ok, 1)
                    sp.dma_start(m.v_row.rearrange("(t p) -> t p", p=P), vT[:]).then_inc(there, 16)
                    sp.wait_ge(there, 16)
                    for k in range(2):
                        sp.dma_start(raw[k * B:(k + 1) * B, :], m.v_row.rearrange("(b n) -> b n", n=N)).then_inc(raw_ok, 16)

                @block.tensor
                def _(pe):
                    pe.wait_ge(step, 2)
                    pe.transpose(ps[0:NT, 0:P], v[:], m.ident[:]).then_inc(vp_ok, 1)

                @block.vector
                def _(dve):
                    n = [0]

                    def link(i):
                        n[0] += 1
                        i.then_inc(step, 1)
                        dve.wait_ge(step, n[0])
                    link(dve.tensor_scalar(v[:], G[:, col, :], 3.0, -3.0, ALU.min, ALU.max))
                    link(dve.tensor_scalar(v[:], v[:], 2.0, None, ALU.subtract))
                    dve.wait_ge(vp_ok, 1)
                    dve.tensor_copy(vT[:], ps[0:NT, 0:P]).then_inc(vT_ok, 1)
                    link(dve.memset(a2[:], -1.0))
                    dve.wait_ge(raw_ok, 32)
                    dve.wait_ge(sign_ok, 16)
                    link(dve.tensor_tensor(a2[0:B, 0:N, 0], raw[0:B, :], sign[0:B, :], ALU.mult))
                    link(dve.tensor_tensor(a2[B:2 * B, 0:N, 0], raw[B:2 * B, ::-1], sign[B:2 * B, :], ALU.mult))
                    dve.tensor_copy(self.cur[:, 0, :], a2[:, 0, :]).then_inc(self.cur_ok, 1)
                    link(dve.tensor_copy(self.d[:, 0, :], a2[:, 0, :]))

    def step(self, dve, i, s):
        cur, sq, mag, rec = self.cur, self.sq, self.mag, self.rec
        dve.wait_ge(self.cur_ok, i + 1)
        dve.tensor_tensor(sq[:, s, :], cur[:, s, :], cur[:, s, :], ALU.mult).then_inc(self.sq_ok, 1)
        dve.wait_ge(self.sq_ok, 2 * i + 1)
        dve.tensor_tensor(mag[:, s:s + 1], sq[:, s, 0:1], sq[:, s, 1:2], ALU.add).then_inc(self.sq_ok, 1)
        dve.wait_ge(self.sq_ok, 2 * i + 2)
        dve.reciprocal(rec[:, s:s + 1], mag[:, s:s + 1]).then_inc(self.rec_ok, 1)
        dve.wait_ge(self.rec_ok, i + 1)
        dve.scalar_tensor_tensor(out=cur[:, 1 - s, :], in0=cur[:, s, :], scalar=rec[:, s:s + 1],
                                 in1=self.a2[:, i + 1, :], op0=ALU.mult, op1=ALU.add).then_inc(self.cur_ok, 1)
        dve.wait_ge(self.cur_ok, i + 2)
        dve.sem_inc(self.m.passed, 1)
        dve.tensor_copy(self.d[:, i + 1, :], cur[:, 1 - s, :]).then_inc(self.d_ok, 1)

    def finish(self, feats):
        m, raw, sign = self.m, self.raw, self.sign
        d = self.d[:, 0:N, :]
        with ExitStack() as c:
            sb = lambda name, shape: m.sb(c, "sp_" + name, shape)
            back = sb("back", [B, N, 2])
            rev = sb("rev", [2 * B, N, 2])
            s2 = sb("s2", [B, N, 2])
            q = sb("q", [B, N, 2])
            n2 = sb("n2", [B, N])
            f = sb("f", [NT, P, 2])
            fp = m.psum(c, "sp_fp", [P, 2, 512])
            step, rev_ok, back_ok, q_ok, q_there, f_in, f_mm = m.sems(c, "sf", "step rev_ok back_ok q_ok q_there f_in f_mm")
            with m.nc.Block() as block:
                @block.sync
                def _(sp):
                    sp.wait_ge(rev_ok, 1)
                    sp.dma_start(back[:], rev[B:2 * B]).then_inc(back_ok, 16)
                    sp.wait_ge(q_ok, 1)
                    sp.dma_start(m.f_row.rearrange("(b n) c -> b n c", n=N), q[:]).then_inc(q_there, 16)
                    sp.wait_ge(q_there, 16)
                    sp.dma_start(f[:], m.f_row.rearrange("(t p) c -> t p c", p=P)).then_inc(f_in, 16)

                @block.tensor
                def _(pe):
                    pe.wait_ge(f_in, 16)
                    for k in range(2):
                        pe.transpose(fp[:, k, 0:NT], f[:, :, k], m.ident[0:NT, 0:NT]).then_inc(f_mm, 1)

                @block.vector
                def _(dve):
                    n = [0]

                    def link(i):
                        n[0] += 1
                        i.then_inc(step, 1)
                        dve.wait_ge(step, n[0])
                    dve.wait_ge(self.d_ok, self.steps)
                    link(dve.tensor_tensor(d[:, :, 0], d[:, :, 0], sign[:], ALU.mult))
                    dve.tensor_copy(rev[B:2 * B], d[B:2 * B, ::-1, :]).then_inc(rev_ok, 1)
                    dve.wait_ge(back_ok, 16)
                    link(dve.tensor_tensor(s2[:], d[0:B], back[:], ALU.add))
                    link(dve.tensor_tensor(s2[:, :, 0], s2[:, :, 0], raw[0:B, :], ALU.subtract))
                    link(dve.tensor_scalar(s2[:, :, 1], s2[:, :, 1], 1.0, None, ALU.add))
                    link(dve.tensor_tensor(q[:], s2[:], s2[:], ALU.mult))
                    link(dve.tensor_tensor(n2[:], q[:, :, 0], q[:, :, 1], ALU.add))
                    link(dve.reciprocal(n2[:], n2[:]))
                    link(dve.tensor_tensor(q[:, :, 0], s2[:, :, 0], n2[:], ALU.mult))
                    link(dve.scalar_tensor_tensor(out=q[:, :, 1], in0=s2[:, :, 1], scalar=-1.0, in1=n2[:],
                                                  op0=ALU.mult, op1=ALU.mult))
                    dve.tensor_scalar(q[:], q[:], 10.0, -10.0, ALU.min, ALU.max).then_inc(q_ok, 1)
                    link(dve.memset(feats[:, :, 2], 1.0))
                    for k in range(2):
                        dve.wait_ge(f_mm, k + 1)
                        link(dve.tensor_copy(feats[:, :, k], fp[:, k, 0:NT]))


def model(nc, ins, out, stop=None):
    with ExitStack() as ctx:
        m = Model(nc, ins, out, ctx)
        m.h0 = nc.dram_tensor("h0", [TOK, D], F32).ap()
        m.xs = nc.dram_tensor("slot_rows", [SLOT0 * P, D], F32).ap()
        m.ys = nc.dram_tensor("slot_out", [SLOT0 * P, D], F32).ap()
        m.v_row = nc.dram_tensor("v_row", [TOK], F32).ap()
        m.f_row = nc.dram_tensor("f_row", [TOK, 2], F32).ap()
        m.kv_rows = nc.dram_tensor("kv_rows", [TPOOL, 2 * A0], F32).ap()
        constants(m, ctx)
        region = m.sb(ctx, "region", [P, 2, TOK])
        xT = region[0:DC]
        m.h = region[:].rearrange("p c n -> p (c n)")[:, 0:NT * D].rearrange("p (t d) -> p t d", d=D)
        stats = m.sb(ctx, "stats", [P, NT, 6])
        with ExitStack() as attn:
            xpT = m.sb(attn, "xpT", [DC, 2, TPOOL])
            ksum = m.sb(attn, "ksum", [P, B, HP])
            with ExitStack() as c:
                h = m.sb(c, "h_in", [P, NT, D])
                posb = m.sb(c, "posb", [P, D])
                embed(m, c, h, posb)
                layernorm_T(m, h, xT, "l0", xpT)
            with ExitStack() as c:
                kcT = m.sb(c, "kcT", [P, HP, NPT * P])
                with ExitStack() as k:
                    kp3 = m.sb(k, "kp3", [P, HP, NPT * P])
                    kp2 = m.sb(k, "kp2", [P, HP, TOK // 4])
                    kp1 = m.sb(k, "kp1", [P, HP, TOK // 2])
                    wk = m.sb(k, "wk", [DC, 2, A0])
                    keys(m, xT, wk, kp1)
                    with ExitStack() as e:
                        mlp(m, "p0", 0, kp1, kp2, TOK // 2 // P, True)
                        clear(m, kp3[:, :, TPOOL:])
                        mlp(m, "p1", 1, kp2, kp3, TOK // 4 // P, True)
                        mlp(m, "p2", 2, kp3, kcT, NPT, False)
                wv = m.sb(c, "wv", [DC, 2, A0])
                pooled_state(m, kcT, xpT, wv, ksum)
            if stop == "kv":
                return dump(m, [(xT, DC, 2 * TOK), (ksum, P, B * HP)])
            aT = m.sb(attn, "aT", [P, HP, TOK])
            with ExitStack() as c:
                wq = m.sb(c, "wq", [DC, 2, A0])
                linear_attention(m, xT, wq, ksum, aT)
            if stop == "att":
                return dump(m, [(aT, P, HP * TOK)])
            for n in range(3):
                mlp(m, f"e{n}", 5 - n, aT, aT, NT, False)
            if stop == "exp":
                return dump(m, [(aT, P, HP * TOK)])
            project(m, "pr0", aT, HP, "attn_wo", "attn_bo", m.h, stats, True)
        if stop == "h1":
            return store_h(m)
        m.recycle()
        mean, rstd, inv = (m.sb(ctx, n, [P, NT]) for n in ("ln_mean", "ln_rstd", "rms_inv"))
        normalised(m, "n1", stats, mean, rstd, inv)
        with ExitStack() as moe:
            slots = m.sb(moe, "slots0", [P, NT, K0], U32)
            weight = m.sb(moe, "weight0", [P, K0, NT])
            comb = m.sb(moe, "comb0", [P, NT, E0])
            expert = m.sb(moe, "expert0", [1, SLOT0], I32)
            with ExitStack() as r:
                G = m.sb(r, "logits0", [P, E0, NT])
                gates(m, "g0", m.h, mean, rstd, inv, G, E0, "gate_w0", "gate_b0")
                route(m, "r0", G, E0, K0, SLOT0, slots, weight, comb, expert)
            w1 = m.sb(moe, "w1_0", [DC + 1, E0, 2, 768])
            w2 = m.sb(moe, "w2_0", [P, E0, I0 // P, D])
            scatter(m, "sc0", m.h, mean, rstd, inv, slots, K0, [(w1[:], "w1_0"), (w2[:], "w2_0")])
            experts(m, "x0", E0, I0 // P, True, SLOT0, w1, w2, expert)
            gather(m, "ga0", m.h, slots, weight, comb, E0, K0, 0, stats)
        if stop == "h2":
            return store_h(m)
        m.recycle()
        with ExitStack() as c:
            xT = m.sb(c, "x1T", [DC, 2, TOK])
            layernorm_T(m, m.h, xT, "l1")
            oT = m.sb(c, "oT", [P, QC, TOK])
            quantised_attention(m, xT, oT)
            project(m, "pr1", oT, QC, "q_wproj", "q_bproj", m.h, stats, False)
        if stop == "h3":
            return store_h(m)
        normalised(m, "n2", stats, mean, rstd)
        with ExitStack() as moe:
            slots = m.sb(moe, "slots1", [P, NT, K1], U32)
            weight = m.sb(moe, "weight1", [P, K1, NT])
            comb = m.sb(moe, "comb1", [P, NT, E1 + 3])
            expert = m.sb(moe, "expert1", [1, SLOT1], I32)
            w1 = m.sb(moe, "w1_1", [DC + 1, E1, 2, 768])
            w2 = m.sb(moe, "w2_1", [P, E1, I1 // P, D])
            green = Spectral(m, moe, 2 * SLOT1)
            with ExitStack() as r:
                G = m.sb(r, "logits1", [P, E1 + 1, NT])
                gates(m, "g1", m.h, mean, rstd, None, G, E1 + 1, "gate_w1", "gate_b1")
                route(m, "r1", G, E1, K1, SLOT1, slots, weight, comb, expert)
                green.start(G, E1)
            scatter(m, "sc1", m.h, mean, rstd, None, slots, K1, [(w1[:], "w1_1"), (w2[:], "w2_1")])
            experts(m, "x1", E1, I1 // P, False, SLOT1, w1, w2, expert,
                    lambda dve, i, part: green.step(dve, 2 * i + part, part))
            green.finish(comb[:, :, E1:])
            gather(m, "ga1", m.h, slots, weight, comb, E1, K1, 3)


def store_h(m):
    with ExitStack() as c:
        done = m.sem(c, "stored_h")
        with m.nc.Block() as block:
            @block.sync
            def _(sp):
                sp.dma_start(m.out.rearrange("(t p) d -> p t d", p=P), m.h[:]).then_inc(done, 16)
                sp.wait_ge(done, 16)


def clear(m, t):
    with ExitStack() as c:
        done = m.sem(c, "cleared")
        with m.nc.Block() as block:
            @block.vector
            def _(dve):
                dve.memset(t, 0.0).then_inc(done, 1)
                dve.wait_ge(done, 1)


def dump(m, what):
    with ExitStack() as c:
        done = m.sem(c, "dumped")
        with m.nc.Block() as block:
            @block.sync
            def _(sp):
                at = 0
                for t, p, n in what:
                    sp.dma_start(m.out[at:at + p, 0:n], t[:].rearrange("p a b -> p (a b)")).then_inc(done, 16)
                    at += p
                sp.wait_ge(done, 16 * len(what))


def arrange(x, txt, **w):
    f = lambda a: np.ascontiguousarray(a, dtype=np.float32)
    rows = lambda a, p=P: f(np.broadcast_to(np.asarray(a), (p,) + np.asarray(a).shape))
    chunk = lambda a, k: f(np.asarray(a).reshape(k, -1, a.shape[-1]).transpose(1, 0, 2))
    o = {}
    patches = np.asarray(x).reshape(B, 4, 16, 4, 16, 3).transpose(2, 4, 5, 0, 1, 3).reshape(768, B * NIMG)
    o["patchesT"] = chunk(patches, 6)
    o["txt"] = f(txt)
    o["tok_w"] = chunk(w["L0_tok_W"], 6)
    o["tok_b"] = rows(w["L0_tok_b"])
    o["pos"] = f(np.tile(np.asarray(w["L0_tok_pos_emb"]), (8, 1)))
    o["ident"] = np.eye(P, dtype=np.float32)
    o["attn_wq"], o["attn_wk"], o["attn_wv"] = (chunk(w["L0_attn_" + k], 2) for k in ("Wq", "Wk", "Wv"))
    mats = np.concatenate([np.asarray(w["L0_attn_pool_W"]), np.asarray(w["L0_attn_exp_W"])])
    pair = np.zeros((P, 6, P), np.float32)
    for k in range(2):
        pair[k * HD:(k + 1) * HD, :, k * HD:(k + 1) * HD] = mats.transpose(1, 0, 2)
    o["mlp_w"] = pair
    both = lambda k: np.concatenate([np.asarray(w["L0_attn_pool_" + k]), np.asarray(w["L0_attn_exp_" + k])])
    o["mlp_b"] = rows(both("b"), 3)
    o["mlp_g"] = f(np.tile(both("g").T, (2, 1)))
    o["mlp_be"] = f(np.tile(both("be").T, (2, 1)))
    of = np.arange(P)[:, None, None] // HD + 2 * np.arange(HP)[None, :, None]
    o["hsel"] = f(of == np.arange(NH)[None, None, :])
    o["hexp"] = f(o["hsel"].transpose(2, 1, 0))
    o["attn_wo"] = chunk(w["L0_attn_Wo"], 6)
    o["attn_bo"] = rows(w["L0_attn_bo"])
    o["norm_scale"] = rows(w["L0_ffn_norm_scale"])
    o["gate_w0"] = chunk(np.asarray(w["L0_ffn_gate_w"]).T, 2)
    o["gate_b0"] = rows(w["L0_ffn_gate_b"])
    up = np.asarray(w["L0_ffn_mlp1_w"]).transpose(2, 0, 1)
    up = np.concatenate([up[:, :, 0::2], up[:, :, 1::2]], axis=2)
    ub = np.asarray(w["L0_ffn_mlp1_b"])
    o["w1_0"] = with_bias(up, np.concatenate([ub[:, 0::2], ub[:, 1::2]], axis=1))
    o["w2_0"] = f(np.asarray(w["L0_ffn_mlp2_w"]).reshape(E0, D, I0 // P, P).transpose(3, 0, 2, 1))
    o["ga0_rows"] = f(w["L0_ffn_mlp2_b"])
    o["ga0_times"] = np.ones((E0, D), np.float32)
    qkv = np.asarray(w["L1_attn_Wqkv"]).reshape(3, QH, QD, D)
    pad = np.zeros((3, QH, 32, D), np.float32)
    pad[:, :, :QD] = qkv
    pad = pad.reshape(3, QH * 32, 2, DC).transpose(3, 2, 0, 1)
    o["q_wqk"] = f(pad[:, :, 0:2])
    o["q_wv"] = f(pad[:, :, 2])
    proj = np.zeros((QH, 32, D), np.float32)
    proj[:, :QD] = np.asarray(w["L1_attn_Wproj"]).T.reshape(QH, QD, D)
    o["q_wproj"] = f(proj.reshape(QC, P, D).transpose(1, 0, 2))
    o["q_bproj"] = rows(w["L1_attn_bproj"])
    o["q_scales"] = f(np.stack([np.broadcast_to(np.asarray(w["L1_attn_s_" + k]), (P,)) for k in ("q", "k", "v", "attn", "after")]
                             + [(np.arange(P) % 32 >= 32 - (N - P)).astype(np.float32)], 1))
    o["gate_w1"] = chunk(np.concatenate([np.asarray(w["L1_ffn_gate_w"]), np.asarray(w["L1_ffn_v_w"])[:, None]], 1), 2)
    o["gate_b1"] = rows(np.concatenate([np.asarray(w["L1_ffn_gate_b"]), np.asarray(w["L1_ffn_v_b"]).reshape(1)]))
    o["w1_1"] = with_bias(np.asarray(w["L1_ffn_w1"]).transpose(1, 0, 2), np.asarray(w["L1_ffn_b1"]))
    o["w2_1"] = f(np.asarray(w["L1_ffn_w2"]).reshape(E1, I1 // P, P, D).transpose(2, 0, 1, 3))
    o["ga1_rows"] = f(np.concatenate([np.asarray(w["L1_ffn_b2"]), np.asarray(w["L1_ffn_out_w"]), np.asarray(w["L1_ffn_out_b"])[None]]))
    o["ga1_times"] = f(np.concatenate([np.ones((E1, D), np.float32), np.tile(np.asarray(w["L1_ffn_bk_scale"]), (3, 1))]))
    for e in (E0, E1):
        o["mask%d" % e] = f(np.broadcast_to(np.arange(NT) > 0, (P, e, NT)))
    o["tri"] = f(np.triu(np.ones((P, P)), 1))
    o["ones"] = np.ones((P, P), np.float32)
    o["steps"] = rows(np.arange(NT, dtype=np.float32) * P)
    o["jrow"] = np.arange(SLOT0, dtype=np.float32)[None]
    alt = np.where(np.arange(N) % 2 == 0, 1.0, -1.0)
    o["sign"] = rows(alt, 2 * B)
    return o


def with_bias(w, b):
    out = np.zeros((DC + 1, w.shape[1], 2, w.shape[2]), np.float32)
    out[:DC] = w.reshape(2, DC, w.shape[1], w.shape[2]).transpose(1, 2, 0, 3)
    out[DC, :, 1] = b
    return out


def kernel(**inputs):
    import concourse.bacc as bacc
    from concourse.bass_utils import run_bass_kernel_spmd

    nc = bacc.Bacc("TRN2", target_bir_lowering=False, num_devices=1)
    arrays = {"in_" + k: v for k, v in arrange(**inputs).items()}
    ins = {k[3:]: nc.dram_tensor(k, a.shape, mybir.dt.from_np(a.dtype), kind="ExternalInput").ap() for k, a in arrays.items()}
    out = nc.dram_tensor("out", [TOK, D], F32, kind="ExternalOutput").ap()
    model(nc, ins, out)
    r = run_bass_kernel_spmd(nc, [arrays], core_ids=[0])
    return r.results[0]["out"].reshape(B, N, D)
```

```python
from contextlib import ExitStack

import numpy as np
import concourse.bass as bass
from concourse import mybir
from concourse.alu_op_type import AluOpType as ALU

F32 = mybir.dt.float32
BF16 = mybir.dt.bfloat16
I32 = mybir.dt.int32
U32 = mybir.dt.uint32
ACT = mybir.ActivationFunctionType
AX = mybir.AxisListType.X

P = 128
B, N, NIMG = 32, 144, 16
D = 192
DC = D // 2
TOK = B * N
NT = TOK // P
LN_EPS = 1e-5
NH, HD = 12, 64
DEN = 64 + NH
HP = NH // 2
A0 = NH * HD
POOL = 8
NPOOL = N // POOL
TPOOL = B * NPOOL
NPT = -(-TPOOL // P)
E0, K0, I0 = 16, 4, 384
E1, K1, I1 = 8, 2, 768
SLOT0 = (TOK * K0 + E0 * (P - 1)) // P
SLOT1 = (TOK * K1 + E1 * (P - 1)) // P
SLOT0 += SLOT0 % 2
SLOT1 += SLOT1 % 2
PITCH = D + 16
QH, QD = 12, 16
QC = QH // 4
CSLOT = 32


def later(i, ring):
    return not isinstance(i, int) or i >= ring


def pipelined(eng, count, unroll, *stages):
    lag = max(s[0] for s in stages)
    first = unroll * (-(-(lag + 2 * unroll) // unroll))
    if count <= first or (count - first) < 2 * unroll:
        first = count
    last = first + (count - first) // unroll * unroll

    def step(i, slot):
        for behind, f in stages:
            if not isinstance(i, int) or 0 <= i - behind < count:
                f(i - behind, (slot - behind) % unroll)

    for i in range(first):
        step(i, i % unroll)
    if last > first:
        with eng.Fori(first // unroll, last // unroll) as j:
            for u in range(unroll):
                step(j * unroll + u, u)
    for i in range(last, count + lag):
        step(i, i % unroll)


class Model:

    def __init__(self, nc, ins, out, ctx):
        self.nc, self.ins, self.out, self.ctx = nc, ins, out, ctx
        self.finished = []
        self.chained, self.chained_so_far = ctx.enter_context(nc.semaphore('chained')), 0
        self.passed = ctx.enter_context(nc.semaphore('passed'))

    def sb(self, ctx, name, shape, dt=F32):
        return ctx.enter_context(self.nc.sbuf_tensor(name, shape, dt))

    def psum(self, ctx, name, shape, dt=F32):
        return ctx.enter_context(self.nc.psum_tensor(name, shape, dt))

    def sem(self, ctx, name):
        handle = self.nc.alloc_semaphore(name=name)
        ctx.callback(self.finished.append, handle)
        return handle

    def recycle(self):
        self.nc.clear_and_free_semaphores(self.finished)
        self.finished = []
        self.nc.all_engine_barrier()

    def sems(self, ctx, prefix, names):
        return [self.sem(ctx, f"{prefix}_{n}") for n in names.split()]


def embed(m, h, posb):
    nc, ins = m.nc, m.ins
    with ExitStack() as c:
        patches = m.sb(c, "patches", [P, 6, 512])
        tok_w = m.sb(c, "tok_w", [P, 6, D])
        tok_b = m.sb(c, "tok_b", [P, D])
        emb = m.sb(c, "emb", [P, 4, D])
        ps = m.psum(c, "emb_ps", [P, 4, 512])
        load_constants, fill_constants, compute_constants = prepare_constants(m, c)
        loaded, posb_ready, emb_mm, emb_done, h_text, h_img = m.sems(
            c, "em", "loaded posb_ready emb_mm emb_done h_text h_img")
        with nc.Block() as block:
            @block.gpsimd
            def _(pool):
                fill_constants(pool)

            @block.sync
            def _(sp):
                load_constants(sp)
                sp.dma_start(tok_w[:], ins["tok_w"]).then_inc(loaded, 16)
                sp.dma_start(patches[:], ins["patchesT"]).then_inc(loaded, 16)
                sp.dma_start(posb[:], ins["pos"]).then_inc(loaded, 16)
                sp.dma_start(tok_b[:], ins["tok_b"]).then_inc(loaded, 16)
                for r in range(8):
                    text = ins["txt"].rearrange("(g r) n d -> r n g d", r=8)[r]
                    first = P - NIMG * (r + 1)
                    if first:
                        sp.dma_start(h[P - first:P, r::9, :], text[0:first]).then_inc(h_text, 16)
                    sp.dma_start(h[0:P - first, r + 1::9, :], text[first:]).then_inc(h_text, 16)
                sp.wait_ge(h_text, 15 * 16)

            @block.scalar
            def _(act):
                act.wait_ge(emb_done, 4)
                for r in range(8):
                    rows = slice(NIMG * r, NIMG * (r + 1))
                    act.dma_start(h[rows, r::9, :], emb[rows]).then_inc(h_img, 16)
                act.wait_ge(h_img, 8 * 16)

            @block.tensor
            def _(pe):
                pe.wait_ge(loaded, 64)
                for g in range(4):
                    for k in range(6):
                        mm = pe.matmul(ps[:, g, 0:D], patches[:, k, g * P:(g + 1) * P], tok_w[:, k, :],
                                       start=(k == 0), stop=(k == 5))
                    mm.then_inc(emb_mm, 1)

            @block.vector
            def _(dve):
                compute_constants(dve)
                dve.wait_ge(loaded, 64)
                dve.tensor_tensor(posb[:], posb[:], tok_b[:], ALU.add).then_inc(posb_ready, 1)
                dve.wait_ge(posb_ready, 1)
                for g in range(4):
                    dve.wait_ge(emb_mm, g + 1)
                    dve.tensor_tensor(emb[:, g, :], ps[:, g, 0:D], posb[:], ALU.add).then_inc(emb_done, 1)


def constants(m, ctx):
    m.ident = m.sb(ctx, "ident", [P, P])
    m.mlp_w = m.sb(ctx, "mlp_w", [P, 6, P])
    m.mlp_g = m.sb(ctx, "mlp_g", [P, 6])
    m.mlp_be = m.sb(ctx, "mlp_be", [P, 6])
    m.mlp_b3 = m.sb(ctx, "mlp_b3", [3, 6, 384], BF16)
    m.ones3 = m.sb(ctx, "ones3", [3, P], BF16)
    m.half = m.sb(ctx, "half", [P, NH])
    m.eps = m.sb(ctx, "eps", [P, 1])


def prepare_constants(m, c):
    ins = m.ins
    mean = m.sb(c, "w_mean", [P, 12])
    braw = m.sb(c, "b_raw", [3, 6, HD])
    bmean = m.sb(c, "b_mean", [3, 6])
    rest = m.sb(c, "b_rest", [3, 6, HD])
    part = m.sb(c, "b_part", [3, 3, 6, HD], BF16)
    psel = m.sb(c, "b_sel", [3, 6, HD], BF16)
    loaded, done, step = m.sems(c, "ct", "loaded done step")

    def load(sp):
        for t, name in ((m.ident, "ident"), (m.mlp_w, "mlp_w"), (m.mlp_g, "mlp_g"),
                        (m.mlp_be, "mlp_be"), (braw, "mlp_b")):
            sp.dma_start(t[:], ins[name]).then_inc(loaded, 16)

    def fill(pool):
        pool.memset(m.half[:], -0.5).then_inc(done, 1)
        pool.memset(m.ones3[:], 1.0).then_inc(done, 1)
        pool.memset(m.eps[:], LN_EPS).then_inc(done, 1)

    def compute(dve):
        count = [0]

        def link(ins_):
            count[0] += 1
            ins_.then_inc(step, 1)
            dve.wait_ge(step, count[0])

        dve.wait_ge(loaded, 80)
        w = m.mlp_w[:].rearrange("p s (h d) -> p (s h) d", h=2)
        link(dve.tensor_reduce(mean[:], w, AX, ALU.add))
        link(dve.tensor_scalar(mean[:], mean[:], 1.0 / HD, None, ALU.mult))
        link(dve.tensor_tensor(w, w, mean[:].unsqueeze(2).to_broadcast([P, 12, HD]), ALU.subtract))
        link(dve.tensor_scalar(m.mlp_g[:], m.mlp_g[:], float(HD) ** 0.5, None, ALU.mult))
        link(dve.tensor_scalar(m.mlp_w[:, 0:3, :], m.mlp_w[:, 0:3, :], 0.5, None, ALU.mult))
        link(dve.tensor_reduce(bmean[:], braw[:], AX, ALU.add))
        link(dve.tensor_scalar(bmean[:], bmean[:], 1.0 / HD, None, ALU.mult))
        link(dve.tensor_tensor(rest[:], braw[:], bmean[:].unsqueeze(2).to_broadcast([3, 6, HD]), ALU.subtract))
        for k in range(3):
            link(dve.tensor_copy(part[:, k], rest[:]))
            link(dve.tensor_tensor(rest[:], rest[:], part[:, k], ALU.subtract))
        link(dve.tensor_scalar(psel[:], part[:, 0], m.ident[0:3, 0:1], None, ALU.mult))
        for k in (1, 2):
            link(dve.scalar_tensor_tensor(out=psel[:], in0=part[:, k], scalar=m.ident[0:3, k:k + 1],
                                          in1=psel[:], op0=ALU.mult, op1=ALU.add))
        for h in range(6):
            dve.tensor_copy(m.mlp_b3[:, :, h * HD:(h + 1) * HD], psel[:]).then_inc(done, 1)
    return load, fill, compute


def layernorm_T(m, h, xT, tag, xpT=None, save=None):
    nc = m.nc
    with ExitStack() as c:
        stats = m.sb(c, tag + "stats", [P, NT, 6])
        mean = m.sb(c, tag + "mean", [P, NT])
        var = m.sb(c, tag + "var", [P, NT])
        tmp = m.sb(c, tag + "tmp", [P, NT])
        rstd = m.sb(c, tag + "rstd", [P, NT])
        xn = m.sb(c, tag + "xn", [P, 4, D])
        tp = m.psum(c, tag + "tp", [P, 4, 512])
        stat, step, var_ok, std_ok, xn_ok, tp_ok, xT_ok, xp_ok, saved = m.sems(
            c, tag, "stat step var_ok std_ok xn_ok tp_ok xT_ok xp_ok saved")
        with nc.Block() as block:
            if save is not None:
                @block.sync
                def _(sp):
                    sp.dma_start(save, h[:]).then_inc(saved, 16)
                    sp.wait_ge(saved, 16)

            @block.vector
            def _(dve):
                pipelined(dve, NT, 2, (0, lambda i, s: dve.bn_stats(stats[:, i, :], h[:, i, :]).then_inc(stat, 1)))
                dve.wait_ge(stat, NT)
                moments(m, dve, stats, mean, var, tmp, step)
                dve.wait_ge(std_ok, 1)
                dve.reciprocal(rstd[:], tmp[:]).then_inc(step, 1)
                dve.wait_ge(step, MOMENTS + 1)

                def norm(i, s):
                    if later(i, 4):
                        dve.wait_ge(tp_ok, i - 3)
                    dve.tensor_scalar(xn[:, s, :], h[:, i, :], mean[:, bass.ds(i, 1)], rstd[:, bass.ds(i, 1)],
                                      ALU.subtract, ALU.mult).then_inc(xn_ok, 1)

                def pool(i, s):
                    dve.wait_ge(xT_ok, i + 1)
                    dve.sem_inc(m.passed, 1)
                    dve.tensor_reduce(xpT[:, :, bass.ds(i * (P // POOL), P // POOL)],
                                      xT[:, :, bass.ds(i * P, P)].rearrange("p c (n k) -> p c n k", k=POOL),
                                      AX, ALU.add).then_inc(xp_ok, 1)
                pipelined(dve, NT, 4, (0, norm), *([(3, pool)] if xpT is not None else []))

            @block.tensor
            def _(pe):
                def turn(i, s):
                    pe.wait_ge(xn_ok, i + 1)
                    if later(i, 4):
                        pe.wait_ge(xT_ok, i - 3)
                    for k in range(2):
                        mm = pe.transpose(tp[0:DC, s, k * P:(k + 1) * P], xn[:, s, k * DC:(k + 1) * DC], m.ident[:])
                    mm.then_inc(tp_ok, 1)
                pipelined(pe, NT, 4, (0, turn))

            @block.scalar
            def _(act):
                act.wait_ge(step, MOMENTS)
                act.activation(tmp[:], var[:], ACT.Sqrt, bias=m.eps[:, 0:1]).then_inc(std_ok, 1)

                def copy(i, s):
                    act.wait_ge(tp_ok, i + 1)
                    act.sem_inc(m.passed, 1)
                    act.activation(xT[:, :, bass.ds(i * P, P)],
                                   tp[0:DC, s, 0:2 * P].rearrange("p (c n) -> p c n", c=2), ACT.Copy).then_inc(xT_ok, 1)
                pipelined(act, NT, 4, (0, copy))


MOMENTS = 6


def moments(m, dve, stats, mean, var, tmp, step):
    even, odd, sq_e, sq_o = (stats[:, :, k] for k in (1, 4, 2, 5))
    n = [0]

    def link(i):
        n[0] += 1
        i.then_inc(step, 1)
        dve.wait_ge(step, n[0])
    link(dve.tensor_tensor(mean[:], even, odd, ALU.add))
    link(dve.tensor_tensor(tmp[:], even, odd, ALU.subtract))
    link(dve.tensor_scalar(mean[:], mean[:], 0.5, None, ALU.mult))
    link(dve.scalar_tensor_tensor(out=tmp[:], in0=tmp[:], scalar=D / 4.0, in1=tmp[:], op0=ALU.mult, op1=ALU.mult))
    link(dve.tensor_tensor(var[:], sq_e, sq_o, ALU.add))
    dve.tensor_tensor(var[:], var[:], tmp[:], ALU.add).then_inc(m.chained, 1)
    m.chained_so_far += 1
    dve.wait_ge(m.chained, m.chained_so_far)
    link(dve.tensor_scalar(var[:], var[:], 1.0 / D, None, ALU.mult))


def keys(m, xT, wk, kpT):
    with ExitStack() as c:
        ex = m.sb(c, "k_exp", [P, 2, HP, N])
        kf = m.sb(c, "k_feat", [P, 2, HP, N])
        ps = m.psum(c, "k_ps", [P, 2, 2, 512])
        loaded, mm_ok, exp_ok, min_ok, k_ok, kp_ok = m.sems(c, "ky", "loaded mm_ok exp_ok min_ok k_ok kp_ok")
        proj = lambda s: ps[:, s, :, 0:3 * N]
        with m.nc.Block() as block:
            @block.sync
            def _(sp):
                sp.dma_start(wk[:], m.ins["attn_wk"]).then_inc(loaded, 16)
                sp.dma_start(m.unused[:], m.ins["unused"]).then_inc(m.empty_in, 16)
                sp.wait_ge(m.zeroed, 2)
                for n, xs in enumerate(m.xs):
                    for c8 in range((SLOT0, SLOT1)[n] // 8):
                        rows = xs.rearrange("(c n p) d -> c p n d", p=P, n=8)[c8]
                        sp.dma_start(rows[:, :, 0:D + 1],
                                     m.empty[:, n].unsqueeze(1).to_broadcast([P, 8, D + 1])).then_inc(m.xs_zero, 16)

            @block.gpsimd
            def _(pool):
                pool.memset(m.empty[:], 0.0).then_inc(m.zeroed, 1)
                pool.wait_ge(m.zeroed, 1)
                pool.wait_ge(m.empty_in, 16)
                pool.tensor_copy(m.empty[:, :, D].bitcast(U32), m.unused[:]).then_inc(m.zeroed, 1)

            @block.tensor
            def _(pe):
                pe.wait_ge(loaded, 16)

                def project(b, s):
                    if later(b, 2):
                        pe.wait_ge(k_ok, b - 1)
                    pe_project(pe, ps, s, wk, xT, b).then_inc(mm_ok, 1)
                pipelined(pe, B, 2, (0, project))

            @block.scalar
            def _(act):
                def exp(b, s):
                    act.wait_ge(mm_ok, b + 1)
                    if later(b, 2):
                        act.wait_ge(k_ok, b - 1)
                    act.activation(ex[:, s].rearrange("p (g h) n -> p g (h n)", g=2), proj(s), ACT.Exp).then_inc(exp_ok, 1)
                pipelined(act, B, 2, (0, exp))

            @block.vector
            def _(dve):
                def elu(b, s):
                    dve.wait_ge(exp_ok, b + 1)
                    dve.tensor_scalar(ex[:, s], ex[:, s], 1.0, None, ALU.min).then_inc(min_ok, 1)
                    dve.wait_ge(min_ok, b + 1)
                    dve.scalar_tensor_tensor(out=kf[:, s].rearrange("p (g h) n -> p g (h n)", g=2), in0=proj(s), scalar=0.0,
                                             in1=ex[:, s].rearrange("p (g h) n -> p g (h n)", g=2),
                                             op0=ALU.max, op1=ALU.add).then_inc(k_ok, 1)
                    dve.wait_ge(k_ok, b + 1)
                    two = kf[:, s].rearrange("p h (n k) -> p h n k", k=2)
                    dve.tensor_tensor(kpT[:, :, bass.ds(b * (N // 2), N // 2)], two[:, :, :, 0], two[:, :, :, 1],
                                      ALU.add).then_inc(kp_ok, 1)
                pipelined(dve, B, 2, (0, elu))
                dve.wait_ge(kp_ok, B)


def pe_project(pe, ps, s, w, xT, b):
    for h in range(HP):
        for k in range(2):
            mm = pe.matmul(ps[:, s, h // 3, (h % 3) * N:(h % 3 + 1) * N], w[:, k, h * P:(h + 1) * P],
                           xT[:, k, bass.ds(b * N, N)], start=(k == 0), stop=(k == 1))
    return mm


def mlp(m, tag, stage, src, dst, tiles, pairs, load=None):
    with ExitStack() as c:
        x = m.sb(c, tag + "x", [P, 3, HP, P])
        sq = m.sb(c, tag + "sq", [P, 3, NH, HD + 1])
        ss = m.sb(c, tag + "ss", [P, 3, NH])
        rstd = m.sb(c, tag + "rstd", [P, 3, NH])
        z = m.sb(c, tag + "z", [P, 3, HP, P])
        g = m.sb(c, tag + "g", [P, 3, HP, P]) if pairs else None
        y = m.psum(c, tag + "y", [P, 3, 2, 512])
        tp = m.psum(c, tag + "tp", [P, 2, 512])
        x0_ok, x1_ok, mm_ok, sq_ok, ss_ok, eps_ok, rstd_ok, z_ok, tp0_ok, tp1_ok, g0_ok, g1_ok, pair_ok = m.sems(
            c, tag, "x0_ok x1_ok mm_ok sq_ok ss_ok eps_ok rstd_ok z_ok tp0_ok tp1_ok g0_ok g1_ok pair_ok")
        tp_ok, g_ok = (tp0_ok, tp1_ok), (g0_ok, g1_ok)
        with m.nc.Block() as block:
            if load is not None:
                @block.sync
                def _(sp):
                    load(sp)

            @block.vector
            def _(dve):
                def stage_in(i, s):
                    if later(i, 3):
                        dve.wait_ge(mm_ok, 2 * i - 5)
                        dve.sem_inc(m.passed, 1)
                    dve.tensor_copy(x[:, s, 0:3], src[:, 0:3, bass.ds(i * P, P)]).then_inc(x0_ok, 1)

                def squares(i, s):
                    for a in range(2):
                        dve.wait_ge(sq_ok, 2 * i + a + 1)
                        dve.tensor_reduce(ss[:, s, 6 * a:6 * a + 6], sq[:, s, 6 * a:6 * a + 6], AX, ALU.add).then_inc(ss_ok, 1)

                def scale(i, s):
                    dve.wait_ge(rstd_ok, i + 1)
                    if later(i, 3):
                        dve.wait_ge(tp_ok[1], i - 2)
                    for a in range(2):
                        dve.tensor_tensor(z[:, s, 3 * a:3 * a + 3].rearrange("p b (e d) -> p (b e) d", d=HD),
                                          y[:, s, a, 0:384].rearrange("p (h d) -> p h d", d=HD),
                                          rstd[:, s, 6 * a:6 * a + 6].unsqueeze(2).to_broadcast([P, 6, HD]),
                                          ALU.mult).then_inc(z_ok, 1)

                def add_pairs(i, s):
                    dve.wait_ge(g_ok[1], i + 1)
                    two = g[:, s].rearrange("p h (n k) -> p h n k", k=2)
                    dve.tensor_tensor(dst[:, :, bass.ds(i * (P // 2), P // 2)], two[:, :, :, 0], two[:, :, :, 1],
                                      ALU.add).then_inc(pair_ok, 1)
                pipelined(dve, tiles, 3, (0, stage_in), (1, squares), (2, scale), *([(3, add_pairs)] if pairs else []))
                if pairs:
                    dve.wait_ge(pair_ok, tiles)

            @block.tensor
            def _(pe):
                def dense(i, s):
                    for a in range(2):
                        pe.wait_ge((x0_ok, x1_ok)[a], i + 1)
                        if later(i, 3):
                            pe.wait_ge(z_ok, 2 * i + a - 5)
                        pe.matmul(y[:, s, a, 0:384], m.ones3[:], m.mlp_b3[:, stage, :], start=True, stop=False)
                        for h in range(3):
                            mm = pe.matmul(y[:, s, a, h * P:(h + 1) * P], x[:, s, 3 * a + h, :], m.mlp_w[:, stage, :],
                                           start=False, stop=(h == 2))
                        mm.then_inc(mm_ok, 1)

                def turn(i, s):
                    for a in range(2):
                        pe.wait_ge(z_ok, 2 * i + a + 1)
                        if later(i, 1):
                            pe.wait_ge(g_ok[a], i)
                        for h in range(3):
                            mm = pe.transpose(tp[:, a, h * P:(h + 1) * P], z[:, s, 3 * a + h, :], m.ident[:])
                        mm.then_inc(tp_ok[a], 1)
                pipelined(pe, tiles, 3, (0, dense), (2, turn))

            @block.scalar
            def _(act):
                def stage_in(i, s):
                    if later(i, 3):
                        act.wait_ge(mm_ok, 2 * i - 4)
                        act.sem_inc(m.passed, 1)
                    act.activation(x[:, s, 3:6], src[:, 3:6, bass.ds(i * P, P)], ACT.Copy).then_inc(x1_ok, 1)

                def square(i, s):
                    if later(i, 3):
                        act.wait_ge(ss_ok, 2 * i - 4)
                    for a in range(2):
                        act.wait_ge(mm_ok, 2 * i + a + 1)
                        act.activation(sq[:, s, 6 * a:6 * a + 6, 0:HD], y[:, s, a, 0:384].rearrange("p (h d) -> p h d", d=HD),
                                       ACT.Square).then_inc(sq_ok, 1)

                def gelu(i, s):
                    for a in range(2):
                        act.wait_ge(tp_ok[a], i + 1)
                        if pairs and later(i, 3):
                            act.wait_ge(pair_ok, i - 2)
                        act.sem_inc(m.passed, 1)
                        to = g[:, s, 3 * a:3 * a + 3, :] if pairs else dst[:, 3 * a:3 * a + 3, bass.ds(i * P, P)]
                        act.activation(to, tp[:, a, 0:384].rearrange("p (h n) -> p h n", n=P), ACT.Gelu,
                                       bias=m.mlp_be[:, stage:stage + 1],
                                       scale=m.mlp_g[:, stage:stage + 1]).then_inc(g_ok[a], 1)
                act.wait_ge(eps_ok, 1)
                pipelined(act, tiles, 3, (0, stage_in), (1, square), (3, gelu))
                act.wait_ge(g_ok[1], tiles)

            @block.gpsimd
            def _(pool):
                pool.memset(sq[:, :, :, HD:], HD * LN_EPS).then_inc(eps_ok, 1)

                def rsqrt(i, s):
                    pool.wait_ge(ss_ok, 2 * i + 2)
                    if later(i, 3):
                        pool.wait_ge(z_ok, 2 * i - 4)
                    pool.tensor_tensor(rstd[:, s], ss[:, s], m.half[:], ALU.pow).then_inc(rstd_ok, 1)
                pipelined(pool, tiles, 3, (0, rsqrt))


def pooled_state(m, kcT, xpT, wv, ksum):
    with ExitStack() as c:
        kt = m.sb(c, "kt", [P, NPT, HP, P])
        vt = m.sb(c, "vt", [P, NPT, A0])
        kps = m.psum(c, "kps", [P, 2, 2, 512])
        vps = m.psum(c, "vps", [P, 2, 2, 512])
        loaded, scaled, sums, k_mm, v_mm, k_ok, v_ok, stored = m.sems(
            c, "pl", "loaded scaled sums k_mm v_mm k_ok v_ok stored")
        rows = [min(P, TPOOL - P * i) for i in range(NPT)]
        with m.nc.Block() as block:
            @block.vector
            def _(dve):
                dve.tensor_scalar(kcT[:, :, 0:TPOOL], kcT[:, :, 0:TPOOL], float(NPOOL) ** -0.5, None,
                                  ALU.mult).then_inc(scaled, 1)
                dve.tensor_scalar(xpT[:], xpT[:], 1.0 / POOL, None, ALU.mult).then_inc(scaled, 1)
                dve.wait_ge(scaled, 2)
                for h in range(HP):
                    dve.tensor_reduce(ksum[:, :, h], kcT[:, h, 0:TPOOL].rearrange("p (b n) -> p b n", n=NPOOL),
                                      AX, ALU.add).then_inc(sums, 1)
                for i in range(NPT):
                    dve.wait_ge(v_mm, i + 1)
                    dve.tensor_copy(vt[0:rows[i], i, :].rearrange("p (a n) -> p a n", a=2),
                                    vps[0:rows[i], i % 2, :, 0:384]).then_inc(v_ok, 1)
                dve.wait_ge(sums, HP)

            @block.tensor
            def _(pe):
                pe.wait_ge(loaded, 16)
                pe.wait_ge(scaled, 2)
                for i, r in enumerate(rows):
                    if i >= 2:
                        pe.wait_ge(k_ok, i - 1)
                        pe.wait_ge(v_ok, i - 1)
                    for h in range(HP):
                        mm = pe.transpose(kps[0:r, i % 2, h // 3, (h % 3) * P:(h % 3 + 1) * P],
                                          kcT[:, h, i * P:i * P + r], m.ident[:])
                    mm.then_inc(k_mm, 1)
                    for a in range(2):
                        for k in range(2):
                            mm = pe.matmul(vps[0:r, i % 2, a, 0:384], xpT[:, k, i * P:i * P + r],
                                           wv[:, k, a * 384:(a + 1) * 384], start=(k == 0), stop=(k == 1))
                    mm.then_inc(v_mm, 1)

            @block.scalar
            def _(act):
                for i, r in enumerate(rows):
                    act.wait_ge(k_mm, i + 1)
                    act.activation(kt[0:r, i].rearrange("p (a h) n -> p a (h n)", a=2), kps[0:r, i % 2, :, 0:384],
                                   ACT.Copy).then_inc(k_ok, 1)

            @block.sync
            def _(sp):
                sp.dma_start(wv[:], m.ins["attn_wv"]).then_inc(loaded, 16)
                for i, r in enumerate(rows):
                    sp.wait_ge(k_ok, i + 1)
                    sp.dma_start(m.kv_rows[i * P:i * P + r, 0:A0], kt[0:r, i].rearrange("p h n -> p (h n)")).then_inc(stored, 16)
                    sp.wait_ge(v_ok, i + 1)
                    sp.dma_start(m.kv_rows[i * P:i * P + r, A0:], vt[0:r, i, :]).then_inc(stored, 16)
                sp.wait_ge(stored, 32 * NPT)


def linear_attention(m, xT, wq, ksum, aT):
    with ExitStack() as c:
        ex = m.sb(c, "q_exp", [P, HP, N])
        q = m.sb(c, "q", [P, 2, HP, N])
        kv_in = m.sb(c, "kv_in", [NPOOL, 2, 2 * A0])
        kv = m.sb(c, "kv", [P, 2, HP, P])
        hsel = m.sb(c, "hsel", [P, HP, DEN])
        hexp = m.sb(c, "hexp", [DEN, HP, P], BF16)
        ksel = m.sb(c, "ksel", [P, 2, HP, DEN])
        rden = m.sb(c, "rden", [DEN, N])
        rest = m.sb(c, "rden_rest", [DEN, N])
        part = m.sb(c, "rden_part", [DEN, 2, N], BF16)
        rb = m.sb(c, "rb", [P, 2, HP, N])
        qps = m.psum(c, "q_ps", [P, 1, 2, 512])
        kvps = m.psum(c, "kv_ps", [P, 2, 512])
        nps = m.psum(c, "num_ps", [P, 2, 512])
        rps = m.psum(c, "rb_ps", [P, 2, 512])
        (loaded, kv_zero, q_mm, exp_ok, min_ok, q_ok, kv_mm, kv_top, kv_low, ksel_ok, den_mm, den_ok, rden_ok,
         num_mm, rb_mm, rb_ok, out_ok, hexp_ok, split_ok) = m.sems(
            c, "la", "loaded kv_zero q_mm exp_ok min_ok q_ok kv_mm kv_top kv_low ksel_ok den_mm den_ok rden_ok "
            "num_mm rb_mm rb_ok out_ok hexp_ok split_ok")
        arrived = m.sems(c, "la_kv", "in0 in1")
        split = lambda t: t.rearrange("p (g h) n -> p g (h n)", g=2)
        with m.nc.Block() as block:
            @block.sync
            def _(sp):
                sp.dma_start(wq[:], m.ins["attn_wq"]).then_inc(loaded, 16)
                sp.dma_start(hsel[:], m.ins["hsel"]).then_inc(loaded, 16)
                sp.dma_start(ex[0:DEN].rearrange("p h n -> p (h n)")[:, 0:HP * P], m.ins["hexp"]).then_inc(loaded, 16)

                def load(b, s):
                    if later(b, 2):
                        sp.wait_ge(kv_mm, b - 1)
                    sp.dma_start(kv_in[:, s, :], m.kv_rows[bass.ds(b * NPOOL, NPOOL), :]).then_inc(arrived[s], 16)
                pipelined(sp, B, 2, (0, load))

            @block.gpsimd
            def _(pool):
                pool.memset(kv[:], 0.0).then_inc(kv_zero, 1)
                pool.wait_ge(loaded, 48)

                def select(b, s):
                    if later(b, 2):
                        pool.wait_ge(den_mm, b - 1)
                    pool.sem_inc(m.passed, 1)
                    pool.tensor_tensor(ksel[:, s], hsel[:], ksum[:, b, :].unsqueeze(2).to_broadcast([P, HP, DEN]),
                                       ALU.mult).then_inc(ksel_ok, 1)
                pipelined(pool, B, 2, (0, select))

            @block.tensor
            def _(pe):
                pe.wait_ge(loaded, 48)

                def first(b, s):
                    if later(b, 1):
                        pe.wait_ge(q_ok, b)
                    pe_project(pe, qps, 0, wq, xT, b).then_inc(q_mm, 1)

                def state(b, s):
                    pe.wait_ge(arrived[s], landed(b, s))
                    if later(b, 1):
                        pe.wait_ge(den_ok, b)
                    for h in range(HP):
                        mm = pe.matmul(kvps[:, h // 3, (h % 3) * P:(h % 3 + 1) * P], kv_in[:, s, h * P:(h + 1) * P],
                                       kv_in[:, s, A0 + h * P:A0 + (h + 1) * P], start=True, stop=True)
                    mm.then_inc(kv_mm, 1)

                def denominators(b, s):
                    pe.wait_ge(q_ok, b + 1)
                    pe.wait_ge(ksel_ok, b + 1)
                    pe.wait_ge(kv_top, b + 1)
                    pe.wait_ge(kv_low, b + 1)
                    for bank, t in ((0, slice(0, P)), (1, slice(P, N))):
                        for h in range(HP):
                            mm = pe.matmul(kvps[0:DEN, bank, 384:384 + t.stop - t.start], ksel[:, s, h, :], q[:, s, h, t],
                                           start=(h == 0), stop=(h == HP - 1))
                    mm.then_inc(den_mm, 1)

                def numerators(b, s):
                    if later(b, 1):
                        pe.wait_ge(out_ok, b)
                    for h in range(HP):
                        mm = pe.matmul(nps[:, h // 3, (h % 3) * N:(h % 3 + 1) * N], kv[:, s, h, :], q[:, s, h, :],
                                       start=True, stop=True)
                    mm.then_inc(num_mm, 1)

                def spread(b, s):
                    pe.wait_ge(rden_ok, b + 1)
                    if later(b, 1):
                        pe.wait_ge(rb_ok, b)
                    for h in range(HP):
                        mm = pe.matmul(rps[:, h // 3, (h % 3) * N:(h % 3 + 1) * N], hexp[:, h, :], part[:, s, :],
                                       start=True, stop=True)
                    mm.then_inc(rb_mm, 1)
                pipelined(pe, B, 2, (0, first), (0, state), (1, numerators), (1, spread), (0, denominators))

            @block.scalar
            def _(act):
                act.wait_ge(kv_zero, 1)
                act.wait_ge(hexp_ok, 1)

                def exp(b, s):
                    act.wait_ge(q_mm, b + 1)
                    if later(b, 1):
                        act.wait_ge(q_ok, b)
                    act.activation(split(ex), qps[:, 0, :, 0:3 * N], ACT.Exp).then_inc(exp_ok, 1)

                def diagonal(b, s):
                    act.wait_ge(kv_mm, b + 1)
                    if later(b, 2):
                        act.wait_ge(num_mm, b - 1)
                    for half, done in ((0, kv_top), (HD, kv_low)):
                        act.activation(kv[half:half + HD, s, :, half:half + HD].rearrange("p (a b) e -> p a b e", a=2),
                                       kvps[half:half + HD, :, 0:384].rearrange("p a (b n) -> p a b n", n=P)[:, :, :, half:half + HD],
                                       ACT.Copy).then_inc(done, 1)

                def widen(b, s):
                    act.wait_ge(rb_mm, b + 1)
                    if later(b, 2):
                        act.wait_ge(out_ok, b - 1)
                    act.activation(split(rb[:, s]), rps[:, :, 0:3 * N], ACT.Copy).then_inc(rb_ok, 1)
                pipelined(act, B, 2, (0, exp), (0, diagonal), (1, widen))

            @block.vector
            def _(dve):
                dve.wait_ge(loaded, 48)
                dve.tensor_copy(hexp[:].rearrange("p h n -> p (h n)"),
                                ex[0:DEN].rearrange("p h n -> p (h n)")[:, 0:HP * P]).then_inc(hexp_ok, 1)

                def elu(b, s):
                    dve.wait_ge(exp_ok, b + 1)
                    dve.tensor_scalar(ex[:], ex[:], 1.0, None, ALU.min).then_inc(min_ok, 1)
                    dve.wait_ge(min_ok, b + 1)
                    if later(b, 2):
                        dve.wait_ge(num_mm, b - 1)
                    dve.scalar_tensor_tensor(out=split(q[:, s]), in0=qps[:, 0, :, 0:3 * N], scalar=0.0,
                                             in1=split(ex), op0=ALU.max, op1=ALU.add).then_inc(q_ok, 1)

                def divide(b, s):
                    dve.wait_ge(den_mm, b + 1)
                    dve.tensor_scalar(rden[:, 0:P], kvps[0:DEN, 0, 384:384 + P], 1e-6, None, ALU.add)
                    dve.tensor_scalar(rden[:, P:N], kvps[0:DEN, 1, 384:384 + N - P], 1e-6, None, ALU.add).then_inc(den_ok, 1)
                    dve.wait_ge(den_ok, b + 1)
                    if later(b, 2):
                        dve.wait_ge(rb_mm, b - 1)
                    dve.reciprocal(rden[:], rden[:]).then_inc(split_ok, 1)
                    last = slice(64, DEN)
                    dve.wait_ge(split_ok, 6 * b + 1)
                    dve.tensor_copy(part[:, s, :], rden[:]).then_inc(split_ok, 1)
                    dve.wait_ge(split_ok, 6 * b + 2)
                    dve.tensor_tensor(rest[:], rden[:], part[:, s, :], ALU.subtract).then_inc(split_ok, 1)
                    dve.wait_ge(split_ok, 6 * b + 3)
                    dve.tensor_copy(part[32:64, s, :], rest[32:64]).then_inc(split_ok, 1)
                    dve.tensor_copy(part[last, s, :], rest[last]).then_inc(split_ok, 1)
                    dve.wait_ge(split_ok, 6 * b + 5)
                    dve.tensor_tensor(rest[last], rest[last], part[last, s, :], ALU.subtract).then_inc(split_ok, 1)
                    dve.wait_ge(split_ok, 6 * b + 6)
                    dve.tensor_copy(part[last, s, :], rest[last]).then_inc(rden_ok, 1)

                def result(b, s):
                    dve.wait_ge(rb_ok, b + 1)
                    dve.wait_ge(num_mm, b + 1)
                    dve.tensor_tensor(aT[:, :, bass.ds(b * N, N)].rearrange("p (g h) n -> p g h n", g=2),
                                      nps[:, :, 0:3 * N].rearrange("p g (h n) -> p g h n", n=N),
                                      rb[:, s].rearrange("p (g h) n -> p g h n", g=2), ALU.mult).then_inc(out_ok, 1)
                pipelined(dve, B, 2, (0, elu), (1, result), (0, divide))
                dve.wait_ge(out_ok, B)


def landed(i, s, ring=2):
    return (i - s) * 16 // ring + 16



def project(m, tag, srcT, chunks, w_name, b_name, h, stats, from_h0):
    with ExitStack() as c:
        x = m.sb(c, tag + "x", [P, 2, chunks, P])
        w = m.sb(c, tag + "w", [P, chunks, D])
        bias = m.sb(c, tag + "b", [P, D])
        ps = m.psum(c, tag + "ps", [P, 2, 512])
        loaded, x_ok, hb_ok, mm_ok, h_ok, stat = m.sems(c, tag, "loaded x_ok hb_ok mm_ok h_ok stat")
        with m.nc.Block() as block:
            @block.sync
            def _(sp):
                sp.dma_start(w[:], m.ins[w_name]).then_inc(loaded, 16)
                sp.dma_start(bias[:], m.ins[b_name]).then_inc(loaded, 16)

            @block.gpsimd
            def _(pool):
                pool.wait_ge(loaded, 32)
                if from_h0:
                    pool.wait_ge(m.h_in, 16)
                pipelined(pool, NT, 2, (0, lambda i, s: pool.tensor_tensor(
                    h[:, i, :], h[:, i, :], bias[:], ALU.add).then_inc(hb_ok, 1)))

            @block.scalar
            def _(act):
                def stage_in(i, s):
                    if later(i, 2):
                        act.wait_ge(mm_ok, i - 1)
                        act.sem_inc(m.passed, 1)
                    act.activation(x[:, s], srcT[:, :, bass.ds(i * P, P)], ACT.Copy).then_inc(x_ok, 1)
                pipelined(act, NT, 2, (0, stage_in))

            @block.tensor
            def _(pe):
                pe.wait_ge(loaded, 32)

                def dense(i, s):
                    pe.wait_ge(x_ok, i + 1)
                    if later(i, 2):
                        pe.wait_ge(h_ok, i - 1)
                    for k in range(chunks):
                        mm = pe.matmul(ps[:, s, 0:D], x[:, s, k, :], w[:, k, :], start=(k == 0), stop=(k == chunks - 1))
                    mm.then_inc(mm_ok, 1)
                pipelined(pe, NT, 2, (0, dense))

            @block.vector
            def _(dve):
                def add(i, s):
                    dve.wait_ge(mm_ok, i + 1)
                    dve.wait_ge(hb_ok, i + 1)
                    dve.tensor_tensor(h[:, i, :], ps[:, s, 0:D], h[:, i, :], ALU.add).then_inc(h_ok, 1)

                def stat_of(i, s):
                    dve.wait_ge(h_ok, i + 1)
                    dve.bn_stats(stats[:, i, :], h[:, i, :]).then_inc(stat, 1)
                pipelined(dve, NT, 2, (0, add), (1, stat_of))
                dve.wait_ge(stat, NT)


def normalised(m, tag, stats, mean, rstd, inv=None):
    with ExitStack() as c:
        var = m.sb(c, tag + "var", [P, NT])
        tmp = m.sb(c, tag + "tmp", [P, NT])
        step, std_ok = m.sems(c, tag, "step std_ok")
        with m.nc.Block() as block:
            @block.vector
            def _(dve):
                moments(m, dve, stats, mean, var, tmp, step)
                dve.wait_ge(std_ok, 1)
                dve.reciprocal(rstd[:], tmp[:]).then_inc(step, 1)
                dve.wait_ge(step, MOMENTS + 1)
                if inv is not None:
                    dve.tensor_tensor(var[:], var[:], rstd[:], ALU.mult).then_inc(step, 1)
                    dve.wait_ge(step, MOMENTS + 2)
                    dve.tensor_tensor(var[:], var[:], rstd[:], ALU.mult).then_inc(step, 1)
                    dve.wait_ge(std_ok, 2)
                    dve.reciprocal(inv[:], tmp[:]).then_inc(step, 1)
                    dve.wait_ge(step, MOMENTS + 4)

            @block.scalar
            def _(act):
                act.wait_ge(step, MOMENTS)
                act.activation(tmp[:], var[:], ACT.Sqrt, bias=m.eps[:, 0:1]).then_inc(std_ok, 1)
                if inv is not None:
                    act.wait_ge(step, MOMENTS + 3)
                    act.activation(tmp[:], var[:], ACT.Sqrt, bias=m.eps[:, 0:1]).then_inc(std_ok, 1)


def gates(m, tag, h, mean, rstd, inv, G, cols, w_name, b_name):
    with ExitStack() as c:
        x = m.sb(c, tag + "x", [P, 4, D])
        tr = m.sb(c, tag + "tr", [P, 4, D])
        tT = m.sb(c, tag + "tT", [DC, 4, 2, P])
        scale = m.sb(c, tag + "scale", [P, D])
        w = m.sb(c, tag + "w", [DC, 2, cols])
        bias = m.sb(c, tag + "b", [P, cols])
        tp = m.psum(c, tag + "tp", [P, 4, 512])
        gp = m.psum(c, tag + "gp", [P, 4, 512])
        loaded, x_ok, t_ok, tp_ok, tT_ok, mm_ok, g_ok = m.sems(c, tag, "loaded x_ok t_ok tp_ok tT_ok mm_ok g_ok")
        with m.nc.Block() as block:
            @block.sync
            def _(sp):
                sp.dma_start(w[:], m.ins[w_name]).then_inc(loaded, 16)
                sp.dma_start(bias[:], m.ins[b_name]).then_inc(loaded, 16)
                sp.dma_start(scale[:], m.ins["norm_scale"]).then_inc(loaded, 16)

            @block.vector
            def _(dve):
                dve.wait_ge(loaded, 48)

                def norm(i, s):
                    if later(i, 4):
                        dve.wait_ge(tp_ok, i - 3)
                    to, done = (tr, t_ok) if inv is None else (x, x_ok)
                    dve.tensor_scalar(to[:, s, :], h[:, i, :], mean[:, bass.ds(i, 1)], rstd[:, bass.ds(i, 1)],
                                      ALU.subtract, ALU.mult).then_inc(done, 1)

                def rms(i, s):
                    dve.wait_ge(x_ok, i + 1)
                    dve.scalar_tensor_tensor(out=tr[:, s, :], in0=x[:, s, :], scalar=inv[:, bass.ds(i, 1)],
                                             in1=scale[:], op0=ALU.mult, op1=ALU.mult).then_inc(t_ok, 1)

                def logits(i, s):
                    dve.wait_ge(mm_ok, i + 1)
                    dve.tensor_tensor(G[:, :, i], gp[:, s, 0:cols], bias[:], ALU.add).then_inc(g_ok, 1)
                pipelined(dve, NT, 4, (0, norm), *([(1, rms)] if inv is not None else []), (3, logits))
                dve.wait_ge(g_ok, NT)

            @block.tensor
            def _(pe):
                pe.wait_ge(loaded, 48)

                def turn(i, s):
                    pe.wait_ge(t_ok, i + 1)
                    if later(i, 4):
                        pe.wait_ge(tT_ok, i - 3)
                    for k in range(2):
                        mm = pe.transpose(tp[0:DC, s, k * P:(k + 1) * P], tr[:, s, k * DC:(k + 1) * DC], m.ident[:])
                    mm.then_inc(tp_ok, 1)

                def dense(i, s):
                    pe.wait_ge(tT_ok, i + 1)
                    if later(i, 4):
                        pe.wait_ge(g_ok, i - 3)
                    for k in range(2):
                        mm = pe.matmul(gp[:, s, 0:cols], tT[:, s, k, :], w[:, k, :], start=(k == 0), stop=(k == 1))
                    mm.then_inc(mm_ok, 1)
                pipelined(pe, NT, 4, (0, turn), (1, dense))

            @block.scalar
            def _(act):
                def copy(i, s):
                    act.wait_ge(tp_ok, i + 1)
                    if later(i, 4):
                        act.wait_ge(mm_ok, i - 3)
                    act.activation(tT[:, s], tp[0:DC, s, 0:2 * P].rearrange("p (c n) -> p c n", c=2), ACT.Copy).then_inc(tT_ok, 1)
                pipelined(act, NT, 4, (0, copy))


def route(m, tag, G, E, K, tiles, slots, weight, comb, expert):
    with ExitStack() as c:
        sb = lambda name, shape, dt=F32: m.sb(c, tag + name, shape, dt)
        rank, cmp_, sel, tot, run, pos, gk = (sb(n, [P, E, NT]) for n in ("rank", "cmp", "sel", "tot", "run", "pos", "gk"))
        top = sb("top", [P, K, NT])
        den = sb("den", [P, NT])
        slot_f = sb("slot_f", [P, K, NT])
        first_mask = sb("mask", [P, E, NT])
        tri = sb("tri", [P, P])
        ones = sb("ones", [P, P])
        steps_of = sb("steps", [P, NT])
        full = sb("full", [P, E, NT])
        ntile, end, base = (sb(n, [P, E]) for n in ("ntile", "end", "base"))
        jrow = sb("jrow", [1, tiles])
        past = sb("past", [1, tiles, E])
        ex_f = sb("ex_f", [1, tiles])
        ps = m.psum(c, tag + "ps", [P, 4, 512])
        loaded, step, sel_ok, mm_ok, e_ok, added, cmp_ok = m.sems(c, tag, "loaded step sel_ok mm_ok e_ok added cmp_ok")
        half = E // 2
        with m.nc.Block() as block:
            @block.sync
            def _(sp):
                sp.dma_start(first_mask[:], m.ins["mask%d" % E]).then_inc(loaded, 16)
                sp.dma_start(tri[:], m.ins["tri"]).then_inc(loaded, 16)
                sp.dma_start(ones[:], m.ins["ones"]).then_inc(loaded, 16)
                sp.dma_start(steps_of[:], m.ins["steps"]).then_inc(loaded, 16)
                sp.dma_start(jrow[:], m.ins["jrow"][:, 0:tiles]).then_inc(loaded, 16)

            @block.tensor
            def _(pe):
                pe.wait_ge(loaded, 80)
                pe.wait_ge(sel_ok, 1)
                for a, w in enumerate((tri, ones)):
                    for q in range(2):
                        mm = pe.matmul(ps[:, 2 * a + q, 0:half * NT], w[:],
                                       sel[:, q * half:(q + 1) * half, :].rearrange("p e t -> p (e t)"), start=True, stop=True)
                mm.then_inc(mm_ok, 1)

            @block.scalar
            def _(act):
                act.wait_ge(sel_ok, 2)
                act.activation(gk[:], gk[:], ACT.Exp).then_inc(e_ok, 1)
                act.activation(top[:], top[:], ACT.Exp).then_inc(e_ok, 1)

            @block.vector
            def _(dve):
                n = [0]

                def link(i):
                    n[0] += 1
                    i.then_inc(step, 1)
                    dve.wait_ge(step, n[0])
                dve.wait_ge(loaded, 80)
                dve.memset(rank[:], 0.0).then_inc(added, 1)
                compared = 0
                for e in range(E + 1):
                    to = (cmp_, gk)[e % 2]
                    if e < E:
                        it = lambda k: G[:, e:e + 1, :].to_broadcast([P, k, NT])
                        if e >= 2:
                            dve.wait_ge(added, e)
                        dve.tensor_tensor(to[:, 0:e + 1, :], it(e + 1), G[:, 0:e + 1, :], ALU.is_gt).then_inc(cmp_ok, 1)
                        if e < E - 1:
                            dve.tensor_tensor(to[:, e + 1:, :], it(E - 1 - e), G[:, e + 1:E, :], ALU.is_ge).then_inc(cmp_ok, 1)
                    if e:
                        compared += 2 if e < E else 1
                        dve.wait_ge(cmp_ok, compared)
                        dve.wait_ge(added, e)
                        dve.tensor_tensor(rank[:], rank[:], (cmp_, gk)[(e - 1) % 2][:], ALU.add).then_inc(added, 1)
                dve.wait_ge(added, E + 1)
                dve.tensor_scalar(sel[:], rank[:], float(K), None, ALU.is_lt).then_inc(sel_ok, 1)
                for k in range(K):
                    link(dve.scalar_tensor_tensor(out=cmp_[:], in0=rank[:], scalar=float(k), in1=G[:, 0:E, :],
                                                  op0=ALU.is_equal, op1=ALU.mult))
                    link(dve.tensor_reduce(top[:, k, :], cmp_[:].rearrange("p e t -> p t e"), AX, ALU.add))
                link(dve.tensor_tensor(gk[:], G[:, 0:E, :], top[:, 0:1, :].to_broadcast([P, E, NT]), ALU.subtract))
                link(dve.tensor_copy(den[:], top[:, 0, :]))
                link(dve.tensor_tensor(top[:], top[:], den[:].unsqueeze(1).to_broadcast([P, K, NT]), ALU.subtract))
                dve.sem_inc(sel_ok, 1)
                dve.wait_ge(e_ok, 2)
                link(dve.tensor_reduce(den[:], top[:].rearrange("p k t -> p t k"), AX, ALU.add))
                link(dve.reciprocal(den[:], den[:]))
                link(dve.tensor_tensor(weight[:], top[:], den[:].unsqueeze(1).to_broadcast([P, K, NT]), ALU.mult))
                link(dve.tensor_tensor(gk[:], gk[:], sel[:], ALU.mult))
                link(dve.tensor_tensor(comb[:, :, 0:E].rearrange("p t e -> p e t"), gk[:],
                                       den[:].unsqueeze(1).to_broadcast([P, E, NT]), ALU.mult))
                dve.wait_ge(mm_ok, 1)
                for q in range(2):
                    link(dve.tensor_copy(tot[:, q * half:(q + 1) * half, :],
                                         ps[:, 2 + q, 0:half * NT].rearrange("p (e t) -> p e t", t=NT)))
                flat = lambda t: t[:].rearrange("p e t -> p (e t)")
                link(dve.tensor_tensor_scan(flat(run), flat(first_mask), flat(tot), 0.0, ALU.mult, ALU.add))
                link(dve.tensor_tensor(full[:], run[:, :, NT - 1:NT].to_broadcast([P, E, NT]),
                                       steps_of[:].unsqueeze(1).to_broadcast([P, E, NT]), ALU.is_gt))
                link(dve.tensor_reduce(ntile[:], full[:], AX, ALU.add))
                link(dve.tensor_tensor_scan(end[:], ones[:, 0:E], ntile[:], 0.0, ALU.mult, ALU.add))
                link(dve.tensor_tensor(base[:], end[:], ntile[:], ALU.subtract))
                link(dve.tensor_scalar(base[:], base[:], float(P), None, ALU.mult))
                link(dve.tensor_tensor(pos[:], run[:], tot[:], ALU.subtract))
                link(dve.tensor_tensor(pos[:], pos[:], base[:].unsqueeze(2).to_broadcast([P, E, NT]), ALU.add))
                for q in range(2):
                    link(dve.tensor_tensor(pos[:, q * half:(q + 1) * half, :],
                                           ps[:, q, 0:half * NT].rearrange("p (e t) -> p e t", t=NT),
                                           pos[:, q * half:(q + 1) * half, :], ALU.add))
                for k in range(K):
                    link(dve.scalar_tensor_tensor(out=cmp_[:], in0=rank[:], scalar=float(k), in1=pos[:],
                                                  op0=ALU.is_equal, op1=ALU.mult))
                    link(dve.tensor_reduce(slot_f[:, k, :], cmp_[:].rearrange("p e t -> p t e"), AX, ALU.add))
                    link(dve.tensor_copy(slots[:, :, k], slot_f[:, k, :]))
                link(dve.tensor_tensor(past[:], jrow[:].unsqueeze(2).to_broadcast([1, tiles, E]),
                                       end[0:1, :].unsqueeze(1).to_broadcast([1, tiles, E]), ALU.is_ge))
                link(dve.tensor_reduce(ex_f[:], past[:], AX, ALU.add))
                link(dve.tensor_scalar(ex_f[:], ex_f[:], float(E - 1), None, ALU.min))
                link(dve.tensor_copy(expert[:], ex_f[:]))


RING = 6


def scatter(m, tag, xs, h, mean, rstd, inv, slots, K, loads):
    with ExitStack() as c:
        x = m.sb(c, tag + "x", [P, RING,  D])
        row = m.sb(c, tag + "row", [P, RING, K, D + 1])
        place = m.sb(c, tag + "place", [P, NT, K], U32)
        scale = m.sb(c, tag + "scale", [P, D])
        at = m.sb(c, tag + "at", [P, RING, K], U32)
        x_ok, h_ok, row_ok, at_ok, loaded, scale_in, place_ok, rep_ok = m.sems(
            c, tag, "x_ok h_ok row_ok at_ok loaded scale_in place_ok rep_ok")
        sent = m.sems(c, tag, "sent0 sent1 sent2 sent3 sent4 sent5")
        with m.nc.Block() as block:
            @block.sync
            def _(sp):
                sp.dma_start(scale[:], m.ins["norm_scale"]).then_inc(scale_in, 16)
                sp.dma_start(place[:], m.ins["place%d" % K]).then_inc(scale_in, 16)
                for to, name in loads:
                    sp.dma_start(to, m.ins[name]).then_inc(loaded, 16)
                sp.wait_ge(loaded, 16 * len(loads))

            @block.vector
            def _(dve):
                dve.wait_ge(scale_in, 32)

                def prepare(i, s):
                    if later(i, RING):
                        dve.wait_ge(sent[s], (i - s) * 16 * K // RING)
                    dve.sem_inc(m.passed, 1)
                    dve.tensor_copy(at[:, s, :], slots[:, i, :]).then_inc(at_ok, 1)
                    dve.tensor_copy(row[:, s, :, D].bitcast(U32), place[:, i, :]).then_inc(place_ok, 1)
                    to, done = (row[:, :, 0, 0:D], row_ok) if inv is None else (x, x_ok)
                    dve.tensor_scalar(to[:, s, :], h[:, i, :], mean[:, bass.ds(i, 1)], rstd[:, bass.ds(i, 1)],
                                      ALU.subtract, ALU.mult).then_inc(done, 1)
                    if inv is not None:
                        dve.wait_ge(x_ok, i + 1)
                        dve.scalar_tensor_tensor(out=row[:, s, 0, 0:D], in0=x[:, s, :], scalar=inv[:, bass.ds(i, 1)],
                                                 in1=scale[:], op0=ALU.mult, op1=ALU.mult).then_inc(row_ok, 1)
                        dve.tensor_tensor(h[:, i, :], h[:, i, :], x[:, s, :], ALU.add).then_inc(h_ok, 1)
                pipelined(dve, NT, RING, (0, prepare))
                if inv is not None:
                    dve.wait_ge(h_ok, NT)

            @block.scalar
            def _(act):
                def repeat(i, s):
                    act.wait_ge(row_ok, i + 1)
                    act.activation(row[:, s, 1:, 0:D], row[:, s, 0:1, 0:D].to_broadcast([P, K - 1, D]),
                                   ACT.Copy).then_inc(rep_ok, 1)
                pipelined(act, NT, RING, (0, repeat))

            @block.gpsimd
            def _(pool):
                pool.wait_ge(m.xs_zero, (SLOT0 + SLOT1) // 8 * 16)

                def send(i, s):
                    pool.wait_ge(rep_ok, i + 1)
                    pool.sem_inc(m.passed, 1)
                    pool.wait_ge(at_ok, i + 1)
                    pool.sem_inc(m.passed, 1)
                    pool.wait_ge(place_ok, i + 1)
                    pool.sem_inc(m.passed, 1)
                    for k in range(K):
                        pool.indirect_dma_start(out=xs, out_offset=bass.IndirectOffsetOnAxis(ap=at[:, s, k:k + 1], axis=0),
                                                in_=row[:, s, k, :], in_offset=None).then_inc(sent[s], 16)
                pipelined(pool, NT, RING, (0, send))
                for s in range(RING):
                    pool.wait_ge(sent[s], 16 * K * (NT // RING))


def experts(m, tag, xs, E, C, gated, tiles, w1, w2, expert, beside=None):
    I = C * P
    HW = 384
    AB = -(-C // 3)
    XB = 2 if AB == 1 else 1
    with ExitStack() as c:
        xin = m.sb(c, tag + "xin", [P, 4, D + 1])
        at = m.sb(c, tag + "at", [P, 8], U32)
        xT = m.sb(c, tag + "xT", [P, 2, 2, P])
        a = m.sb(c, tag + "a", [P, 2, I])
        glu, lin, sig = ((m.sb(c, tag + n, [P, 2, HW]) for n in ("glu", "lin", "sig")) if gated else (None,) * 3)
        aT = m.sb(c, tag + "aT", [P, 2, C, P])
        y = m.sb(c, tag + "y", [P, 2, D])
        xps = m.psum(c, tag + "xps", [P, XB, 512])
        hps = m.psum(c, tag + "hps", [P, 2, 2, 512])
        aps = m.psum(c, tag + "aps", [P, AB, 512])
        yps = m.psum(c, tag + "yps", [P, 512])
        ones_ok, xp_ok, xT_ok, h0_ok, h1_ok, glu_ok, sig_ok, lin_ok, prod_ok, a_ok, ap_ok, aT_ok, y_mm, y_ok, at_ok = m.sems(
            c, tag, "ones_ok xp_ok xT_ok h0_ok h1_ok glu_ok sig_ok lin_ok prod_ok a_ok ap_ok aT_ok y_mm y_ok at_ok")
        arrived = m.sems(c, tag, "in0 in1 in2 in3")
        stored = m.sems(c, tag, "out0 out1")
        with m.nc.Block() as block:
            @block.sync
            def _(sp):
                def load(i, s):
                    if later(i, 4):
                        sp.wait_ge(xp_ok, i - 3)
                        sp.wait_ge(at_ok, i - 3)
                    sp.dma_start(xin[:, s, :], xs[bass.ds(i * P, P), 0:D + 1]).then_inc(arrived[s], 16)
                pipelined(sp, tiles, 4, (0, load))

            @block.gpsimd
            def _(pool):
                pool.memset(xT[DC:DC + 1, :, 1, :], 1.0).then_inc(ones_ok, 1)
                pool.wait_ge(ones_ok, 1)

                def places(i, s):
                    pool.wait_ge(arrived[s % 4], landed(i, s % 4, 4))
                    pool.sem_inc(m.passed, 1)
                    if later(i, 8):
                        pool.wait_ge(stored[s % 2], (i - 8 - s % 2) * 8 + 16)
                        pool.sem_inc(m.passed, 1)
                    pool.tensor_copy(at[:, s:s + 1], xin[:, s % 4, D:].bitcast(U32)).then_inc(at_ok, 1)

                def store(i, s):
                    pool.wait_ge(y_ok, i + 1)
                    pool.sem_inc(m.passed, 1)
                    pool.wait_ge(at_ok, i + 1)
                    pool.sem_inc(m.passed, 1)
                    if later(i, 1):
                        pool.wait_ge(stored[(s + 1) % 2], (i - 1 - (s + 1) % 2) * 8 + 16)
                        pool.sem_inc(m.passed, 1)
                    pool.indirect_dma_start(out=m.ys, out_offset=bass.IndirectOffsetOnAxis(ap=at[:, s:s + 1], axis=0),
                                            in_=y[:, s % 2, :], in_offset=None).then_inc(stored[s % 2], 16)
                pipelined(pool, tiles, 8, (5, store), (0, places))
                for s in range(2):
                    pool.wait_ge(stored[s], 16 * (tiles // 2))

            @block.tensor
            def _(pe):
                pe.wait_ge(ones_ok, 1)

                def turn_x(i, s):
                    s %= 4
                    pe.wait_ge(arrived[s], landed(i, s, 4))
                    if later(i, XB):
                        pe.wait_ge(xT_ok, i - XB + 1)
                    for k in range(2):
                        mm = pe.transpose(xps[0:DC, s % XB, k * P:(k + 1) * P], xin[:, s, k * DC:(k + 1) * DC], m.ident[:])
                    mm.then_inc(xp_ok, 1)

                def up(i, s, half):
                    s %= 2
                    if half == 0:
                        pe.wait_ge(xT_ok, i + 1)
                        if later(i, 2):
                            pe.wait_ge(lin_ok if gated else a_ok, i - 1)
                    e = expert_of["up"]
                    for k in range(2):
                        r = DC + k
                        mm = pe.matmul(hps[:, s, half, 0:HW], xT[0:r, s, k, :],
                                       w1[0:r, e, k, half * HW:(half + 1) * HW], start=(k == 0), stop=(k == 1))
                    mm.then_inc((h0_ok, h1_ok)[half], 1)

                def turn_a(i, s):
                    s %= 2
                    pe.wait_ge(a_ok, i + 1)
                    if later(i, 1):
                        pe.wait_ge(aT_ok, i * AB)
                    for k in range(C):
                        mm = pe.transpose(aps[:, k // 3, (k % 3) * P:(k % 3 + 1) * P], a[:, s, k * P:(k + 1) * P], m.ident[:])
                    mm.then_inc(ap_ok, 1)

                def down(i, s):
                    s %= 2
                    pe.wait_ge(aT_ok, (i + 1) * AB)
                    if later(i, 1):
                        pe.wait_ge(y_ok, i)
                    e = expert_of["down"]
                    for k in range(C):
                        mm = pe.matmul(yps[:, 0:D], aT[:, s, k, :], w2[:, e, k, :], start=(k == 0), stop=(k == C - 1))
                    mm.then_inc(y_mm, 1)

                expert_of = {}

                def look_up(use):
                    def fetch(i, s):
                        at = expert[0:1, i:i + 1] if isinstance(i, int) else expert[0:1, bass.ds(i, 1)]
                        expert_of[use] = pe.value_load(at, min_val=0, max_val=E - 1)
                    return fetch
                pipelined(pe, tiles, 8, (1, look_up("up")), (0, turn_x), (1, lambda i, s: up(i, s, 0)), (3, turn_a),
                          (1, lambda i, s: up(i, s, 1)), (3, look_up("down")), (3, down))

            @block.scalar
            def _(act):
                def copy_x(i, s):
                    act.wait_ge(xp_ok, i + 1)
                    if later(i, 2):
                        act.wait_ge(h1_ok, i - 1)
                    act.activation(xT[0:DC, s], xps[0:DC, s % XB, 0:2 * P].rearrange("p (c n) -> p c n", c=2),
                                   ACT.Copy).then_inc(xT_ok, 1)

                def copy_a(i, s):
                    act.wait_ge(ap_ok, i + 1)
                    if later(i, 2):
                        act.wait_ge(y_mm, i - 1)
                    act.activation(aT[:, s, 0:3, :], aps[:, 0, 0:HW].rearrange("p (c n) -> p c n", n=P),
                                   ACT.Copy).then_inc(aT_ok, 1)

                def squash(i, s):
                    act.wait_ge(glu_ok, i + 1)
                    if later(i, 2):
                        act.wait_ge(prod_ok, i - 1)
                    act.activation(sig[:, s, :], glu[:, s, :], ACT.Sigmoid, scale=1.702).then_inc(sig_ok, 1)

                def gelu(i, s):
                    act.wait_ge(h1_ok, i + 1)
                    if later(i, 2):
                        act.wait_ge(ap_ok, i - 1)
                    act.activation(a[:, s, :].rearrange("p (g n) -> p g n", g=2), hps[:, s, :, 0:HW],
                                   ACT.Gelu_apprx_tanh).then_inc(a_ok, 1)

                def copy_y(i, s):
                    act.wait_ge(y_mm, i + 1)
                    if later(i, 2):
                        act.wait_ge(stored[s], landed(i, s) - 16)
                    act.activation(y[:, s, :], yps[:, 0:D], ACT.Copy).then_inc(y_ok, 1)
                pipelined(act, tiles, 2, (0, copy_x), (3, copy_a), (1, squash if gated else gelu), (3, copy_y))

            @block.vector
            def _(dve):
                def gate(i, s):
                    dve.wait_ge(h0_ok, i + 1)
                    dve.tensor_scalar(glu[:, s, :], hps[:, s, 0, 0:HW], 7.0, None, ALU.min).then_inc(glu_ok, 1)
                    dve.wait_ge(sig_ok, i + 1)
                    dve.tensor_tensor(sig[:, s, :], glu[:, s, :], sig[:, s, :], ALU.mult).then_inc(prod_ok, 1)
                    dve.wait_ge(h1_ok, i + 1)
                    dve.tensor_scalar(lin[:, s, :], hps[:, s, 1, 0:HW], 7.0, -7.0, ALU.min, ALU.max).then_inc(lin_ok, 1)
                    dve.wait_ge(lin_ok, i + 1)
                    dve.wait_ge(prod_ok, i + 1)
                    if later(i, 2):
                        dve.wait_ge(ap_ok, i - 1)
                    dve.scalar_tensor_tensor(out=a[:, s, :], in0=lin[:, s, :], scalar=1.0, in1=sig[:, s, :],
                                             op0=ALU.add, op1=ALU.mult).then_inc(a_ok, 1)

                def copy_a(i, s):
                    dve.wait_ge(ap_ok, i + 1)
                    if later(i, 2):
                        dve.wait_ge(y_mm, i - 1)
                    dve.tensor_copy(aT[:, s, 3:6, :], aps[:, 1, 0:HW].rearrange("p (c n) -> p c n", n=P)).then_inc(aT_ok, 1)
                pipelined(dve, tiles, 2, *([(1, gate)] if gated else [
                    (0, lambda i, s: beside(dve, i, 0)), (3, copy_a), (0, lambda i, s: beside(dve, i, 1))]))


def gather(m, tag, h, weight, comb, E, K, extra, stats=None):
    R = E + extra
    with ExitStack() as c:
        g = m.sb(c, tag + "g", [P, RING,  K, D])
        cb = m.sb(c, tag + "cb", [P, 3, R])
        cT = m.sb(c, tag + "cT", [R, 3, P])
        rows = m.sb(c, tag + "rows", [R, D])
        times = m.sb(c, tag + "times", [R, D])
        tp = m.psum(c, tag + "tp", [P, 3, 512])
        ps = m.psum(c, tag + "ps", [P, 3, 512])
        cb_ok, tp_ok, cT_ok, mm_ok, bias_ok, stat, loaded, rows_ok, stored = m.sems(
            c, tag, "cb_ok tp_ok cT_ok mm_ok bias_ok stat loaded rows_ok stored")
        added = m.sems(c, tag, " ".join("added%d" % k for k in range(K)))
        used = added[K - 1]
        here = m.sems(c, tag, "g0 g1 g2 g3 g4 g5")
        with m.nc.Block() as block:
            @block.sync
            def _(sp):
                sp.dma_start(rows[:], m.ins[tag + "_rows"]).then_inc(loaded, 16)
                sp.dma_start(times[:], m.ins[tag + "_times"]).then_inc(loaded, 16)

                def fetch(i, s):
                    if later(i, RING):
                        sp.wait_ge(used, i - RING + 1)
                    sp.dma_start(g[:, s], m.ys[bass.ds(i * P * K, P * K), :].rearrange("(p k) d -> p k d", k=K)
                                 ).then_inc(here[s], 16)

                def store(i, s):
                    sp.wait_ge(used, i + 1)
                    sp.dma_start(m.out[bass.ds(i * P, P), :], h[:, i, :]).then_inc(stored, 16)
                pipelined(sp, NT, RING, (0, fetch), *([(4, store)] if stats is None else []))
                if stats is None:
                    sp.wait_ge(stored, 16 * NT)

            @block.scalar
            def _(act):
                def copy(i, s):
                    if later(i, 3):
                        act.wait_ge(tp_ok, i - 2)
                    act.sem_inc(m.passed, 1)
                    act.activation(cb[:, s, :], comb[:, i, 0:R], ACT.Copy).then_inc(cb_ok, 1)

                def rows_of(i, s):
                    act.wait_ge(tp_ok, i + 1)
                    if later(i, 3):
                        act.wait_ge(mm_ok, i - 2)
                    act.activation(cT[:, s, :], tp[0:R, s, 0:P], ACT.Copy).then_inc(cT_ok, 1)
                pipelined(act, NT, 3, (0, copy), (1, rows_of))

            @block.tensor
            def _(pe):
                pe.wait_ge(rows_ok, 1)

                def turn(i, s):
                    pe.wait_ge(cb_ok, i + 1)
                    if later(i, 3):
                        pe.wait_ge(cT_ok, i - 2)
                    pe.transpose(tp[0:R, s, 0:P], cb[:, s, :], m.ident[:]).then_inc(tp_ok, 1)

                def dense(i, s):
                    pe.wait_ge(cT_ok, i + 1)
                    if later(i, 3):
                        pe.wait_ge(bias_ok, i - 2)
                    pe.matmul(ps[:, s, 0:D], cT[:, s, :], rows[:], start=True, stop=True).then_inc(mm_ok, 1)
                pipelined(pe, NT, 3, (0, turn), (1, dense))

            @block.vector
            def _(dve):
                dve.wait_ge(loaded, 32)
                dve.tensor_tensor(rows[:], rows[:], times[:], ALU.mult).then_inc(rows_ok, 1)

                def bias(i, s):
                    dve.wait_ge(mm_ok, i + 1)
                    dve.tensor_tensor(h[:, i, :], ps[:, s % 3, 0:D], h[:, i, :], ALU.add).then_inc(bias_ok, 1)

                def add(k):
                    def one(i, s):
                        if k == 0:
                            dve.wait_ge(here[s], landed(i, s, RING))
                        dve.wait_ge(added[k - 1] if k else bias_ok, i + 1)
                        dve.scalar_tensor_tensor(out=h[:, i, :], in0=g[:, s, k, :], scalar=weight[:, k, bass.ds(i, 1)],
                                                 in1=h[:, i, :], op0=ALU.mult, op1=ALU.add).then_inc(added[k], 1)
                    return one

                def stat_of(i, s):
                    dve.wait_ge(used, i + 1)
                    dve.bn_stats(stats[:, i, :], h[:, i, :]).then_inc(stat, 1)
                early = [bias] + [add(k) for k in range(K // 2)]
                late = [add(k) for k in range(K // 2, K)] + ([stat_of] if stats is not None else [])
                turns = []
                for n in range(max(len(early), len(late))):
                    turns += [(0, f) for f in early[n:n + 1]] + [(1, f) for f in late[n:n + 1]]
                pipelined(dve, NT, RING, *turns)
                if stats is not None:
                    dve.wait_ge(stat, NT)


MAGIC = 12582912.0


def quantised_attention(m, xT, oT):
    LAST = slice(N - 32, N)
    VC = QH * 32
    with ExitStack() as c:
        sb = lambda name, shape, dt=F32: m.sb(c, "qa_" + name, shape, dt)
        wqk = sb("wqk", [DC, 2, 2, QC * P])
        wv = sb("wv", [DC, 2, QH * 32])
        sc = sb("sc", [P, 6])
        inv = sb("inv", [P, 6])
        mul = sb("mul", [P, 4])
        magic = sb("magic", [P, 1])
        xs = sb("xs", [DC, 2, 2, N])
        r = sb("r", [P, 2, 2, QC * N])
        rv = sb("rv", [P, 2, VC + QC * 32])
        qk = sb("qk", [P, 2, 2, QC * N], BF16)
        v = sb("v", [P, 2, VC + QC * 32], BF16)
        rs = sb("rs", [P, 5, 3 * N])
        s = sb("s", [P, 2, 5, 3 * N], BF16)
        ro = sb("ro", [P, 2, QC * N])
        qps = m.psum(c, "qa_qps", [P, 2, 512])
        sps = m.psum(c, "qa_sps", [P, 5, 512])
        ops_ = m.psum(c, "qa_ops", [P, 512])
        (loaded, const, xs_ok, q_mm, r_ok, rc_ok, qk_ok, v_mm, rv_ok, rvc_ok, v_ok, s_mm, rs_ok, rsc_ok, s_ok, o_mm, ro_ok,
         roc_ok, o_ok, magic_ok) = m.sems(
            c, "qa", "loaded const xs_ok q_mm r_ok rc_ok qk_ok v_mm rv_ok rvc_ok v_ok s_mm rs_ok rsc_ok s_ok o_mm ro_ok "
            "roc_ok o_ok magic_ok")
        with m.nc.Block() as block:
            @block.sync
            def _(sp):
                sp.dma_start(wqk[:], m.ins["q_wqk"]).then_inc(loaded, 16)
                sp.dma_start(wv[:], m.ins["q_wv"]).then_inc(loaded, 16)
                sp.dma_start(sc[:], m.ins["q_scales"]).then_inc(loaded, 16)

            @block.gpsimd
            def _(pool):
                pool.memset(magic[:], MAGIC).then_inc(magic_ok, 1)

                def widen(b, p):
                    pool.wait_ge(rc_ok, b + 1)
                    if later(b, 2):
                        pool.wait_ge(s_mm, b - 1)
                    pool.sem_inc(m.passed, 1)
                    pool.tensor_scalar(qk[:, p], r[:, p], -MAGIC, 1.0, ALU.add, ALU.mult).then_inc(qk_ok, 1)

                def widen_v(b, p):
                    pool.wait_ge(rvc_ok, b + 1)
                    if later(b, 2):
                        pool.wait_ge(o_mm, b - 1)
                    pool.sem_inc(m.passed, 1)
                    pool.tensor_scalar(v[:, p], rv[:, p], -MAGIC, 1.0, ALU.add, ALU.mult).then_inc(v_ok, 1)
                pipelined(pool, B, 2, (0, widen), (0, widen_v))

            @block.tensor
            def _(pe):
                pe.wait_ge(loaded, 48)

                def project_(b, p):
                    pe.wait_ge(xs_ok, b + 1)
                    if later(b, 1):
                        pe.wait_ge(rv_ok, b)
                    for w in range(2):
                        for ch in range(QC):
                            for k in range(2):
                                mm = pe.matmul(qps[:, w, ch * N:(ch + 1) * N], wqk[:, k, w, ch * P:(ch + 1) * P],
                                               xs[:, p, k, :], start=(k == 0), stop=(k == 1))
                    mm.then_inc(q_mm, 1)

                def values(b, p):
                    pe.wait_ge(r_ok, b + 1)
                    for k in range(2):
                        pe.matmul(qps[:, 0, 0:QH * 32], xs[:, p, k, 0:P], wv[:, k, :], start=(k == 0), stop=(k == 1))
                    for j in range(4):
                        for k in range(2):
                            mm = pe.matmul(qps[32 * j:32 * j + 32, 1, 0:QC * 32], xs[:, p, k, LAST],
                                           wv[:, k, :].rearrange("p (c j d) -> p j c d", j=4, d=32)[:, j],
                                           start=(k == 0), stop=(k == 1), tile_position=(0, 32 * j))
                    mm.then_inc(v_mm, 1)

                def scores(b, p):
                    pe.wait_ge(qk_ok, b + 1)
                    if later(b, 1):
                        pe.wait_ge(rs_ok, b)
                    for h in range(QH):
                        ch, j = h // 4, h % 4
                        at = slice(32 * j, 32 * j + QD)
                        q_, k_ = (qk[at, p, w, ch * N:(ch + 1) * N] for w in (0, 1))
                        pe.matmul(sps[:, j, ch * N:(ch + 1) * N], k_[:, 0:P], q_, start=True, stop=True,
                                  tile_position=(32 * j, 0))
                        mm = pe.matmul(sps[32 * j:32 * j + 32, 4, ch * N:(ch + 1) * N], k_[:, LAST], q_, start=True, stop=True,
                                       tile_position=(32 * j, 32 * j))
                    mm.then_inc(s_mm, 1)

                def outputs(b, p):
                    pe.wait_ge(s_ok, b + 1)
                    pe.wait_ge(v_ok, b + 1)
                    if later(b, 1):
                        pe.wait_ge(ro_ok, b)
                    for h in range(QH):
                        ch, j = h // 4, h % 4
                        to = ops_[32 * j:32 * j + 32, ch * N:(ch + 1) * N]
                        pe.matmul(to, v[:, p, h * 32:(h + 1) * 32], s[:, p, j, ch * N:(ch + 1) * N],
                                  start=True, stop=False, tile_position=(0, 32 * j))
                        at = slice(32 * j, 32 * j + 32)
                        mm = pe.matmul(to, v[at, p, VC + ch * 32:VC + (ch + 1) * 32], s[at, p, 4, ch * N:(ch + 1) * N],
                                       start=False, stop=True, tile_position=(32 * j, 32 * j))
                    mm.then_inc(o_mm, 1)
                pipelined(pe, B, 2, (0, project_), (1, scores), (0, values), (2, outputs))

            @block.scalar
            def _(act):
                act.wait_ge(const, 2)
                act.wait_ge(magic_ok, 1)
                bias = magic[:, 0:1]

                def round_qk(b, p):
                    act.wait_ge(q_mm, b + 1)
                    if later(b, 2):
                        act.wait_ge(qk_ok, b - 1)
                    for w in range(2):
                        i = act.activation(r[:, p, w, :], qps[:, w, 0:QC * N], ACT.Identity, bias=bias, scale=inv[:, w:w + 1])
                    i.then_inc(r_ok, 1)

                def round_v(b, p):
                    act.wait_ge(v_mm, b + 1)
                    if later(b, 2):
                        act.wait_ge(v_ok, b - 1)
                    act.activation(rv[:, p, 0:VC], qps[:, 0, 0:VC], ACT.Identity, bias=bias, scale=inv[:, 2:3])
                    act.activation(rv[:, p, VC:], qps[:, 1, 0:QC * 32], ACT.Identity, bias=bias,
                                   scale=inv[:, 5:6]).then_inc(rv_ok, 1)

                def round_s(b, p):
                    act.wait_ge(s_mm, b + 1)
                    if later(b, 1):
                        act.wait_ge(s_ok, b)
                    act.activation(rs[:], sps[:, :, 0:3 * N], ACT.Identity, bias=bias, scale=mul[:, 0:1]).then_inc(rs_ok, 1)

                def round_o(b, p):
                    act.wait_ge(o_mm, b + 1)
                    if later(b, 2):
                        act.wait_ge(o_ok, b - 1)
                    act.activation(ro[:, p, :], ops_[:, 0:QC * N], ACT.Identity, bias=bias, scale=mul[:, 1:2]).then_inc(ro_ok, 1)
                pipelined(act, B, 2, (0, round_qk), (1, round_s), (0, round_v), (2, round_o))

            @block.vector
            def _(dve):
                dve.wait_ge(loaded, 48)
                dve.reciprocal(inv[:, 0:5], sc[:, 0:5]).then_inc(const, 1)
                n = [0]

                def link(i):
                    n[0] += 1
                    i.then_inc(m.chained, 1)
                    m.chained_so_far += 1
                    dve.wait_ge(m.chained, m.chained_so_far)
                dve.wait_ge(const, 1)
                link(dve.tensor_tensor(mul[:, 0:1], sc[:, 0:1], sc[:, 1:2], ALU.mult))
                link(dve.tensor_tensor(mul[:, 0:1], mul[:, 0:1], inv[:, 3:4], ALU.mult))
                link(dve.tensor_scalar(mul[:, 0:1], mul[:, 0:1], float(QD) ** -0.5 / N, None, ALU.mult))
                link(dve.tensor_tensor(mul[:, 1:2], sc[:, 3:4], sc[:, 2:3], ALU.mult))
                link(dve.tensor_tensor(inv[:, 5:6], inv[:, 2:3], sc[:, 5:6], ALU.mult))
                dve.tensor_tensor(mul[:, 1:2], mul[:, 1:2], inv[:, 4:5], ALU.mult).then_inc(const, 1)

                def stage_in(b, p):
                    if later(b, 2):
                        dve.wait_ge(v_mm, b - 1)
                    dve.sem_inc(m.passed, 1)
                    dve.tensor_copy(xs[:, p], xT[:, :, bass.ds(b * N, N)]).then_inc(xs_ok, 1)

                def clip(t, low, high, done):
                    dve.tensor_scalar(t, t, MAGIC + low, MAGIC + high, ALU.max, ALU.min).then_inc(done, 1)

                def inputs(b, p):
                    dve.wait_ge(r_ok, b + 1)
                    clip(r[:, p], -4.0, 3.0, rc_ok)

                def input_v(b, p):
                    dve.wait_ge(rv_ok, b + 1)
                    clip(rv[:, p], -4.0, 3.0, rvc_ok)

                def scores(b, p):
                    dve.wait_ge(rs_ok, b + 1)
                    clip(rs[:], 0.0, 7.0, rsc_ok)
                    dve.wait_ge(rsc_ok, b + 1)
                    if later(b, 2):
                        dve.wait_ge(o_mm, b - 1)
                    dve.tensor_scalar(s[:, p], rs[:], MAGIC, None, ALU.subtract).then_inc(s_ok, 1)

                def outputs(b, p):
                    dve.wait_ge(ro_ok, b + 1)
                    clip(ro[:, p, :], -4.0, 3.0, roc_ok)
                    dve.wait_ge(roc_ok, b + 1)
                    dve.tensor_scalar(oT[:, :, bass.ds(b * N, N)], ro[:, p, :].rearrange("p (c n) -> p c n", c=QC),
                                      MAGIC, sc[:, 4:5], ALU.subtract, ALU.mult).then_inc(o_ok, 1)
                pipelined(dve, B, 2, (0, stage_in), (1, inputs), (2, scores), (1, input_v), (3, outputs))
                dve.wait_ge(o_ok, B)


class Spectral:

    def __init__(self, m, ctx, steps):
        assert steps >= N - 1
        sb = lambda name, shape: m.sb(ctx, "sp_" + name, shape)
        self.m, self.steps = m, steps
        self.raw = sb("raw", [2 * B, N])
        self.sign = sb("sign", [2 * B, N])
        self.a2 = sb("a2", [2 * B, steps + 1, 2])
        self.d = sb("d", [2 * B, steps + 1, 2])
        self.cur = sb("cur", [2 * B, 2, 2])
        self.sq = sb("sq", [2 * B, 2, 2])
        self.mag = sb("mag", [2 * B, 2])
        self.rec = sb("rec", [2 * B, 2])
        self.sq_ok, self.rec_ok, self.cur_ok, self.d_ok = m.sems(ctx, "sp", "sq_ok rec_ok cur_ok d_ok")

    def start(self, G, col):
        m, raw, sign, a2 = self.m, self.raw, self.sign, self.a2
        with ExitStack() as c:
            v = m.sb(c, "sp_v", [P, NT])
            vT = m.sb(c, "sp_vT", [NT, P])
            ps = m.psum(c, "sp_ps", [P, 512])
            step, vp_ok, vT_ok, there, raw_ok, sign_ok = m.sems(c, "ss", "step vp_ok vT_ok there raw_ok sign_ok")
            with m.nc.Block() as block:
                @block.sync
                def _(sp):
                    sp.dma_start(sign[:], m.ins["sign"]).then_inc(sign_ok, 16)
                    sp.wait_ge(vT_ok, 1)
                    sp.dma_start(m.v_row.rearrange("(t p) -> t p", p=P), vT[:]).then_inc(there, 16)
                    sp.wait_ge(there, 16)
                    for k in range(2):
                        sp.dma_start(raw[k * B:(k + 1) * B, :], m.v_row.rearrange("(b n) -> b n", n=N)).then_inc(raw_ok, 16)

                @block.tensor
                def _(pe):
                    pe.wait_ge(step, 2)
                    pe.transpose(ps[0:NT, 0:P], v[:], m.ident[:]).then_inc(vp_ok, 1)

                @block.vector
                def _(dve):
                    n = [0]

                    def link(i):
                        n[0] += 1
                        i.then_inc(step, 1)
                        dve.wait_ge(step, n[0])
                    link(dve.tensor_scalar(v[:], G[:, col, :], 3.0, -3.0, ALU.min, ALU.max))
                    link(dve.tensor_scalar(v[:], v[:], 2.0, None, ALU.subtract))
                    dve.wait_ge(vp_ok, 1)
                    dve.tensor_copy(vT[:], ps[0:NT, 0:P]).then_inc(vT_ok, 1)
                    link(dve.memset(a2[:], -1.0))
                    dve.wait_ge(raw_ok, 32)
                    dve.wait_ge(sign_ok, 16)
                    link(dve.tensor_tensor(a2[0:B, 0:N, 0], raw[0:B, :], sign[0:B, :], ALU.mult))
                    link(dve.tensor_tensor(a2[B:2 * B, 0:N, 0], raw[B:2 * B, ::-1], sign[B:2 * B, :], ALU.mult))
                    dve.tensor_copy(self.cur[:, 0, :], a2[:, 0, :]).then_inc(self.cur_ok, 1)
                    link(dve.tensor_copy(self.d[:, 0, :], a2[:, 0, :]))

    def step(self, dve, i, s):
        cur, sq, mag, rec = self.cur, self.sq, self.mag, self.rec
        dve.wait_ge(self.cur_ok, i + 1)
        dve.tensor_tensor(sq[:, s, :], cur[:, s, :], cur[:, s, :], ALU.mult).then_inc(self.sq_ok, 1)
        dve.wait_ge(self.sq_ok, 2 * i + 1)
        dve.tensor_tensor(mag[:, s:s + 1], sq[:, s, 0:1], sq[:, s, 1:2], ALU.add).then_inc(self.sq_ok, 1)
        dve.wait_ge(self.sq_ok, 2 * i + 2)
        dve.reciprocal(rec[:, s:s + 1], mag[:, s:s + 1]).then_inc(self.rec_ok, 1)
        dve.wait_ge(self.rec_ok, i + 1)
        dve.scalar_tensor_tensor(out=cur[:, 1 - s, :], in0=cur[:, s, :], scalar=rec[:, s:s + 1],
                                 in1=self.a2[:, i + 1, :], op0=ALU.mult, op1=ALU.add).then_inc(self.cur_ok, 1)
        dve.wait_ge(self.cur_ok, i + 2)
        dve.sem_inc(self.m.passed, 1)
        dve.tensor_copy(self.d[:, i + 1, :], cur[:, 1 - s, :]).then_inc(self.d_ok, 1)

    def finish(self, feats):
        m, raw, sign = self.m, self.raw, self.sign
        d = self.d[:, 0:N, :]
        with ExitStack() as c:
            sb = lambda name, shape: m.sb(c, "sp_" + name, shape)
            back = sb("back", [B, N, 2])
            rev = sb("rev", [2 * B, N, 2])
            s2 = sb("s2", [B, N, 2])
            q = sb("q", [B, N, 2])
            n2 = sb("n2", [B, N])
            f = sb("f", [NT, P, 2])
            fp = m.psum(c, "sp_fp", [P, 2, 512])
            step, rev_ok, back_ok, q_ok, q_there, f_in, f_mm = m.sems(c, "sf", "step rev_ok back_ok q_ok q_there f_in f_mm")
            with m.nc.Block() as block:
                @block.sync
                def _(sp):
                    sp.wait_ge(rev_ok, 1)
                    sp.dma_start(back[:], rev[B:2 * B]).then_inc(back_ok, 16)
                    sp.wait_ge(q_ok, 1)
                    sp.dma_start(m.f_row.rearrange("(b n) c -> b n c", n=N), q[:]).then_inc(q_there, 16)
                    sp.wait_ge(q_there, 16)
                    sp.dma_start(f[:], m.f_row.rearrange("(t p) c -> t p c", p=P)).then_inc(f_in, 16)

                @block.tensor
                def _(pe):
                    pe.wait_ge(f_in, 16)
                    for k in range(2):
                        pe.transpose(fp[:, k, 0:NT], f[:, :, k], m.ident[0:NT, 0:NT]).then_inc(f_mm, 1)

                @block.vector
                def _(dve):
                    n = [0]

                    def link(i):
                        n[0] += 1
                        i.then_inc(step, 1)
                        dve.wait_ge(step, n[0])
                    dve.wait_ge(self.d_ok, self.steps)
                    link(dve.tensor_tensor(d[:, :, 0], d[:, :, 0], sign[:], ALU.mult))
                    dve.tensor_copy(rev[B:2 * B], d[B:2 * B, ::-1, :]).then_inc(rev_ok, 1)
                    dve.wait_ge(back_ok, 16)
                    link(dve.tensor_tensor(s2[:], d[0:B], back[:], ALU.add))
                    link(dve.tensor_tensor(s2[:, :, 0], s2[:, :, 0], raw[0:B, :], ALU.subtract))
                    link(dve.tensor_scalar(s2[:, :, 1], s2[:, :, 1], 1.0, None, ALU.add))
                    link(dve.tensor_tensor(q[:], s2[:], s2[:], ALU.mult))
                    link(dve.tensor_tensor(n2[:], q[:, :, 0], q[:, :, 1], ALU.add))
                    link(dve.reciprocal(n2[:], n2[:]))
                    link(dve.tensor_tensor(q[:, :, 0], s2[:, :, 0], n2[:], ALU.mult))
                    link(dve.scalar_tensor_tensor(out=q[:, :, 1], in0=s2[:, :, 1], scalar=-1.0, in1=n2[:],
                                                  op0=ALU.mult, op1=ALU.mult))
                    dve.tensor_scalar(q[:], q[:], 10.0, -10.0, ALU.min, ALU.max).then_inc(q_ok, 1)
                    link(dve.memset(feats[:, :, 2], 1.0))
                    for k in range(2):
                        dve.wait_ge(f_mm, k + 1)
                        link(dve.tensor_copy(feats[:, :, k], fp[:, k, 0:NT]))


def model(nc, ins, out):
    with ExitStack() as ctx:
        m = Model(nc, ins, out, ctx)
        m.h0 = nc.dram_tensor("h0", [P, NT, D], F32).ap()
        m.xs = [nc.dram_tensor("slot_rows%d" % n, [tiles * P, PITCH], F32).ap() for n, tiles in ((0, SLOT0), (1, SLOT1))]
        m.ys = nc.dram_tensor("expert_out", [TOK * K0 + P, D], F32).ap()
        m.v_row = nc.dram_tensor("v_row", [TOK], F32).ap()
        m.f_row = nc.dram_tensor("f_row", [TOK, 2], F32).ap()
        m.kv_rows = nc.dram_tensor("kv_rows", [TPOOL, 2 * A0], F32).ap()
        constants(m, ctx)
        region = m.sb(ctx, "region", [P, 2, TOK])
        xT = region[0:DC]
        m.empty = m.sb(ctx, "empty", [P, 2, D + 1])
        m.unused = m.sb(ctx, "unused", [P, 2], U32)
        m.h_in = m.sem(ctx, "h_in")
        m.zeroed, m.empty_in, m.xs_zero = m.sems(ctx, "xs", "zeroed empty_in zero")
        m.h = region[:].rearrange("p c n -> p (c n)")[:, 0:NT * D].rearrange("p (t d) -> p t d", d=D)
        stats = m.sb(ctx, "stats", [P, NT, 6])
        with ExitStack() as attn:
            ksum = m.sb(attn, "ksum", [P, B, HP])
            pooling = attn.enter_context(ExitStack())
            xpT = m.sb(pooling, "xpT", [DC, 2, TPOOL])
            with ExitStack() as c:
                h = m.sb(c, "h_in", [P, NT, D])
                posb = m.sb(c, "posb", [P, D])
                embed(m, h, posb)
                layernorm_T(m, h, xT, "l0", xpT, m.h0)
            with ExitStack() as c:
                kcT = m.sb(c, "kcT", [P, HP, NPT * P])
                with ExitStack() as k:
                    kp3 = m.sb(k, "kp3", [P, HP, NPT * P])
                    kp2 = m.sb(k, "kp2", [P, HP, TOK // 4])
                    kp1 = m.sb(k, "kp1", [P, HP, TOK // 2])
                    wk = m.sb(k, "wk", [DC, 2, A0])
                    keys(m, xT, wk, kp1)
                    mlp(m, "p0", 0, kp1, kp2, TOK // 2 // P, True)
                    clear(m, kp3[:, :, TPOOL:])
                    mlp(m, "p1", 1, kp2, kp3, TOK // 4 // P, True)
                    mlp(m, "p2", 2, kp3, kcT, NPT, False)
                wv = m.sb(c, "wv", [DC, 2, A0])
                pooled_state(m, kcT, xpT, wv, ksum)
            pooling.close()
            aT = m.sb(attn, "aT", [P, HP, TOK])
            with ExitStack() as c:
                wq = m.sb(c, "wq", [DC, 2, A0])
                linear_attention(m, xT, wq, ksum, aT)
            load_h0 = lambda sp: sp.dma_start(m.h, m.h0).then_inc(m.h_in, 16)
            for n in range(3):
                mlp(m, f"e{n}", 5 - n, aT, aT, NT, False, load_h0 if n == 2 else None)
            project(m, "pr0", aT, HP, "attn_wo", "attn_bo", m.h, stats, True)
        m.recycle()
        mean, rstd, inv = (m.sb(ctx, n, [P, NT]) for n in ("ln_mean", "ln_rstd", "rms_inv"))
        normalised(m, "n1", stats, mean, rstd, inv)
        with ExitStack() as moe:
            slots = m.sb(moe, "slots0", [P, NT, K0], U32)
            weight = m.sb(moe, "weight0", [P, K0, NT])
            comb = m.sb(moe, "comb0", [P, NT, E0])
            expert = m.sb(moe, "expert0", [1, SLOT0], I32)
            with ExitStack() as r:
                G = m.sb(r, "logits0", [P, E0, NT])
                gates(m, "g0", m.h, mean, rstd, inv, G, E0, "gate_w0", "gate_b0")
                route(m, "r0", G, E0, K0, SLOT0, slots, weight, comb, expert)
            w1 = m.sb(moe, "w1_0", [DC + 1, E0, 2, 768])
            w2 = m.sb(moe, "w2_0", [P, E0, I0 // P, D])
            scatter(m, "sc0", m.xs[0], m.h, mean, rstd, inv, slots, K0, [(w1[:], "w1_0"), (w2[:], "w2_0")])
            experts(m, "x0", m.xs[0], E0, I0 // P, True, SLOT0, w1, w2, expert)
            gather(m, "ga0", m.h, weight, comb, E0, K0, 0, stats)
        m.recycle()
        with ExitStack() as c:
            xT = m.sb(c, "x1T", [DC, 2, TOK])
            layernorm_T(m, m.h, xT, "l1")
            oT = m.sb(c, "oT", [P, QC, TOK])
            quantised_attention(m, xT, oT)
            project(m, "pr1", oT, QC, "q_wproj", "q_bproj", m.h, stats, False)
        normalised(m, "n2", stats, mean, rstd)
        with ExitStack() as moe:
            slots = m.sb(moe, "slots1", [P, NT, K1], U32)
            weight = m.sb(moe, "weight1", [P, K1, NT])
            comb = m.sb(moe, "comb1", [P, NT, E1 + 3])
            expert = m.sb(moe, "expert1", [1, SLOT1], I32)
            w1 = m.sb(moe, "w1_1", [DC + 1, E1, 2, 768])
            w2 = m.sb(moe, "w2_1", [P, E1, I1 // P, D])
            green = Spectral(m, moe, 2 * SLOT1)
            with ExitStack() as r:
                G = m.sb(r, "logits1", [P, E1 + 1, NT])
                gates(m, "g1", m.h, mean, rstd, None, G, E1 + 1, "gate_w1", "gate_b1")
                route(m, "r1", G, E1, K1, SLOT1, slots, weight, comb, expert)
                green.start(G, E1)
            scatter(m, "sc1", m.xs[1], m.h, mean, rstd, None, slots, K1, [(w1[:], "w1_1"), (w2[:], "w2_1")])
            experts(m, "x1", m.xs[1], E1, I1 // P, False, SLOT1, w1, w2, expert,
                    lambda dve, i, part: green.step(dve, 2 * i + part, part))
            green.finish(comb[:, :, E1:])
            gather(m, "ga1", m.h, weight, comb, E1, K1, 3)


def clear(m, t):
    with ExitStack() as c:
        done = m.sem(c, "cleared")
        with m.nc.Block() as block:
            @block.vector
            def _(dve):
                dve.memset(t, 0.0).then_inc(done, 1)
                dve.wait_ge(done, 1)


def arrange(x, txt, **w):
    f = lambda a: np.ascontiguousarray(a, dtype=np.float32)
    rows = lambda a, p=P: f(np.broadcast_to(np.asarray(a), (p,) + np.asarray(a).shape))
    chunk = lambda a, k: f(np.asarray(a).reshape(k, -1, a.shape[-1]).transpose(1, 0, 2))
    o = {}
    patches = np.asarray(x).reshape(B, 4, 16, 4, 16, 3).transpose(2, 4, 5, 0, 1, 3).reshape(768, B * NIMG)
    o["patchesT"] = chunk(patches, 6)
    o["txt"] = f(txt)
    o["tok_w"] = chunk(w["L0_tok_W"], 6)
    o["tok_b"] = rows(w["L0_tok_b"])
    o["pos"] = f(np.tile(np.asarray(w["L0_tok_pos_emb"]), (8, 1)))
    o["ident"] = np.eye(P, dtype=np.float32)
    o["attn_wq"], o["attn_wk"], o["attn_wv"] = (chunk(w["L0_attn_" + k], 2) for k in ("Wq", "Wk", "Wv"))
    mats = np.concatenate([np.asarray(w["L0_attn_pool_W"]), np.asarray(w["L0_attn_exp_W"])])
    pair = np.zeros((P, 6, P), np.float32)
    for k in range(2):
        pair[k * HD:(k + 1) * HD, :, k * HD:(k + 1) * HD] = mats.transpose(1, 0, 2)
    o["mlp_w"] = pair
    both = lambda k: np.concatenate([np.asarray(w["L0_attn_pool_" + k]), np.asarray(w["L0_attn_exp_" + k])])
    o["mlp_b"] = rows(both("b"), 3)
    o["mlp_g"] = f(np.tile(both("g").T, (2, 1)))
    o["mlp_be"] = f(np.tile(both("be").T, (2, 1)))
    of = np.arange(P)[:, None, None] // HD + 2 * np.arange(HP)[None, :, None]
    o["hsel"] = f((of == np.arange(DEN)[None, None, :] % 32) & (np.arange(DEN) % 32 < NH))
    o["hexp"] = f(o["hsel"].transpose(2, 1, 0).reshape(DEN, HP * P))
    o["attn_wo"] = chunk(w["L0_attn_Wo"], 6)
    o["attn_bo"] = rows(w["L0_attn_bo"])
    o["norm_scale"] = rows(w["L0_ffn_norm_scale"])
    o["gate_w0"] = chunk(np.asarray(w["L0_ffn_gate_w"]).T, 2)
    o["gate_b0"] = rows(w["L0_ffn_gate_b"])
    up = np.asarray(w["L0_ffn_mlp1_w"]).transpose(2, 0, 1)
    up = np.concatenate([up[:, :, 0::2], up[:, :, 1::2]], axis=2)
    ub = np.asarray(w["L0_ffn_mlp1_b"])
    o["w1_0"] = with_bias(up, np.concatenate([ub[:, 0::2], ub[:, 1::2]], axis=1))
    o["w2_0"] = f(np.asarray(w["L0_ffn_mlp2_w"]).reshape(E0, D, I0 // P, P).transpose(3, 0, 2, 1))
    o["ga0_rows"] = f(w["L0_ffn_mlp2_b"])
    o["ga0_times"] = np.ones((E0, D), np.float32)
    qkv = np.asarray(w["L1_attn_Wqkv"]).reshape(3, QH, QD, D)
    pad = np.zeros((3, QH, 32, D), np.float32)
    pad[:, :, :QD] = qkv
    pad = pad.reshape(3, QH * 32, 2, DC).transpose(3, 2, 0, 1)
    o["q_wqk"] = f(pad[:, :, 0:2])
    o["q_wv"] = f(pad[:, :, 2])
    proj = np.zeros((QH, 32, D), np.float32)
    proj[:, :QD] = np.asarray(w["L1_attn_Wproj"]).T.reshape(QH, QD, D)
    o["q_wproj"] = f(proj.reshape(QC, P, D).transpose(1, 0, 2))
    o["q_bproj"] = rows(w["L1_attn_bproj"])
    o["q_scales"] = f(np.stack([np.broadcast_to(np.asarray(w["L1_attn_s_" + k]), (P,)) for k in ("q", "k", "v", "attn", "after")]
                             + [(np.arange(P) % 32 >= 32 - (N - P)).astype(np.float32)], 1))
    o["gate_w1"] = chunk(np.concatenate([np.asarray(w["L1_ffn_gate_w"]), np.asarray(w["L1_ffn_v_w"])[:, None]], 1), 2)
    o["gate_b1"] = rows(np.concatenate([np.asarray(w["L1_ffn_gate_b"]), np.asarray(w["L1_ffn_v_b"]).reshape(1)]))
    o["w1_1"] = with_bias(np.asarray(w["L1_ffn_w1"]).transpose(1, 0, 2), np.asarray(w["L1_ffn_b1"]))
    o["w2_1"] = f(np.asarray(w["L1_ffn_w2"]).reshape(E1, I1 // P, P, D).transpose(2, 0, 1, 3))
    o["ga1_rows"] = f(np.concatenate([np.asarray(w["L1_ffn_b2"]), np.asarray(w["L1_ffn_out_w"]), np.asarray(w["L1_ffn_out_b"])[None]]))
    o["ga1_times"] = f(np.concatenate([np.ones((E1, D), np.float32), np.tile(np.asarray(w["L1_ffn_bk_scale"]), (3, 1))]))
    for e in (E0, E1):
        o["mask%d" % e] = f(np.broadcast_to(np.arange(NT) > 0, (P, e, NT)))
    o["tri"] = f(np.triu(np.ones((P, P)), 1))
    o["ones"] = np.ones((P, P), np.float32)
    o["steps"] = rows(np.arange(NT, dtype=np.float32) * P)
    for k in (K0, K1):
        o["place%d" % k] = (np.arange(TOK, dtype=np.uint32)[:, None] * k + np.arange(k, dtype=np.uint32)).reshape(
            NT, P, k).transpose(1, 0, 2).copy()
    o["unused"] = np.arange(P, dtype=np.uint32)[:, None] + np.array([[TOK * K0, TOK * K1]], np.uint32)
    o["jrow"] = np.arange(SLOT0, dtype=np.float32)[None]
    alt = np.where(np.arange(N) % 2 == 0, 1.0, -1.0)
    o["sign"] = rows(alt, 2 * B)
    return o


def with_bias(w, b):
    out = np.zeros((DC + 1, w.shape[1], 2, w.shape[2]), np.float32)
    out[:DC] = w.reshape(2, DC, w.shape[1], w.shape[2]).transpose(1, 2, 0, 3)
    out[DC, :, 1] = b
    return out


def kernel(**inputs):
    import concourse.bacc as bacc
    from concourse.bass_utils import run_bass_kernel_spmd

    nc = bacc.Bacc("TRN2", target_bir_lowering=False, num_devices=1)
    arrays = {"in_" + k: v for k, v in arrange(**inputs).items()}
    ins = {k[3:]: nc.dram_tensor(k, a.shape, mybir.dt.from_np(a.dtype), kind="ExternalInput").ap() for k, a in arrays.items()}
    out = nc.dram_tensor("out", [TOK, D], F32, kind="ExternalOutput").ap()
    model(nc, ins, out)
    r = run_bass_kernel_spmd(nc, [arrays], core_ids=[0])
    return r.results[0]["out"].reshape(B, N, D)
```
